# Optimizing a Trainium2 kernel written in Bass

```python
import numpy as np
import jax
import jax.numpy as jnp

def _softmax(x, axis=-1):
    return jax.nn.softmax(x, axis=axis)

def _gelu(x):
    return jax.nn.gelu(x, approximate=True)

def _silu(x):
    return jax.nn.silu(x)

def _sigmoid(x):
    return jax.nn.sigmoid(x)

def _layernorm(x, axis=-1, eps=1e-05):
    m = jnp.mean(x, axis=axis, keepdims=True)
    v = jnp.var(x, axis=axis, keepdims=True)
    return (x - m) / jnp.sqrt(v + eps)

def _scatter_add(tgt, idx, src, axis=0):
    return tgt.at[idx].add(src)

def _segment_sum(src, seg, n):
    return jax.ops.segment_sum(src, seg, n)
kernel_name = 'mk_xattn_ffn_d1_seqx_r2_09bacb'

def setup_inputs(seed: int=0):
    np.random.seed(seed)
    _w = jnp.asarray

    def _rec_inputs():
        import jax
        import jax.numpy as jnp
        _rk = jax.random.key(seed)
        x = 7.22e-05 + 1 * jax.random.normal(jax.random.fold_in(_rk, 1), (2, 2048, 512), jnp.float32)
        _lenS = 2048 - jax.random.randint(jax.random.fold_in(_rk, 7), (2,), 0, max(1, 2048 // 4) + 1, jnp.int32)
        _lenS2 = 128 - jax.random.randint(jax.random.fold_in(_rk, 8), (2,), 0, max(1, 128 // 4) + 1, jnp.int32)
        _ctx_1024P = jax.random.normal(jax.random.fold_in(_rk, 11), (2, 16, 512), jnp.float32)
        _ctx_1024c = jax.random.dirichlet(jax.random.fold_in(_rk, 511), 0.3 * jnp.ones((16,), jnp.float32), (2, 128))
        _ctx_1024t = jnp.einsum('bsk,bkd->bsd', _ctx_1024c, _ctx_1024P)
        _ctx_1024t = _ctx_1024t * jax.lax.rsqrt(jnp.mean(jnp.square(_ctx_1024t)) + 1e-12) * 0.953939
        ctx_1024 = 4.13588e-05 + 0.999923 * (_ctx_1024t + 0.3 * jax.random.normal(jax.random.fold_in(_rk, 611), (2, 128, 512), jnp.float32))
        return (x, ctx_1024)
    x, ctx_1024 = _rec_inputs()

    def _L0_xattn_setup():
        import math
        import jax, jax.numpy as jnp
        import numpy as np
        H = 16
        D_MODEL = 512
        DK = D_MODEL // H
        K_FACTOR = 2

        def _time_delay_agg_inference(v, corr):
            B, _, _, L = v.shape
            top_k = min(int(K_FACTOR * math.log(L)), L)
            mean_value = jnp.mean(corr, axis=(1, 2))
            weights, delay = jax.lax.top_k(mean_value, top_k)
            tmp_corr = jax.nn.softmax(weights, axis=-1)
            idx = (delay[:, :, None] + jnp.arange(L)) % L
            gathered = jnp.take_along_axis(v[:, None], idx[:, :, None, None, :], axis=-1)
            return jnp.einsum('bk,bkhdl->bhdl', tmp_corr, gathered)
        key = jax.random.key(seed)
        ks = jax.random.split(key, 11)
        B, L, D = (4, 1024, D_MODEL)
        s = 1.0 / math.sqrt(D)
        return {'queries': jax.random.normal(ks[0], (B, L, D), jnp.float32), 'keys': jax.random.normal(ks[1], (B, L, D), jnp.float32), 'values': jax.random.normal(ks[2], (B, L, D), jnp.float32), 'Wq': jax.random.normal(ks[3], (D, H * DK), jnp.float32) * s, 'bq': jnp.zeros((H * DK,), jnp.float32), 'Wk': jax.random.normal(ks[4], (D, H * DK), jnp.float32) * s, 'bk': jnp.zeros((H * DK,), jnp.float32), 'Wv': jax.random.normal(ks[5], (D, H * DK), jnp.float32) * s, 'bv': jnp.zeros((H * DK,), jnp.float32), 'Wo': jax.random.normal(ks[6], (H * DK, D), jnp.float32) * s, 'bo': jnp.zeros((D,), jnp.float32)}
    _L0_xattn_all = _L0_xattn_setup()
    _L0_xattn_in = {k: v for k, v in _L0_xattn_all.items() if k in ('Wq', 'bq', 'Wk', 'bk', 'Wv', 'bv', 'Wo', 'bo')}
    del _L0_xattn_all

    def _L0_ffn_setup():
        import jax, jax.numpy as jnp
        import numpy as np
        E = 16
        G = 4
        EPG = E // G
        K = 4
        TOPK_GROUP = 2
        PER_GROUP_K = K // TOPK_GROUP

        def _route(xf, router_w, correction_bias):
            S = xf.shape[0]
            logits = xf @ router_w.T
            scores = jax.nn.sigmoid(logits)
            sb = scores + correction_bias
            grp_top = jax.lax.top_k(sb.reshape(S, G, EPG), PER_GROUP_K)[0]
            group_scores = grp_top.sum(axis=-1)
            _, group_idx = jax.lax.top_k(group_scores, TOPK_GROUP)
            group_mask = jnp.zeros((S, G), sb.dtype).at[jnp.arange(S)[:, None], group_idx].set(1.0)
            score_mask = jnp.broadcast_to(group_mask[:, :, None], (S, G, EPG)).reshape(S, E)
            masked = jnp.where(score_mask > 0, sb, -jnp.inf)
            _, topk_idx = jax.lax.top_k(masked, K)
            w = jnp.take_along_axis(scores, topk_idx, axis=1)
            w = w / (w.sum(axis=-1, keepdims=True) + 1e-20)
            return (topk_idx, w, scores)
        key = jax.random.key(seed)
        ks = jax.random.split(key, 9)
        B, T, C, H, HS = (2, 512, 512, 128, 1024)
        std = 0.02
        return {'x': jax.random.normal(ks[0], (B, T, C), jnp.float32), 'router_w': jax.random.normal(ks[1], (E, C), jnp.float32) * std, 'correction_bias': jnp.zeros((E,), jnp.float32), 'gate_w': jax.random.normal(ks[2], (E, C, H), jnp.float32) * std, 'up_w': jax.random.normal(ks[3], (E, C, H), jnp.float32) * std, 'down_w': jax.random.normal(ks[4], (E, H, C), jnp.float32) * std, 'shared_gate_w': jax.random.normal(ks[5], (HS, C), jnp.float32) * std, 'shared_up_w': jax.random.normal(ks[6], (HS, C), jnp.float32) * std, 'shared_down_w': jax.random.normal(ks[7], (C, HS), jnp.float32) * std}
    _L0_ffn_all = _L0_ffn_setup()
    _L0_ffn_in = {k: v for k, v in _L0_ffn_all.items() if k in ('router_w', 'correction_bias', 'gate_w', 'up_w', 'down_w', 'shared_gate_w', 'shared_up_w', 'shared_down_w')}
    del _L0_ffn_all
    return {'x': x, 'ctx_1024': ctx_1024, 'L0_xattn_Wq': _L0_xattn_in['Wq'], 'L0_xattn_bq': _L0_xattn_in['bq'], 'L0_xattn_Wk': _L0_xattn_in['Wk'], 'L0_xattn_bk': _L0_xattn_in['bk'], 'L0_xattn_Wv': _L0_xattn_in['Wv'], 'L0_xattn_bv': _L0_xattn_in['bv'], 'L0_xattn_Wo': _L0_xattn_in['Wo'], 'L0_xattn_bo': _L0_xattn_in['bo'], 'L0_ffn_router_w': _L0_ffn_in['router_w'], 'L0_ffn_correction_bias': _L0_ffn_in['correction_bias'], 'L0_ffn_gate_w': _L0_ffn_in['gate_w'], 'L0_ffn_up_w': _L0_ffn_in['up_w'], 'L0_ffn_down_w': _L0_ffn_in['down_w'], 'L0_ffn_shared_gate_w': _L0_ffn_in['shared_gate_w'], 'L0_ffn_shared_up_w': _L0_ffn_in['shared_up_w'], 'L0_ffn_shared_down_w': _L0_ffn_in['shared_down_w']}

def reference(x, ctx_1024, L0_xattn_Wq, L0_xattn_bq, L0_xattn_Wk, L0_xattn_bk, L0_xattn_Wv, L0_xattn_bv, L0_xattn_Wo, L0_xattn_bo, L0_ffn_router_w, L0_ffn_correction_bias, L0_ffn_gate_w, L0_ffn_up_w, L0_ffn_down_w, L0_ffn_shared_gate_w, L0_ffn_shared_up_w, L0_ffn_shared_down_w):
    import jax
    import jax.numpy as jnp

    def _L0_xattn_ref(queries, keys, values, Wq, bq, Wk, bk, Wv, bv, Wo, bo):
        import math
        import jax, jax.numpy as jnp
        import numpy as np
        H = 16
        D_MODEL = 512
        DK = D_MODEL // H
        K_FACTOR = 2

        def _time_delay_agg_inference(v, corr):
            B, _, _, L = v.shape
            top_k = min(int(K_FACTOR * math.log(L)), L)
            mean_value = jnp.mean(corr, axis=(1, 2))
            weights, delay = jax.lax.top_k(mean_value, top_k)
            tmp_corr = jax.nn.softmax(weights, axis=-1)
            idx = (delay[:, :, None] + jnp.arange(L)) % L
            gathered = jnp.take_along_axis(v[:, None], idx[:, :, None, None, :], axis=-1)
            return jnp.einsum('bk,bkhdl->bhdl', tmp_corr, gathered)
        B, Lq, _ = queries.shape
        Lk = keys.shape[1]
        q = (queries @ Wq + bq).reshape(B, Lq, H, DK)
        k = (keys @ Wk + bk).reshape(B, Lk, H, DK)
        v = (values @ Wv + bv).reshape(B, Lk, H, DK)
        if Lq > Lk:
            pad = ((0, 0), (0, Lq - Lk), (0, 0), (0, 0))
            k = jnp.pad(k, pad)
            v = jnp.pad(v, pad)
        else:
            k = k[:, :Lq]
            v = v[:, :Lq]
        qt = jnp.transpose(q, (0, 2, 3, 1))
        kt = jnp.transpose(k, (0, 2, 3, 1))
        vt = jnp.transpose(v, (0, 2, 3, 1))
        qf = jnp.fft.rfft(qt)
        kf = jnp.fft.rfft(kt)
        c = qf.real * kf.real + 1j * -(qf.imag * kf.imag)
        corr = jnp.fft.irfft(c, n=Lq).astype(qt.dtype)
        agg = _time_delay_agg_inference(vt, corr)
        out = jnp.transpose(agg, (0, 3, 1, 2)).reshape(B, Lq, H * DK)
        return out @ Wo + bo

    def _L0_ffn_ref(x, router_w, correction_bias, gate_w, up_w, down_w, shared_gate_w, shared_up_w, shared_down_w):
        import jax, jax.numpy as jnp
        import numpy as np
        E = 16
        G = 4
        EPG = E // G
        K = 4
        TOPK_GROUP = 2
        PER_GROUP_K = K // TOPK_GROUP

        def _route(xf, router_w, correction_bias):
            S = xf.shape[0]
            logits = xf @ router_w.T
            scores = jax.nn.sigmoid(logits)
            sb = scores + correction_bias
            grp_top = jax.lax.top_k(sb.reshape(S, G, EPG), PER_GROUP_K)[0]
            group_scores = grp_top.sum(axis=-1)
            _, group_idx = jax.lax.top_k(group_scores, TOPK_GROUP)
            group_mask = jnp.zeros((S, G), sb.dtype).at[jnp.arange(S)[:, None], group_idx].set(1.0)
            score_mask = jnp.broadcast_to(group_mask[:, :, None], (S, G, EPG)).reshape(S, E)
            masked = jnp.where(score_mask > 0, sb, -jnp.inf)
            _, topk_idx = jax.lax.top_k(masked, K)
            w = jnp.take_along_axis(scores, topk_idx, axis=1)
            w = w / (w.sum(axis=-1, keepdims=True) + 1e-20)
            return (topk_idx, w, scores)
        B, T, C = x.shape
        S = B * T
        xf = x.reshape(S, C)
        sg = xf @ shared_gate_w.T
        su = xf @ shared_up_w.T
        shared_out = jax.nn.silu(sg) * su @ shared_down_w.T
        topk_idx, w, _scores = _route(xf, router_w, correction_bias)
        combine = jnp.zeros((S, E), xf.dtype).at[jnp.arange(S)[:, None], topk_idx].add(w)
        g = jnp.einsum('sc,ech->esh', xf, gate_w)
        u = jnp.einsum('sc,ech->esh', xf, up_w)
        h = jax.nn.silu(g) * u
        hw = h * combine.T[:, :, None]
        routed = jnp.einsum('esh,ehc->sc', hw, down_w)
        return (shared_out + routed).reshape(B, T, C)
    x = x + _L0_xattn_ref(_layernorm(x, axis=-1), ctx_1024, ctx_1024, L0_xattn_Wq, L0_xattn_bq, L0_xattn_Wk, L0_xattn_bk, L0_xattn_Wv, L0_xattn_bv, L0_xattn_Wo, L0_xattn_bo)
    x = x + _L0_ffn_ref(_layernorm(x, axis=-1), L0_ffn_router_w, L0_ffn_correction_bias, L0_ffn_gate_w, L0_ffn_up_w, L0_ffn_down_w, L0_ffn_shared_gate_w, L0_ffn_shared_up_w, L0_ffn_shared_down_w)
    return x

_drawn_inputs = setup_inputs


def setup_inputs(seed=0):
    import zlib

    import numpy as np

    out = dict(_drawn_inputs(seed))
    spreads = {'L0_xattn_bq': (0.0, 0.8),
     'L0_xattn_bk': (0.0, 0.344),
     'L0_xattn_bv': (0.0, 0.775),
     'L0_xattn_bo': (0.0, 0.1),
     'L0_ffn_correction_bias': (0.0, 0.741)}
    factors = {'L0_ffn_router_w': 5.891,
     'L0_ffn_gate_w': 4.701,
     'L0_ffn_up_w': 4.613,
     'L0_ffn_down_w': 4.617}
    for name, (base, spread) in spreads.items():
        noise = np.random.default_rng([zlib.crc32(name.encode()), seed]).standard_normal(out[name].shape)
        drawn = base * np.exp(spread * noise) if base else spread * noise
        out[name] = jnp.asarray(drawn.astype(out[name].dtype))
    for name, factor in factors.items():
        out[name] = (out[name] * factor).astype(out[name].dtype)
    return out
```

```python
from contextlib import ExitStack

import numpy as np

import concourse.bass as bass
from concourse import mybir

F32 = mybir.dt.float32
F16 = mybir.dt.float16
ALU = mybir.AluOpType
ACT = mybir.ActivationFunctionType
AX_X = mybir.AxisListType.X

P = 128
B, L, D = 2, 2048, 512
M = 128
TOP_K = int(2 * np.log(L))
E, H = 16, 128
GROUPS, PER_GROUP, TOP_GROUPS, TOP_E = 4, 4, 2, 4
HS = 1024
SH = HS // H
KC = D // P
S = B * L
T = S // P
TB = 4
NB = S // (P * TB)
BLK = P * TB
NA = L // P
PTW = M + L + M
EPS = 1e-5
WS = 64.0
NP = S * TOP_E
BLOCKS = (NP + E * (P - 1)) // P + 1
FIRST = 4
LAG = TB + 1
ROUND = 12582912.0
GONE = -3.0e38

C_ID, C_ONES, C_J0, C_J1, C_IS, C_T = 0, 128, 132, 260, 388, 516
C_END = C_T + NA * P
R_EXP, R_BLK, R_TRI = 0, E, E + BLOCKS
R_END = R_TRI + P


def constants():
    c = np.zeros((P, C_END), np.float32)
    eye = np.eye(P, dtype=np.float32)
    c[:, C_ID:C_ID + P] = eye
    c[:, C_ONES:C_ONES + 4] = [1, 1, 1, -1]
    c[0, C_J0] = 1
    c[:, C_J1:C_J1 + P][1:, 1:] = eye[1:, 1:][::-1]
    scale = 1.0 / (4 * D)
    c[:, C_IS:C_IS + P] = eye * scale
    d = np.arange(L)
    hilbert = np.zeros(L)
    hilbert[1::2] = -2.0 / L / np.tan(np.pi * d[1::2] / L)
    q, p = np.arange(P)[:, None], np.arange(P)[None, :]
    for a in range(NA):
        c[:, C_T + a * P:C_T + (a + 1) * P] = scale * hilbert[(P * a + p - q) % L]
    r = np.zeros((P, R_END), np.float32)
    r[:, R_EXP:R_EXP + E] = np.arange(E)
    r[:, R_BLK:R_BLK + BLOCKS] = np.arange(BLOCKS)
    r[:, R_TRI:R_TRI + P] = q < p
    return c, r


class Links:

    def __init__(self, engine, semaphore):
        self.engine, self.semaphore, self.count = engine, semaphore, 0

    def start(self, instruction):
        self.count += 1
        instruction.then_inc(self.semaphore, 1)

    def wait(self):
        self.engine.wait_ge(self.semaphore, self.count)

    def done(self, instruction):
        self.start(instruction)
        self.wait()


def build(nc, x, ctxT, wk, wqT, wv, wo, biases, bo, cb, routerT, gu_w, dn_w, const, const_r, out):
    with ExitStack() as ctx:
        def sem(name):
            return ctx.enter_context(nc.semaphore(name))

        KB = 1024
        R1, R2, R3 = 48 * KB, 96 * KB, 65024
        arena = ctx.enter_context(nc.sbuf_tensor("arena", [P, (R1 + R2 + R3) // 4], F32))

        def view(offset, shape, dt=F32):
            n = int(np.prod(shape))
            v = arena[:, offset // 4:(offset + n * (2 if dt == F16 else 4)) // 4]
            if dt != F32:
                v = v.bitcast(dt)
            if len(shape) == 2:
                v = v.rearrange("p (a b) -> p a b", a=shape[0])
            elif len(shape) == 3:
                v = v.rearrange("p (a b c) -> p a b c", a=shape[0], b=shape[1])
            return v

        wk_sb, wq_sb = view(0, [KC, D]), view(8 * KB, [KC, D])
        wv_sb, wo_sb = view(16 * KB, [KC, D]), view(24 * KB, [KC, D])
        ctx_sb = view(32 * KB, [KC, B * M])
        kT, vT = view(36 * KB, [KC, B * M]), view(40 * KB, [KC, B * M])
        gu_hi_s, gu_lo_s = view(0, [SH, 2 * D], F16), view(16 * KB, [SH, 2 * D], F16)
        dn_hi_s, dn_lo_s = view(32 * KB, [SH, D], F16), view(40 * KB, [SH, D], F16)
        o = R1
        x_sb = view(o, [T, D])
        xnT = [view(o + 64 * KB, [KC, BLK]), view(o + 72 * KB, [KC, BLK])]
        skew_c, skew_d = view(o + 80 * KB, [L]), view(o + 88 * KB, [L])
        row, taken = view(o + 64 * KB, [L]), view(o + 72 * KB, [L])
        gu_hi_r, gu_lo_r = view(o, [E, 2 * D], F16), view(o + 32 * KB, [E, 2 * D], F16)
        dn_hi_r, dn_lo_r = view(o + 64 * KB, [E, D], F16), view(o + 80 * KB, [E, D], F16)
        scores, biased, tmp, cnt, slot = (view(o + 80 * KB + 2 * KB * i, [T * E]) for i in range(5))
        picked = [view(o + 90 * KB + KB * i, [T * E], F16) for i in range(TOP_E)]
        o1 = R1 + R2
        c_sb = view(o1, [C_END])
        vo = view(o1 + 10368, [B, D])
        st = [view(o1 + 14464, [BLK]), view(o1 + 16512, [BLK])]
        x1b = view(o1, [TB, D])
        s_silu, s_h = view(o1 + 8 * KB, [BLK]), view(o1 + 10 * KB, [BLK])
        s_hb = view(o1 + 12 * KB, [2, 2, BLK], F16)
        o2 = o1 + 18560
        pt = [view(o2, [PTW]), view(o2 + PTW * 4, [PTW])]
        hi16, lo16 = view(o2, [TB, D], F16), view(o2 + 4 * KB, [TB, D], F16)
        top8 = view(o2, [T, 8])
        top8_at = view(o2 + KB, [T, 8], mybir.dt.uint32)
        top8_e = view(o2 + 2 * KB, [T, 8])
        xg = view(o2, [4, 2 * D], F16)
        ybuf0 = view(o2, [TOP_E, D])
        xtb = view(o2 + 8 * KB, [2, 2 * KC, BLK], F16)
        bo_sb = view(o2 + 20 * KB, [D])
        o3 = o2 + 24 * KB
        xn = view(o3, [TB, D])
        g_sb = view(o3 + 8 * KB, [KC, B * M])
        stage = [view(o3, [3 * D]), view(o3 + 6 * KB, [3 * D])]
        xgT = view(o3, [2, 2 * KC, P], F16)
        y_sb = view(o3 + 4 * KB, [2, D])
        r_silu, r_h = view(o3 + 8 * KB, [2, H]), view(o3 + 9 * KB, [2, H])
        r_hb, r_hT = view(o3 + 10 * KB, [2, 2, H], F16), view(o3 + 11 * KB, [2, 2, P], F16)
        ybuf = [ybuf0, view(o3, [TOP_E, D])]
        x1c = view(o3 + 8 * KB, [2, D])
        o4 = o3 + 12 * KB
        small = view(o4, [(R1 + R2 + R3 - o4) // 4])
        at = [0]

        def little(n, dt=F32):
            words = n if dt != F16 else (n + 1) // 2
            v = small[:, at[0]:at[0] + words]
            at[0] += words
            assert at[0] <= (R1 + R2 + R3 - o4) // 4
            return v if dt == F32 else v.bitcast(dt)

        I32 = mybir.dt.int32
        blocks_e = little(BLOCKS + 8, I32)
        chosen_after = little((T + 1) * E, F16)
        chosen = chosen_after[:, E:]
        bias_sb = little(3 * KC)
        bqk = little(B)
        id16 = little(P, F16)
        rt32 = little(KC * E)
        rt_hi, rt_lo = (little(KC * E, F16).rearrange("p (k e) -> p k e", k=KC) for _ in range(2))
        cb_sb = little(E)
        cr_sb = little(R_END)
        tri16, ones16 = little(P, F16), little(P, F16)
        stats = little(TB * 6).rearrange("p (t s) -> p t s", t=TB)
        mv = little(TB * 2).rearrange("p (t s) -> p t s", t=TB)
        var_eps, std, rstd = little(TB), little(TB), little(TB)
        sums = little(2 * NA).rearrange("p (v a) -> p v a", v=2)
        mirrored = little(2 * (NA + 1)).rearrange("p (v a) -> p v a", v=2)
        even_s = little(NA)
        even_w = little(2 * NA)
        mean_sb = little(NA)
        meanT = little(P)
        best = little(16)
        top_e = little(16)
        negmax, total, inv = little(1), little(1), little(1)
        token_id = little(T, I32)
        token_of = little(BLOCKS, I32)
        put_at, row_of = little(NP // P, I32), little(NP // P, I32)
        put_now, row_now = (little(4 * TOP_E, I32).rearrange("p (r i) -> p r i", r=4) for _ in range(2))
        id_now, token_now = little(4, I32), little(8, I32)
        pair_slot, pair_w, pair_blk = little(NP // P), little(NP // P), little(NP // P)
        load_e, nblk, first_a, first_b, last_blk = (little(E) for _ in range(5))

        bank = [ctx.enter_context(nc.psum_tensor(f"bank{i}", [P, 512], F32)) for i in range(8)]
        bank16 = [bk[:, :].bitcast(F16) for bk in bank]

        pt_dram = nc.dram_tensor("pt_dram", [B, P, PTW], F32)
        mean_dram = nc.dram_tensor("mean_dram", [B, L], F32)
        g_dram = nc.dram_tensor("g_dram", [B, M + L], F32)
        xt_dram = nc.dram_tensor("xt_dram", [NB, P, 2 * KC * BLK], F16)
        xr_dram = nc.dram_tensor("xr_dram", [S, 2 * D], F16)
        x1_dram = nc.dram_tensor("x1_dram", [S, D], F32)
        x1s_dram = nc.dram_tensor("x1s_dram", [S, D], F32)
        token_dram = nc.dram_tensor("token_dram", [P * BLOCKS, 1], I32)
        y_dram = nc.dram_tensor("y_dram", [BLOCKS * P, D], F32)
        x_rows = x.rearrange("(q t p) d -> q p t d", t=TB, p=P)
        xr_rows = xr_dram.rearrange("(q t p) d -> q p t d", t=TB, p=P)
        x1_rows = x1_dram.rearrange("(q t p) d -> q p t d", t=TB, p=P)
        x1s_rows = x1s_dram.rearrange("(q t p) d -> q p t d", t=TB, p=P)
        x1s_tiles = x1s_dram.rearrange("(t p) d -> t p d", p=P)
        out_tiles = out.rearrange("(t p) d -> t p d", p=P)
        y_tiles = y_dram.rearrange("(n p) d -> n p d", p=P)

        def only(v, i, *rest):
            v = v[(slice(None), bass.ds(i, 1)) + rest]
            names = "abcd"[:len(v.shape) - 1]
            if len(v.shape) == 3:
                return v.rearrange("p a b -> p (a b)")
            return v.rearrange("p a b c -> p (a b) c")

        def item(d, i):
            d = d[bass.ds(i, 1)]
            if len(d.shape) == 3:
                return d.rearrange("a p n -> (a p) n")
            return d.rearrange("a p t n -> (a p) t n")

        def skewed(b, start, pitch):
            return bass.AP(pt_dram, b * P * PTW + start, [[pitch, P], [1, L]])

        s_const, s_kw, s_qw, s_vw, s_ow = (sem(n) for n in ("const_in", "wk_in", "wq_in", "wv_in", "wo_in"))
        s_x = [sem(f"x_in{q}") for q in range(NB)]
        s_misc = sem("router_in")
        s_mm, s_mm_sb = sem("projection_done"), sem("projection_saved")
        s_var, s_std, s_xn = sem("var_ready"), sem("std_ready"), sem("xn_ready")
        s_tp, s_tp_sb = sem("transposed"), sem("transposes_saved")
        s_pt, s_pt_sb = sem("pt_done"), sem("pt_saved")
        s_ptw = [sem(f"pt_written{b}") for b in range(B)]
        s_sk = [sem(f"skew_in{b}") for b in range(B)]
        s_u, s_u_sb = sem("sums_done"), sem("sums_saved")
        s_ev, s_ev_sb = sem("even_done"), sem("even_saved")
        s_mean, s_mean_sb = sem("mean_done"), sem("mean_saved")
        s_mT, s_mT_sb = sem("mean_turned"), sem("meanT_saved")
        s_mw = [sem(f"mean_written{b}") for b in range(B)]
        s_row = [sem(f"row_in{b}") for b in range(B)]
        s_best, s_exp = sem("best_ready"), sem("exp_done")
        s_g, s_gw = sem("g_ready"), sem("g_written")
        s_xbo = sem("x_plus_bo")
        s_st = [sem("circulant_in0"), sem("circulant_in1")]
        s_at, s_x1, s_bn = sem("attention_done"), sem("x1_ready"), sem("bn_stats_done")
        s_mv, s_rstd = sem("moments_ready"), sem("rstd_ready")
        s_var2, s_std2, s_xn2 = sem("var2_ready"), sem("std2_ready"), sem("xn2_ready")
        s_hi, s_lo = sem("xn2_hi_ready"), sem("xn2_lo_ready")
        s_tp2, s_tp2_sb = sem("xn2_turned"), sem("xn2_turned_saved")
        s_lg = sem("logits_done")
        s_xtw, s_xrw, s_x1w = sem("xt_written"), sem("xr_written"), sem("x1_written")
        s_stage = [sem("stage_in0"), sem("stage_in1")]
        s_stage_r = sem("routed_stage_in")
        s_whi, s_w64, s_wlo = sem("shared_w_hi"), sem("shared_w_scaled"), sem("shared_w_lo")
        s_whi_r, s_wlo_r = sem("routed_w_hi"), sem("routed_w_lo")
        s_rt = sem("router_split")
        s_sig, s_chosen, s_rank = sem("scores_ready"), sem("chosen_ready"), sem("ranks_done")
        s_put, s_expert = sem("pair_places_ready"), sem("block_experts_ready")
        s_zero, s_cleared, s_tok = sem("zero_ready"), sem("tokens_cleared"), sem("tokens_in")
        s_scattered = [sem(f"tokens_scattered{r}") for r in range(4)]
        s_put_now, s_token_now, s_row_now = sem("places_copied"), sem("tokens_copied"), sem("rows_copied")
        s_ids = sem("token_ids_ready")
        s_dve = sem("dve_step")
        s_xt, s_x1i = [sem("xt_in0"), sem("xt_in1")], sem("x1_in")
        s_sg, s_su, s_ss, s_sh32 = sem("shared_gate"), sem("shared_up"), sem("shared_silu"), sem("shared_h32")
        s_shh, s_shl, s_sd = sem("shared_h_hi"), sem("shared_h_lo"), sem("shared_down")
        s_x1s, s_x1sw = sem("x1s_ready"), sem("x1s_written")
        s_xg = [sem(f"rows_gathered{r}") for r in range(4)]
        s_tx, s_txe = sem("rows_turned"), sem("rows_turned_saved")
        s_rg, s_rs, s_rh = sem("routed_gate_up"), sem("routed_silu"), sem("routed_h32")
        s_rhh, s_rhl = sem("routed_h_hi"), sem("routed_h_lo")
        s_ht, s_hte, s_rd = sem("routed_h_turned"), sem("routed_h_turned_saved"), sem("routed_down")
        s_ye = sem("y_saved")
        s_yw = [sem("y_written0"), sem("y_written1")]
        s_yg = [sem("y_gathered0"), sem("y_gathered1")]
        s_x1c = [sem("x1s_in0"), sem("x1s_in1")]
        s_cmb = sem("result_added")
        s_out = [sem("out_written0"), sem("out_written1")]

        block = ctx.enter_context(nc.Block())
        PARTS = ((0, 0), (0, 1), (1, 0))

        def settled(engine):
            engine.wait_ge(s_const, 16)

        @block.sync
        def _(sp):
            sp.dma_start(c_sb, const).then_inc(s_const, 16)
            sp.dma_start(ctx_sb, ctxT).then_inc(s_kw, 16)
            sp.dma_start(bias_sb, biases).then_inc(s_kw, 16)
            sp.dma_start(wk_sb, wk).then_inc(s_kw, 16)
            for q in range(NB):
                sp.dma_start(x_sb[:, TB * q:TB * q + TB, :], x_rows[q]).then_inc(s_x[q], 16)
                if q == 0:
                    sp.dma_start(wq_sb, wqT).then_inc(s_qw, 16)
                if q == 1:
                    sp.dma_start(bo_sb, bo).then_inc(s_misc, 16)
                    sp.dma_start(rt32, routerT).then_inc(s_misc, 16)
                    sp.dma_start(cb_sb, cb).then_inc(s_misc, 16)
                    sp.dma_start(cr_sb, const_r).then_inc(s_misc, 16)
            sp.dma_start(wv_sb, wv).then_inc(s_vw, 16)
            sp.dma_start(wo_sb, wo).then_inc(s_ow, 16)
            for b in range(B):
                sp.wait_ge(s_pt_sb, 4 * (b + 1))
                sp.dma_start(pt_dram[b], pt[b]).then_inc(s_ptw[b], 16)
                sp.wait_ge(s_ptw[b], 16)
                if b:
                    sp.wait_ge(s_u, b)
                sp.dma_start(skew_c, skewed(b, 2 * M - 1, PTW - 1)).then_inc(s_sk[b], 16)
                sp.dma_start(skew_d, skewed(b, 1, PTW + 1)).then_inc(s_sk[b], 16)

            def means(b):
                sp.wait_ge(s_mT_sb, b + 1)
                sp.dma_start(mean_dram[b].rearrange("(a p) -> a p", p=P), meanT[0:NA, :]).then_inc(s_mw[b], 16)
                sp.wait_ge(s_mw[b], 16)
                if b:
                    sp.wait_ge(s_gw, 32 * b)
                sp.dma_start(row[0:1, :], mean_dram[b:b + 1, :]).then_inc(s_row[b], 16)

            def delays(b):
                sp.wait_ge(s_g, b + 1)
                sp.dma_start(g_dram[b:b + 1, M:M + L], row[0:1, :]).then_inc(s_gw, 16)
                sp.dma_start(g_dram[b:b + 1, 0:M], row[0:1, L - M:L]).then_inc(s_gw, 16)

            means(0)
            for n in range(SH):
                if n == 0:
                    sp.wait_ge(s_mm_sb, 15)
                if n >= 2:
                    sp.wait_ge(s_wlo, n - 1)
                if n == 3:
                    delays(0)
                    means(1)
                sp.dma_start(stage[n % 2][:, 0:2 * D], gu_w[n]).then_inc(s_stage[n % 2], 16)
                sp.dma_start(stage[n % 2][:, 2 * D:3 * D], dn_w[n]).then_inc(s_stage[n % 2], 16)
            delays(1)

            def circulant(k, j):
                sp.dma_start(st[j], bass.AP(g_dram, (k // (NB // B)) * (M + L) + k % (NB // B) * BLK + 1, [[1, P], [1, BLK]])
                             ).then_inc(s_st[j], 16)

            sp.wait_ge(s_gw, 64)
            for k in range(2):
                circulant(k, k)

            def second_norm_out(k, j, more):
                if more:
                    sp.wait_ge(s_at, TB * (k + 1))
                    circulant(k + 2, j)
                sp.wait_ge(s_x1, TB * (k + 1))
                sp.dma_start(item(x1_rows, k), x_sb[:, bass.ds(k * TB, TB), :]).then_inc(s_x1w, 16)
                sp.wait_ge(s_hi, k + 1)
                sp.dma_start(item(xr_rows, k)[:, :, 0:D], hi16).then_inc(s_xrw, 16)
                sp.wait_ge(s_lo, k + 1)
                sp.dma_start(item(xr_rows, k)[:, :, D:2 * D], lo16).then_inc(s_xrw, 16)
                settled(sp)
                sp.wait_ge(s_tp2_sb, TB * (k + 1))
                if not isinstance(k, int) or k:
                    sp.wait_ge(s_xtw, 16 * k)
                sp.dma_start(item(xt_dram, k), xtb[:, j, :, :].rearrange("p n q -> p (n q)")).then_inc(s_xtw, 16)

            for j in range(2):
                second_norm_out(j, j, True)
            with sp.Fori(1, NB // 2 - 1) as i:
                for j in range(2):
                    second_norm_out(2 * i + j, j, True)
            for j in range(2):
                second_norm_out(NB - 2 + j, j, False)

            sp.wait_ge(s_xtw, 16 * NB)
            sp.wait_ge(s_x1w, 16 * NB)
            sp.wait_ge(s_lg, NB)
            for k in range(2):
                sp.dma_start(xtb[:, k, :, :].rearrange("p n q -> p (n q)"), xt_dram[k]).then_inc(s_xt[k], 16)
            sp.dma_start(x1b, x1_rows[0]).then_inc(s_x1i, 16)

            def routed_weights(n):
                sp.wait_ge(s_wlo_r, n)
                sp.dma_start(stage[0][:, 0:2 * D], item3(gu_w, SH + n)).then_inc(s_stage_r, 16)
                sp.dma_start(stage[0][:, 2 * D:3 * D], item3(dn_w, SH + n)).then_inc(s_stage_r, 16)

            def item3(d, i):
                return d[bass.ds(i, 1)].rearrange("a p n -> (a p) n")

            def shared_io(k, j, more_x, more_xt):
                sp.wait_ge(s_x1s, TB * (k + 1))
                sp.dma_start(item(x1s_rows, k), x1b).then_inc(s_x1sw, 16)
                if more_xt:
                    sp.dma_start(xtb[:, j, :, :].rearrange("p n q -> p (n q)"), item(xt_dram, k + 2)).then_inc(s_xt[j], 16)
                if more_x:
                    sp.wait_ge(s_x1sw, 16 * (k + 1))
                    sp.dma_start(x1b, item(x1_rows, k + 1)).then_inc(s_x1i, 16)

            with sp.Fori(0, FIRST // 2) as i:
                for j in range(2):
                    for e in range(E // FIRST):
                        routed_weights((2 * i + j) * (E // FIRST) + e)
                    shared_io(2 * i + j, j, True, True)
            with sp.Fori(0, BLOCKS // 2) as i:
                for j in range(2):
                    sp.wait_ge(s_ye, 2 * i + j + 1)
                    sp.dma_start(item(y_tiles, 2 * i + j), y_sb[:, j, :]).then_inc(s_yw[j], 16)
            for k in range(FIRST, NB):
                shared_io(k, k % 2, k + 1 < NB, k + 2 < NB)
            sp.wait_ge(s_x1sw, 16 * NB)
            for j in range(2):
                sp.wait_ge(s_yw[j], 16 * BLOCKS // 2)

        @block.tensor
        def _(pe):
            mm, turn = nc.tensor.matmul, nc.tensor.transpose

            def project(dst, lhs, rhs):
                for k in range(KC):
                    last = mm(dst, lhs(k), rhs(k), start=(k == 0), stop=(k == KC - 1))
                last.then_inc(s_mm, 1)

            pe.wait_ge(s_const, 16)
            pe.wait_ge(s_kw, 48)
            for c in range(KC):
                project(bank[c][:, 0:B * M], lambda k: wk_sb[:, k, c * P:c * P + P], lambda k: ctx_sb[:, k, :])
            pe.wait_ge(s_qw, 16)
            pe.wait_ge(s_mm_sb, 4)
            for c in range(KC):
                project(bank[4 + c][:, 0:B * M], lambda k: wq_sb[:, k, c * P:c * P + P], lambda k: kT[:, k, :])
            for b in range(B):
                for k in range(KC):
                    last = mm(bank[0][:, b:b + 1], kT[:, k, b * M:b * M + M], bias_sb[:, k:k + 1],
                              start=(k == 0), stop=(k == KC - 1))
            last.then_inc(s_mm, 1)
            pe.wait_ge(s_mm_sb, 9)
            for q in range(NB):
                for t in range(TB):
                    pe.wait_ge(s_xn, q * TB + t + 1)
                    if q:
                        pe.wait_ge(s_tp_sb, (q - 1) * TB + t + 1)
                    for k in range(KC):
                        last = turn(bank[t][:, k * P:k * P + P], xn[:, t, k * P:k * P + P], c_sb[:, C_ID:C_ID + P])
                    last.then_inc(s_tp, 1)
                pe.wait_ge(s_tp_sb, q * TB + TB)
                if q >= 2:
                    pe.wait_ge(s_pt_sb, q - 1)
                b = q // 4
                for k in range(KC):
                    last = mm(bank[4 + q % 2][:, :], g_sb[:, k, b * M:b * M + M], xnT[q % 2][:, k, :],
                              start=(k == 0), stop=(k == KC - 1))
                last.then_inc(s_pt, 1)
            pe.wait_ge(s_vw, 16)
            for c in range(KC):
                project(bank[c][:, 0:B * M], lambda k: wv_sb[:, k, c * P:c * P + P], lambda k: ctx_sb[:, k, :])
            pe.wait_ge(s_ow, 16)
            pe.wait_ge(s_mm_sb, 13)
            pe.wait_ge(s_pt_sb, NB)
            for b in range(B):
                project(bank[4 + b][:, :], lambda k: vT[:, k, b * M:b * M + M], lambda k: wo_sb[:, k, :])
            for b in range(B):
                pe.wait_ge(s_sk[b], 32)
                if b:
                    pe.wait_ge(s_mT_sb, b)
                for a in range(NA):
                    mm(bank[6][:, 2 * a:2 * a + 2], skew_c[:, a * P:a * P + P], c_sb[:, C_ONES:C_ONES + 2],
                       start=True, stop=False)
                    last = mm(bank[6][:, 2 * a:2 * a + 2], skew_d[:, a * P:a * P + P],
                              c_sb[:, C_ONES + 2:C_ONES + 4], start=False, stop=True)
                last.then_inc(s_u, 1)
                pe.wait_ge(s_u_sb, 3 * (b + 1))
                e = bank[7][:, 0:2 * NA].rearrange("p (v a) -> p v a", v=2)
                mm(e, c_sb[:, C_ID:C_ID + P], sums, start=True, stop=False)
                mm(e, c_sb[:, C_J0:C_J0 + P], mirrored[:, :, 0:NA], start=False, stop=False)
                mm(e, c_sb[:, C_J1:C_J1 + P], mirrored[:, :, 1:NA + 1], start=False, stop=True).then_inc(s_ev, 1)
                pe.wait_ge(s_ev_sb, 3 * (b + 1))
                m = bank[7][:, 64:64 + NA]
                mm(m, c_sb[:, C_IS:C_IS + P], even_s, start=True, stop=False)
                for a in range(NA):
                    last = mm(m, c_sb[:, C_T + a * P:C_T + a * P + P], even_w[:, NA - a:2 * NA - a],
                              start=False, stop=(a == NA - 1))
                last.then_inc(s_mean, 1)
                pe.wait_ge(s_mean_sb, b + 1)
                turn(bank[6][0:NA, 64:64 + P], mean_sb, c_sb[:, C_ID:C_ID + P]).then_inc(s_mT, 1)

            pe.wait_ge(s_rt, 3)
            pe.wait_ge(s_mm_sb, 15)

            def attention(k, j):
                pe.wait_ge(s_st[j], 16 * ((k >> 1) + 1))
                for t in range(TB):
                    if not isinstance(k, int) or k * TB + t >= 2:
                        pe.wait_ge(s_x1, k * TB + t - 1)
                    mm(bank[t % 2][:, :], st[j][:, t * P:t * P + P], only(vo, k // (NB // B)), start=True, stop=True
                       ).then_inc(s_at, 1)

            def turn_and_route(k, j):
                pe.wait_ge(s_hi, k + 1)
                pe.wait_ge(s_lo, k + 1)
                for t in range(TB):
                    if not isinstance(k, int) or k * TB + t >= 2:
                        pe.wait_ge(s_tp2_sb, k * TB + t - 1)
                    for n in range(2 * KC):
                        src = (hi16, lo16)[n // KC]
                        last = turn(bank16[2 + t % 2][:, n * P:n * P + P], src[:, t, n % KC * P:n % KC * P + P], id16)
                    last.then_inc(s_tp2, 1)
                for t in range(TB):
                    pe.wait_ge(s_tp2_sb, k * TB + t + 1)
                    lg = bank[4][:, bass.ds((k * TB + t) * E, E)]
                    n = 0
                    for xv, wp in PARTS:
                        for c in range(KC):
                            last = mm(lg, xtb[:, j, xv * KC + c, t * P:t * P + P], (rt_hi, rt_lo)[wp][:, c, :],
                                      start=(n == 0), stop=(n == 3 * KC - 1))
                            n += 1
                last.then_inc(s_lg, 1)

            attention(0, 0)
            attention(1, 1)
            turn_and_route(0, 0)
            with pe.Fori(0, NB // 2 - 1) as i:
                for j in range(2):
                    attention(2 * i + 2 + j, j)
                    turn_and_route(2 * i + 1 + j, 1 - j)
            turn_and_route(NB - 1, 1)

            pe.wait_ge(s_chosen, 1)
            mm(bank[5][:, :], tri16, chosen, start=True, stop=False)
            for t in range(T - 1, 1, -1):
                mm(bank[5][:, t * E:T * E], ones16, chosen[:, 0:(T - t) * E], start=False, stop=False, skip_group_check=True)
            mm(bank[5][:, :], ones16, chosen_after[:, 0:T * E], start=False, stop=True)
            for t in range(T):
                last = mm(bank[6][:, 0:E], ones16, chosen[:, t * E:t * E + E], start=(t == 0), stop=(t == T - 1))
            last.then_inc(s_rank, 1)

            pe.wait_ge(s_whi, SH)
            pe.wait_ge(s_wlo, SH)

            def shared_gate_up(k, j, c, first):
                for g, s_done, s_read in ((0, s_sg, s_ss), (1, s_su, s_sh32)):
                    if not first:
                        pe.wait_ge(s_read, k * SH + c)
                    n = 0
                    for xv, wp in PARTS:
                        for kc in range(KC):
                            w = only((gu_hi_s, gu_lo_s)[wp], c, slice(kc * 2 * H + g * H, kc * 2 * H + g * H + H))
                            last = mm(bank[g][:, :], w, xtb[:, j, xv * KC + kc, :],
                                      start=(n == 0), stop=(n == 3 * KC - 1))
                            n += 1
                    last.then_inc(s_done, 1)

            def shared_down(k, c, half, first, final):
                pe.wait_ge(s_shl, k * SH + c + 1)
                for t in range(TB):
                    for n, (hv, wp) in enumerate(PARTS):
                        last = mm(bank[2 + t][:, :], s_hb[:, half, hv, t * P:t * P + P], only((dn_hi_s, dn_lo_s)[wp], c),
                                  start=(first and n == 0), stop=(final and n == 2))
                last.then_inc(s_sd, 1)

            def shared(k, j, again):
                pe.wait_ge(s_xt[j], 16 * ((k >> 1) + 1))
                if again:
                    pe.wait_ge(s_sh32, k * SH)
                shared_gate_up(k, j, 0, True)
                shared_gate_up(k, j, 1, False)
                if again:
                    pe.wait_ge(s_x1s, k * TB)
                shared_down(k, 0, 0, True, False)
                with pe.Fori(0, SH // 2 - 1) as i:
                    for h in range(2):
                        shared_gate_up(k, j, 2 * i + 2 + h, False)
                        shared_down(k, 2 * i + 1 + h, 1 - h, False, False)
                shared_down(k, SH - 1, 1, False, True)

            pe.wait_ge(s_put, 1)
            with pe.Fori(0, FIRST // 2) as i:
                for j in range(2):
                    shared(2 * i + j, j, True)

            pe.wait_ge(s_sh32, FIRST * SH)
            pe.wait_ge(s_x1s, FIRST * TB)
            pe.wait_ge(s_whi_r, E)
            pe.wait_ge(s_wlo_r, E)
            pe.wait_ge(s_expert, 1)

            def experts(at):
                return nc.values_load_multi_w_load_instructions(
                    blocks_e[0:1, bass.ds(at, 8)], engines=[mybir.EngineType.PE], min_val=0, max_val=E - 1)[1]

            def turn_rows(s, r, j, fresh):
                pe.wait_ge(s_xg[r], 16 * ((s >> 2) + 1))
                if not fresh:
                    pe.wait_ge(s_txe, s - 1)
                for n in range(2 * KC):
                    last = turn(bank16[j][:, n * P:n * P + P], xg[:, r, n * P:n * P + P], id16)
                last.then_inc(s_tx, 1)

            def gate_up(s, j, e, fresh):
                pe.wait_ge(s_txe, s + 1)
                if not fresh:
                    pe.wait_ge(s_rh, s - 1)
                n = 0
                for xv, wp in PARTS:
                    for kc in range(KC):
                        last = mm(bank[2 + j][:, 0:2 * H], xgT[:, j, xv * KC + kc, :],
                                  only((gu_hi_r, gu_lo_r)[wp], e, slice(kc * 2 * H, (kc + 1) * 2 * H)),
                                  start=(n == 0), stop=(n == 3 * KC - 1))
                        n += 1
                last.then_inc(s_rg, 1)

            def turn_h(s, j, fresh):
                pe.wait_ge(s_rhl, s + 1)
                if not fresh:
                    pe.wait_ge(s_hte, s - 1)
                for v in range(2):
                    last = turn(bank16[4 + j][:, v * P:v * P + P], r_hb[:, j, v, :], id16)
                last.then_inc(s_ht, 1)

            def down(s, j, e, fresh):
                pe.wait_ge(s_hte, s + 1)
                if not fresh:
                    pe.wait_ge(s_ye, s - 1)
                for n, (hv, wp) in enumerate(PARTS):
                    last = mm(bank[6 + j][:, :], r_hT[:, j, hv, :], only((dn_hi_r, dn_lo_r)[wp], e),
                              start=(n == 0), stop=(n == 2))
                last.then_inc(s_rd, 1)

            e = experts(0)
            turn_rows(0, 0, 0, True)
            turn_rows(1, 1, 1, True)
            gate_up(0, 0, e[0], True)
            turn_rows(2, 2, 0, False)
            gate_up(1, 1, e[1], True)
            turn_h(0, 0, True)
            def four(i, first):
                e = experts(4 * i)
                for n in range(4):
                    s = 4 * i + 1 + n
                    turn_rows(s + 2, (3 + n) % 4, (1 + n) % 2, False)
                    gate_up(s + 1, n % 2, e[n + 2], False)
                    turn_h(s, (1 + n) % 2, first and n == 0)
                    down(s - 1, n % 2, e[n], first and n < 2)

            four(0, True)
            with pe.Fori(1, BLOCKS // 4 - 1) as i:
                four(i, False)
            e = experts(BLOCKS - 4)
            turn_rows(BLOCKS - 1, 3, 1, False)
            gate_up(BLOCKS - 2, 0, e[2], False)
            turn_h(BLOCKS - 3, 1, False)
            down(BLOCKS - 4, 0, e[0], False)
            gate_up(BLOCKS - 1, 1, e[3], False)
            turn_h(BLOCKS - 2, 0, False)
            down(BLOCKS - 3, 1, e[1], False)
            turn_h(BLOCKS - 1, 1, False)
            down(BLOCKS - 2, 0, e[2], False)
            down(BLOCKS - 1, 1, e[3], False)

            pe.wait_ge(s_ye, BLOCKS)
            with pe.Fori(FIRST // 2, NB // 2) as i:
                for j in range(2):
                    shared(2 * i + j, j, True)

        @block.scalar
        def _(act):
            A = nc.scalar.activation

            for c in range(KC):
                act.wait_ge(s_mm, c + 1)
                A(kT[:, c, :], bank[c][:, 0:B * M], ACT.Identity, bias=bias_sb[:, KC + c:KC + c + 1]).then_inc(s_mm_sb, 1)
            for c in range(KC):
                act.wait_ge(s_mm, 4 + c + 1)
                A(g_sb[:, c, :], bank[4 + c][:, 0:B * M], ACT.Copy).then_inc(s_mm_sb, 1)
            act.wait_ge(s_mm, 9)
            A(bqk, bank[0][:, 0:B], ACT.Copy).then_inc(s_mm_sb, 1)
            act.wait_ge(s_mm_sb, 9)

            def save_pt(q):
                b, n = q // 4, q % 4
                act.wait_ge(s_pt, q + 1)
                src, bias = bank[4 + q % 2], bqk[:, b:b + 1]
                if n == 0:
                    A(pt[b][:, M + L:PTW], src[:, 0:M], ACT.Identity, bias=bias)
                if n == 3:
                    A(pt[b][:, 0:M], src[:, BLK - M:BLK], ACT.Identity, bias=bias)
                A(pt[b][:, M + n * BLK:M + (n + 1) * BLK], src[:, :], ACT.Identity, bias=bias).then_inc(s_pt_sb, 1)

            for q in range(NB):
                act.wait_ge(s_var, q + 1)
                A(std, var_eps, ACT.Sqrt).then_inc(s_std, 1)
                if q:
                    save_pt(q - 1)
                for t in range(TB):
                    act.wait_ge(s_tp, q * TB + t + 1)
                    A(xnT[q % 2][:, :, t * P:t * P + P], bank[t][:, :].rearrange("p (k n) -> p k n", k=KC), ACT.Copy
                      ).then_inc(s_tp_sb, 1)
            save_pt(NB - 1)
            for c in range(KC):
                act.wait_ge(s_mm, 9 + c + 1)
                A(vT[:, c, :], bank[c][:, 0:B * M], ACT.Identity, bias=bias_sb[:, 2 * KC + c:2 * KC + c + 1]
                  ).then_inc(s_mm_sb, 1)
            for b in range(B):
                act.wait_ge(s_mm, 13 + b + 1)
                A(vo[:, b, :], bank[4 + b][:, :], ACT.Copy).then_inc(s_mm_sb, 1)
            def softmax(b):
                nc.scalar.wait_ge(s_best, b + 1)
                nc.scalar.activation(top_e[0:1, :], best[0:1, :], ACT.Exp, bias=negmax[0:1, :],
                                     accum_out=total[0:1, :]).then_inc(s_exp, 1)
                nc.scalar.activation(row[0:1, :], row[0:1, :], ACT.Exp, bias=negmax[0:1, :]).then_inc(s_exp, 1)

            act.wait_ge(s_mm_sb, 15)
            for n in range(SH):
                act.wait_ge(s_stage[n % 2], 32 * (n // 2 + 1))
                A(gu_hi_s[:, n, :], stage[n % 2][:, 0:2 * D], ACT.Copy, scale=WS)
                A(dn_hi_s[:, n, :], stage[n % 2][:, 2 * D:3 * D], ACT.Copy, scale=WS).then_inc(s_whi, 1)
                if n == 2:
                    softmax(0)
            softmax(1)

            def second_norm(k, j):
                act.wait_ge(s_var2, k + 1)
                A(std, var_eps, ACT.Sqrt).then_inc(s_std2, 1)
                act.wait_ge(s_xn2, TB * (k + 1))
                if not isinstance(k, int) or k:
                    act.wait_ge(s_tp2, TB * k)
                    act.wait_ge(s_xrw, 32 * k)
                A(hi16, xn, ACT.Copy).then_inc(s_hi, 1)
                if not isinstance(k, int) or k >= 2:
                    act.wait_ge(s_xtw, 16 * (k - 1))
                    act.wait_ge(s_lg, k - 1)
                for t in range(TB):
                    act.wait_ge(s_tp2, k * TB + t + 1)
                    A(xtb[:, j, :, t * P:t * P + P], bank16[2 + t % 2].rearrange("p (n q) -> p n q", n=2 * KC), ACT.Copy
                      ).then_inc(s_tp2_sb, 1)

            for j in range(2):
                second_norm(j, j)
            with act.Fori(1, NB // 2) as i:
                for j in range(2):
                    second_norm(2 * i + j, j)
            act.wait_ge(s_lg, NB)
            A(scores, bank[4][:, :], ACT.Sigmoid, scale=1.0 / WS).then_inc(s_sig, 1)

            def shared_chunk(k, c, h):
                n = k * SH + c
                act.wait_ge(s_sg, n + 1)
                act.wait_ge(s_sh32, n)
                A(s_silu, bank[0][:, :], ACT.Silu, scale=1.0 / WS).then_inc(s_ss, 1)
                act.wait_ge(s_sh32, n + 1)
                if not isinstance(n, int) or n >= 2:
                    act.wait_ge(s_sd, n - 1)
                A(s_hb[:, h, 0, :], s_h, ACT.Copy).then_inc(s_shh, 1)

            def routed_weights_hi(n):
                act.wait_ge(s_stage_r, 32 * (n + 1))
                A(only(gu_hi_r, n), stage[0][:, 0:2 * D], ACT.Copy, scale=WS)
                A(only(dn_hi_r, n), stage[0][:, 2 * D:3 * D], ACT.Copy, scale=WS).then_inc(s_whi_r, 1)

            act.wait_ge(s_x1w, 16 * NB)
            act.wait_ge(s_xn2, TB * NB)
            for h in range(2):
                shared_chunk(0, h, h)
            routed_weights_hi(0)
            with act.Fori(1, FIRST * SH // 2) as i:
                for h in range(2):
                    shared_chunk(0, 2 * i + h, h)
                routed_weights_hi(i)

            def silu_hi(s, j, fresh):
                act.wait_ge(s_rg, s + 1)
                if not fresh:
                    act.wait_ge(s_rh, s - 1)
                A(r_silu[:, j, :], bank[2 + j][:, 0:H], ACT.Silu, scale=1.0 / WS).then_inc(s_rs, 1)
                act.wait_ge(s_rh, s + 1)
                if not fresh:
                    act.wait_ge(s_ht, s - 1)
                A(r_hb[:, j, 0, :], r_h[:, j, :], ACT.Copy).then_inc(s_rhh, 1)

            def save_y(s, j, half):
                act.wait_ge(s_rd, s + 1)
                if not isinstance(half, int) or half:
                    act.wait_ge(s_yw[j], 16 * half)
                A(y_sb[:, j, :], bank[6 + j][:, :], ACT.Copy, scale=1.0 / WS).then_inc(s_ye, 1)

            silu_hi(0, 0, True)
            silu_hi(1, 1, True)
            with act.Fori(0, BLOCKS // 4 - 1) as i:
                for n in range(4):
                    silu_hi(4 * i + 2 + n, n % 2, False)
                    save_y(4 * i + n, n % 2, 2 * i + n // 2)
            for n in range(2):
                silu_hi(BLOCKS - 2 + n, n, False)
                save_y(BLOCKS - 4 + n, n, BLOCKS // 2 - 2)
            for n in range(2):
                save_y(BLOCKS - 2 + n, n, BLOCKS // 2 - 1)

            def take(m, j):
                if not isinstance(m, int) or m >= 2:
                    act.wait_ge(s_cmb, TOP_E * (m - 2) + 1)
                act.dma_start(x1c[:, j, :], item(x1s_tiles, m)).then_inc(s_x1c[j], 16)

            def give(m, j):
                act.wait_ge(s_cmb, TOP_E * (m + 1))
                act.dma_start(item(out_tiles, m), ybuf[j][:, TOP_E - 1, :]).then_inc(s_out[j], 16)

            act.wait_ge(s_rd, BLOCKS)
            act.wait_ge(s_x1sw, 16 * FIRST)
            for c in range(SH):
                shared_chunk(FIRST, c, c % 2)
                m = c - LAG
                if m >= 0:
                    if m:
                        give(m - 1, (m - 1) % 2)
                    if m == 0:
                        take(0, 0)
                    take(m + 1, (m + 1) % 2)
            with act.Fori(FIRST + 1, NB) as k:
                act.wait_ge(s_x1sw, 16 * k)
                for c in range(SH):
                    shared_chunk(k, c, c % 2)
                    m = (k - FIRST) * SH + c - LAG
                    give(m - 1, (c - LAG + 1) % 2)
                    take(m + 1, (c - LAG + 1) % 2)
            act.wait_ge(s_x1sw, 16 * NB)
            for m in range(T - LAG, T):
                give(m - 1, (m - 1) % 2)
                if m + 1 < T:
                    take(m + 1, (m + 1) % 2)
            give(T - 1, (T - 1) % 2)
            for j in range(2):
                act.wait_ge(s_out[j], 16 * T // 2)

        @block.vector
        def _(dve):
            link = Links(dve, s_dve)
            V = nc.vector

            for q in range(NB):
                dve.wait_ge(s_x[q], 16)
                for t in range(TB):
                    link.start(V.bn_stats(stats[:, t, :], x_sb[:, q * TB + t, :]))
                link.wait()
                if q:
                    dve.wait_ge(s_xn, q * TB)
                for t in range(TB):
                    link.start(V.bn_aggr(mv[:, t, :], stats[:, t, :]))
                link.wait()
                V.tensor_scalar(var_eps, mv[:, :, 1], EPS, None, ALU.add).then_inc(s_var, 1)
                dve.wait_ge(s_std, q + 1)
                link.done(V.reciprocal(rstd, std))
                for t in range(TB):
                    if q:
                        dve.wait_ge(s_tp, (q - 1) * TB + t + 1)
                    V.tensor_scalar(xn[:, t, :], x_sb[:, q * TB + t, :], mv[:, t, 0:1], rstd[:, t:t + 1],
                                    ALU.subtract, ALU.mult).then_inc(s_xn, 1)
                if q == 2:
                    dve.wait_ge(s_misc, 64)
                    dve.wait_ge(s_const, 16)
                    r3 = rt32.rearrange("p (k e) -> p k e", k=KC)
                    link.done(V.tensor_scalar(rt_hi, r3, WS, None, ALU.mult))
                    V.scalar_tensor_tensor(rt_lo, r3, WS, rt_hi, ALU.mult, ALU.subtract).then_inc(s_rt, 1)
                    V.tensor_copy(id16, c_sb[:, C_ID:C_ID + P]).then_inc(s_rt, 1)
                    V.tensor_copy(tri16, cr_sb[:, R_TRI:R_TRI + P])
                    V.memset(chosen_after[:, 0:E], 0.0)
                    V.memset(ones16, 1.0).then_inc(s_rt, 1)

            def mean_correlation(b):
                dve.wait_ge(s_u, b + 1)
                u = bank[6][:, 0:2 * NA].rearrange("p (a v) -> p v a", v=2)
                V.tensor_copy(sums, u).then_inc(s_u_sb, 1)
                V.tensor_copy(mirrored[:, :, 0:1], u[:, :, 0:1]).then_inc(s_u_sb, 1)
                V.tensor_copy(mirrored[:, :, 1:NA + 1], u[:, :, ::-1]).then_inc(s_u_sb, 1)
                dve.wait_ge(s_ev, b + 1)
                V.tensor_copy(even_s, bank[7][:, 0:NA]).then_inc(s_ev_sb, 1)
                V.tensor_copy(even_w[:, 0:NA], bank[7][:, NA:2 * NA]).then_inc(s_ev_sb, 1)
                V.tensor_copy(even_w[:, NA:2 * NA], bank[7][:, NA:2 * NA]).then_inc(s_ev_sb, 1)
                dve.wait_ge(s_mean, b + 1)
                V.tensor_copy(mean_sb, bank[7][:, 64:64 + NA]).then_inc(s_mean_sb, 1)
                dve.wait_ge(s_mT, b + 1)
                if b:
                    dve.wait_ge(s_mw[0], 16)
                V.tensor_copy(meanT[0:NA, :], bank[6][0:NA, 64:64 + P]).then_inc(s_mT_sb, 1)

            def delays(b):
                r, k = row[0:1, :], taken[0:1, :]
                dve.wait_ge(s_row[b], 16)
                link.done(V.max(best[0:1, 0:8], r))
                link.done(V.match_replace(k, best[0:1, 0:8], r, GONE))
                link.done(V.max(best[0:1, 8:16], k))
                link.start(V.memset(best[0:1, TOP_K:16], GONE))
                link.start(V.tensor_scalar(negmax[0:1, :], best[0:1, 0:1], -1.0, None, ALU.mult))
                link.wait()
                V.match_replace(k, best[0:1, 8:16], k, GONE).then_inc(s_best, 1)
                dve.wait_ge(s_best, b + 1)
                dve.wait_ge(s_exp, 2 * b + 2)
                link.done(V.reciprocal(inv[0:1, :], total[0:1, :]))
                link.done(V.tensor_scalar(k, k, GONE, inv[0:1, :], ALU.is_le, ALU.mult))
                V.tensor_tensor(r, r, k, ALU.mult).then_inc(s_g, 1)

            mean_correlation(0)
            delays(0)
            mean_correlation(1)
            delays(1)

            dve.wait_ge(s_wlo, SH)
            dve.wait_ge(s_xbo, NB)
            with dve.Fori(0, NB) as k:
                for t in range(TB):
                    n = k * TB + t
                    xr = only(x_sb, n)
                    dve.wait_ge(s_at, n + 1)
                    V.tensor_tensor(xr, bank[t % 2][:, :], xr, ALU.add).then_inc(s_x1, 1)
                    settled(dve)
                    dve.wait_ge(s_x1, n + 1)
                    V.bn_stats(stats[:, t, :], xr).then_inc(s_bn, 1)
                settled(dve)
                dve.wait_ge(s_bn, k * TB + TB)
                for t in range(TB):
                    V.bn_aggr(mv[:, t, :], stats[:, t, :]).then_inc(s_mv, 1)
                dve.wait_ge(s_mv, k * TB + TB)
                V.tensor_scalar(var_eps, mv[:, :, 1], EPS, None, ALU.add).then_inc(s_var2, 1)
                dve.wait_ge(s_std2, k + 1)
                V.reciprocal(rstd, std).then_inc(s_rstd, 1)
                dve.wait_ge(s_rstd, k + 1)
                dve.wait_ge(s_hi, k)
                dve.wait_ge(s_lo, k)
                for t in range(TB):
                    V.tensor_scalar(xn[:, t, :], only(x_sb, k * TB + t), mv[:, t, 0:1], rstd[:, t:t + 1],
                                    ALU.subtract, ALU.mult).then_inc(s_xn2, 1)

            def tiles(v, n=E):
                return v.rearrange("p (t e) -> p t e", e=n)

            dve.wait_ge(s_sig, 1)
            dve.wait_ge(s_lo, NB)
            dve.wait_ge(s_xrw, 32 * NB)
            link.done(V.tensor_tensor(tiles(biased), tiles(scores), cb_sb.unsqueeze(1).broadcast_to([P, T, E]), ALU.add))
            G4 = T * GROUPS
            pairs = biased.rearrange("p (g a) -> p g a", a=2)
            hi2, lo2 = tmp[:, 0:2 * G4], tmp[:, 2 * G4:4 * G4]
            one = lambda v: v.unsqueeze(2)
            link.start(V.tensor_tensor(one(hi2), pairs[:, :, 0:1], pairs[:, :, 1:2], ALU.max))
            link.done(V.tensor_tensor(one(lo2), pairs[:, :, 0:1], pairs[:, :, 1:2], ALU.min))
            hv, lv = (v.rearrange("p (g a) -> p g a", a=2) for v in (hi2, lo2))
            m1, m2, m3 = (cnt[:, i * G4:(i + 1) * G4] for i in range(3))
            link.start(V.tensor_tensor(one(m1), hv[:, :, 0:1], hv[:, :, 1:2], ALU.max))
            link.start(V.tensor_tensor(one(m2), hv[:, :, 0:1], hv[:, :, 1:2], ALU.min))
            link.done(V.tensor_tensor(one(m3), lv[:, :, 0:1], lv[:, :, 1:2], ALU.max))
            link.done(V.tensor_tensor(m2, m2, m3, ALU.max))
            link.done(V.tensor_tensor(m1, m1, m2, ALU.add))
            gs, rank, beats = tiles(m1, GROUPS), tiles(m2, GROUPS), tiles(m3, GROUPS)
            for i in range(GROUPS):
                link.start(V.memset(rank[:, :, i:i + 1], float(GROUPS - 1 - i)))
            for d in range(1, GROUPS):
                n = GROUPS - d
                link.done(V.tensor_tensor(beats[:, :, 0:n], gs[:, :, 0:n], gs[:, :, d:GROUPS], ALU.is_ge))
                link.done(V.tensor_tensor(rank[:, :, d:GROUPS], rank[:, :, d:GROUPS], beats[:, :, 0:n], ALU.add))
                link.done(V.tensor_tensor(rank[:, :, 0:n], rank[:, :, 0:n], beats[:, :, 0:n], ALU.subtract))
            link.done(V.tensor_scalar(m2, m2, float(TOP_GROUPS) - 0.5, 1.0e30, ALU.is_gt, ALU.mult))
            by_group = biased.rearrange("p (g a) -> p g a", a=PER_GROUP)
            link.done(V.tensor_tensor(by_group, by_group, m2.unsqueeze(2).broadcast_to([P, G4, PER_GROUP]), ALU.subtract))
            b3 = tiles(biased)
            for t in range(T):
                link.start(V.max(top8[:, t, :], b3[:, t, :]))
            link.wait()
            for t in range(T):
                link.start(V.max_index(top8_at[:, t, :], top8[:, t, :], b3[:, t, :]))
            link.wait()
            link.done(V.tensor_copy(top8_e, top8_at))
            expert = cr_sb[:, R_EXP:R_EXP + E].unsqueeze(1).broadcast_to([P, T, E])
            for i in range(TOP_E):
                link.start(V.tensor_tensor(tiles(picked[i]), expert, top8_e[:, :, i:i + 1].broadcast_to([P, T, E]),
                                           ALU.is_equal))
            link.wait()
            link.start(V.tensor_tensor(chosen, picked[0], picked[1], ALU.add))
            link.done(V.tensor_tensor(cnt, picked[2], picked[3], ALU.add))
            V.tensor_tensor(chosen, chosen, cnt, ALU.add).then_inc(s_chosen, 1)
            w3 = pair_w.rearrange("p (i t) -> p i t", i=TOP_E)
            for i in range(TOP_E):
                link.done(V.tensor_tensor(tmp, picked[i], scores, ALU.mult))
                link.done(V.tensor_reduce(w3[:, i, :], tiles(tmp), AX_X, ALU.add))
            link.done(V.tensor_reduce(tmp[:, 0:T], pair_w.rearrange("p (i t) -> p t i", i=TOP_E), AX_X, ALU.add))
            link.done(V.tensor_scalar(tmp[:, 0:T], tmp[:, 0:T], 1e-20, None, ALU.add))
            link.done(V.reciprocal(tmp[:, T:2 * T], tmp[:, 0:T]))
            link.done(V.tensor_tensor(w3, w3, tmp[:, T:2 * T].unsqueeze(1).broadcast_to([P, TOP_E, T]), ALU.mult))

            dve.wait_ge(s_rank, 1)
            def whole(v, src, low):
                link.done(V.tensor_scalar(v, src, 1.0 / P, low, ALU.mult, ALU.add))
                link.done(V.tensor_scalar(v, v, ROUND, ROUND, ALU.add, ALU.subtract))

            link.done(V.tensor_copy(load_e, bank[6][:, 0:E]))
            whole(nblk, load_e, (P - 1.0) / P - 0.5 + 0.5 / P)
            link.done(V.tensor_copy(first_a, nblk))
            src, dst = first_a, first_b
            for d in (1, 2, 4, 8):
                link.start(V.tensor_copy(dst[:, 0:d], src[:, 0:d]))
                link.done(V.tensor_tensor(dst[:, d:E], src[:, d:E], src[:, 0:E - d], ALU.add))
                src, dst = dst, src
            link.done(V.tensor_copy(last_blk, src))
            link.done(V.tensor_tensor(first_b, last_blk, nblk, ALU.subtract))
            link.done(V.tensor_scalar(first_b, first_b, float(P), None, ALU.mult))
            link.done(V.tensor_tensor(tiles(slot), bank[5][:, :].rearrange("p (t e) -> p t e", e=E),
                                      first_b.unsqueeze(1).broadcast_to([P, T, E]), ALU.add))
            sl3 = pair_slot.rearrange("p (i t) -> p i t", i=TOP_E)
            for i in range(TOP_E):
                link.done(V.tensor_tensor(tmp, picked[i], slot, ALU.mult))
                link.done(V.tensor_reduce(sl3[:, i, :], tiles(tmp), AX_X, ALU.add))
            whole(pair_blk, pair_slot, -0.5 + 0.5 / P)
            link.start(V.tensor_copy(row_of, pair_slot))
            link.done(V.tensor_scalar(pair_blk, pair_blk, 1.0 - P * BLOCKS, None, ALU.mult))
            link.done(V.scalar_tensor_tensor(pair_blk, pair_slot, float(BLOCKS), pair_blk, ALU.mult, ALU.add))
            V.tensor_copy(put_at, pair_blk).then_inc(s_put, 1)
            link.done(V.memset(tmp[:, 0:BLOCKS], 0.0))
            for e in range(E - 1):
                link.done(V.scalar_tensor_tensor(tmp[:, 0:BLOCKS], cr_sb[:, R_BLK:R_BLK + BLOCKS], last_blk[:, e:e + 1],
                                                 tmp[:, 0:BLOCKS], ALU.is_ge, ALU.add))
            link.start(V.memset(blocks_e[:, BLOCKS:BLOCKS + 8], 0))
            link.done(V.tensor_copy(blocks_e[:, 0:BLOCKS], tmp[:, 0:BLOCKS]))
            V.engine_nop().then_inc(s_expert, 1)

            def shared_chunk(k, c, h):
                n = k * SH + c
                dve.wait_ge(s_ss, n + 1)
                dve.wait_ge(s_su, n + 1)
                if not isinstance(n, int) or n >= 1:
                    dve.wait_ge(s_shh, n)
                    dve.wait_ge(s_shl, n)
                V.scalar_tensor_tensor(s_h, bank[1][:, :], 1.0 / WS, s_silu, ALU.mult, ALU.mult).then_inc(s_sh32, 1)
                dve.wait_ge(s_shh, n + 1)
                V.tensor_tensor(s_hb[:, h, 1, :], s_h, s_hb[:, h, 0, :], ALU.subtract).then_inc(s_shl, 1)

            def shared_sum(k):
                dve.wait_ge(s_sd, SH * (k + 1))
                dve.wait_ge(s_x1i, 16 * (k + 1))
                for t in range(TB):
                    V.scalar_tensor_tensor(x1b[:, t, :], bank[2 + t][:, :], 1.0 / WS, x1b[:, t, :], ALU.mult, ALU.add
                                           ).then_inc(s_x1s, 1)

            def routed_weights_lo(n):
                dve.wait_ge(s_whi_r, n + 1)
                V.scalar_tensor_tensor(only(gu_lo_r, n), stage[0][:, 0:2 * D], WS, only(gu_hi_r, n), ALU.mult, ALU.subtract)
                V.scalar_tensor_tensor(only(dn_lo_r, n), stage[0][:, 2 * D:3 * D], WS, only(dn_hi_r, n),
                                       ALU.mult, ALU.subtract).then_inc(s_wlo_r, 1)

            with dve.Fori(0, FIRST) as k:
                with dve.Fori(0, SH // 2) as i:
                    for h in range(2):
                        shared_chunk(k, 2 * i + h, h)
                    routed_weights_lo(k * (SH // 2) + i)
                shared_sum(k)

            def save_rows(s, j, fresh):
                dve.wait_ge(s_tx, s + 1)
                if not fresh:
                    dve.wait_ge(s_rg, s - 1)
                V.tensor_copy(xgT[:, j, :, :], bank16[j].rearrange("p (n q) -> p n q", n=2 * KC)).then_inc(s_txe, 1)

            def save_h(s, j, fresh):
                dve.wait_ge(s_ht, s + 1)
                if not fresh:
                    dve.wait_ge(s_rd, s - 1)
                V.tensor_copy(r_hT[:, j, :, :], bank16[4 + j][:, 0:2 * P].rearrange("p (v q) -> p v q", v=2)
                              ).then_inc(s_hte, 1)

            def hidden(s, j, fresh):
                dve.wait_ge(s_rs, s + 1)
                if not fresh:
                    dve.wait_ge(s_rhh, s - 1)
                    dve.wait_ge(s_rhl, s - 1)
                V.scalar_tensor_tensor(r_h[:, j, :], bank[2 + j][:, H:2 * H], 1.0 / WS, r_silu[:, j, :], ALU.mult, ALU.mult
                                       ).then_inc(s_rh, 1)
                dve.wait_ge(s_rhh, s + 1)
                V.tensor_tensor(r_hb[:, j, 1, :], r_h[:, j, :], r_hb[:, j, 0, :], ALU.subtract).then_inc(s_rhl, 1)

            save_rows(0, 0, True)
            save_rows(1, 1, True)
            hidden(0, 0, True)
            save_rows(2, 0, False)
            hidden(1, 1, True)
            save_h(0, 0, True)
            with dve.Fori(0, BLOCKS // 4 - 1) as i:
                for n in range(4):
                    s = 4 * i + 1 + n
                    save_rows(s + 2, (1 + n) % 2, False)
                    hidden(s + 1, n % 2, False)
                    save_h(s, (1 + n) % 2, False)
            save_rows(BLOCKS - 1, 1, False)
            hidden(BLOCKS - 2, 0, False)
            save_h(BLOCKS - 3, 1, False)
            hidden(BLOCKS - 1, 1, False)
            save_h(BLOCKS - 2, 0, False)
            save_h(BLOCKS - 1, 1, False)

            def combine(m, j, half):
                dve.wait_ge(s_x1c[j], 16 * (half + 1))
                dve.wait_ge(s_yg[j], 16 * TOP_E * (half + 1))
                acc = x1c[:, j, :]
                for i in range(TOP_E):
                    if i:
                        dve.wait_ge(s_cmb, TOP_E * m + i)
                    y = ybuf[j][:, i, :]
                    w = pair_w[:, bass.ds(m + i * T, 1)]
                    V.scalar_tensor_tensor(y, y, w, acc, ALU.mult, ALU.add).then_inc(s_cmb, 1)
                    acc = y

            for c in range(SH):
                shared_chunk(FIRST, c, c % 2)
                if c >= LAG:
                    combine(c - LAG, (c - LAG) % 2, (c - LAG) // 2)
            shared_sum(FIRST)
            with dve.Fori(FIRST + 1, NB) as k:
                for c in range(SH):
                    shared_chunk(k, c, c % 2)
                    combine((k - FIRST) * SH + c - LAG, (c - LAG) % 2, (k - FIRST) * (SH // 2) + (c - LAG) // 2)
                shared_sum(k)
            for m in range(T - LAG, T):
                combine(m, m % 2, m // 2)

        @block.gpsimd
        def _(pool):
            pool.memset(token_of, 0).then_inc(s_zero, 1)
            pool.wait_ge(s_zero, 1)
            pool.dma_start(token_dram.rearrange("(p n) o -> p (n o)", p=P), token_of).then_inc(s_cleared, 16)
            pool.iota(token_id, pattern=[[P, T]], base=0, channel_multiplier=1).then_inc(s_ids, 1)
            pool.wait_ge(s_misc, 64)
            for q in range(NB):
                pool.wait_ge(s_xn, q * TB + TB)
                xq = x_sb[:, q * TB:q * TB + TB, :]
                pool.tensor_tensor(xq, xq, bo_sb.unsqueeze(1).broadcast_to([P, TB, D]), ALU.add).then_inc(s_xbo, 1)
            for n in range(SH):
                pool.wait_ge(s_whi, n + 1)
                w = stage[n % 2]
                pool.tensor_scalar(w, w, WS, 1.0, ALU.mult, ALU.mult).then_inc(s_w64, 1)
                pool.wait_ge(s_w64, n + 1)
                pool.tensor_tensor(gu_lo_s[:, n, :], w[:, 0:2 * D], gu_hi_s[:, n, :], ALU.subtract)
                pool.tensor_tensor(dn_lo_s[:, n, :], w[:, 2 * D:3 * D], dn_hi_s[:, n, :], ALU.subtract).then_inc(s_wlo, 1)
            with pool.Fori(0, NB) as k:
                pool.wait_ge(s_hi, k + 1)
                pool.wait_ge(s_tp2, TB * k)
                pool.wait_ge(s_xrw, 32 * k)
                pool.tensor_tensor(lo16, xn, hi16, ALU.subtract).then_inc(s_lo, 1)
            pool.wait_ge(s_put, 1)
            pool.wait_ge(s_ids, 1)
            pool.wait_ge(s_cleared, 16)
            put3 = put_at.rearrange("p (i t) -> p i t", i=TOP_E)
            row3 = row_of.rearrange("p (i t) -> p i t", i=TOP_E)

            def copy_places(t, r):
                pool.tensor_copy(put_now[:, r, :].unsqueeze(2), put3[:, :, bass.ds(t, 1)])
                pool.tensor_copy(id_now[:, r:r + 1], token_id[:, bass.ds(t, 1)]).then_inc(s_put_now, 1)

            def scatter(t, r, last):
                pool.wait_ge(s_put_now, t + 1)
                if not last:
                    n = (r + 1) % 4
                    if not isinstance(t, int) or t >= 3:
                        pool.wait_ge(s_scattered[n], 16 * TOP_E * ((t + 1) // 4))
                    copy_places(t + 1, n)
                for i in range(TOP_E):
                    pool.indirect_dma_start(
                        out=token_dram[:, :], out_offset=bass.IndirectOffsetOnAxis(ap=put_now[:, r, i:i + 1], axis=0),
                        in_=id_now[:, r:r + 1], in_offset=None).then_inc(s_scattered[r], 16)

            copy_places(0, 0)
            for t in range(4):
                scatter(t, t, False)
            with pool.Fori(1, T // 4 - 1) as h:
                for r in range(4):
                    scatter(4 * h + r, r, False)
            for r in range(4):
                scatter(T - 4 + r, r, r == 3)
            for r in range(4):
                pool.wait_ge(s_scattered[r], 16 * NP // P // 4)
            pool.dma_start(token_of, token_dram.rearrange("(p n) o -> p (n o)", p=P)).then_inc(s_tok, 16)
            pool.wait_ge(s_tok, 16)

            def copy_tokens(s, r):
                pool.tensor_copy(token_now[:, r:r + 1], token_of[:, bass.ds(s, 1)]).then_inc(s_token_now, 1)

            def gather(s, r, fresh, last):
                if not fresh:
                    pool.wait_ge(s_tx, s - 3)
                pool.wait_ge(s_token_now, s + 1)
                if not last:
                    copy_tokens(s + 1, (r + 1) % 8)
                pool.indirect_dma_start(
                    out=xg[:, r % 4, :], out_offset=None, in_=xr_dram[:, :],
                    in_offset=bass.IndirectOffsetOnAxis(ap=token_now[:, r:r + 1], axis=0)).then_inc(s_xg[r % 4], 16)

            copy_tokens(0, 0)
            for r in range(8):
                gather(r, r, r < 4, False)
            with pool.Fori(1, BLOCKS // 8 - 1) as i:
                for r in range(8):
                    gather(8 * i + r, r, False, False)
            for r in range(8):
                gather(BLOCKS - 8 + r, r, False, r == 7)
            for j in range(2):
                pool.wait_ge(s_yw[j], 16 * BLOCKS // 2)
            pool.wait_ge(s_rd, BLOCKS)

            def copy_rows(m, r):
                pool.tensor_copy(row_now[:, r, :].unsqueeze(2), row3[:, :, bass.ds(m, 1)]).then_inc(s_row_now, 1)

            def gather_y(m, r, half, last):
                j = r % 2
                if not isinstance(half, int) or half:
                    pool.wait_ge(s_out[j], 16 * half)
                pool.wait_ge(s_row_now, m + 1)
                if not last:
                    copy_rows(m + 1, (r + 1) % 4)
                for i in range(TOP_E):
                    pool.indirect_dma_start(
                        out=ybuf[j][:, i, :], out_offset=None, in_=y_dram[:, :],
                        in_offset=bass.IndirectOffsetOnAxis(ap=row_now[:, r, i:i + 1], axis=0)).then_inc(s_yg[j], 16)

            copy_rows(0, 0)
            for r in range(4):
                gather_y(r, r, r // 2, False)
            with pool.Fori(1, T // 4 - 1) as i:
                for r in range(4):
                    gather_y(4 * i + r, r, 2 * i + r // 2, False)
            for r in range(4):
                gather_y(T - 4 + r, r, T // 2 - 2 + r // 2, r == 3)


def kernel(x, ctx_1024, L0_xattn_Wq, L0_xattn_bq, L0_xattn_Wk, L0_xattn_bk, L0_xattn_Wv, L0_xattn_bv,
           L0_xattn_Wo, L0_xattn_bo, L0_ffn_router_w, L0_ffn_correction_bias, L0_ffn_gate_w, L0_ffn_up_w,
           L0_ffn_down_w, L0_ffn_shared_gate_w, L0_ffn_shared_up_w, L0_ffn_shared_down_w):
    import concourse.bacc as bacc
    from concourse.bass_utils import run_bass_kernel_spmd

    def chunks(w):
        w = np.asarray(w)
        return np.ascontiguousarray(w.reshape(-1, P, w.shape[-1]).transpose(1, 0, 2))

    def columns(v):
        return np.asarray(v).reshape(-1, P).T

    def rows(v):
        return np.ascontiguousarray(np.broadcast_to(np.asarray(v)[None, :], (P, len(v))))

    ctx = np.asarray(ctx_1024)[:, ::-1, :].reshape(B * M, D)
    gate = np.concatenate([np.asarray(L0_ffn_shared_gate_w).reshape(SH, H, D).transpose(0, 2, 1),
                           np.asarray(L0_ffn_gate_w)])
    up = np.concatenate([np.asarray(L0_ffn_shared_up_w).reshape(SH, H, D).transpose(0, 2, 1),
                         np.asarray(L0_ffn_up_w)])
    gu = np.concatenate([gate, up], axis=2).reshape(SH + E, KC, P, 2 * H).transpose(0, 2, 1, 3)
    dn = np.concatenate([np.asarray(L0_ffn_shared_down_w).T.reshape(SH, H, D), np.asarray(L0_ffn_down_w)])
    const, const_r = constants()
    arrays = {
        "x": np.ascontiguousarray(np.asarray(x).reshape(S, D)),
        "ctxT": chunks(ctx.T),
        "wk": chunks(L0_xattn_Wk), "wqT": chunks(np.asarray(L0_xattn_Wq).T),
        "wv": chunks(L0_xattn_Wv), "wo": chunks(L0_xattn_Wo),
        "biases": np.ascontiguousarray(np.concatenate(
            [columns(L0_xattn_bq), columns(L0_xattn_bk), columns(L0_xattn_bv)], axis=1)),
        "bo": rows(L0_xattn_bo), "cb": rows(L0_ffn_correction_bias),
        "routerT": np.ascontiguousarray(chunks(np.asarray(L0_ffn_router_w).T).reshape(P, KC * E)),
        "gu_w": np.ascontiguousarray(gu.reshape(SH + E, P, 2 * D)),
        "dn_w": np.ascontiguousarray(dn),
        "const": const, "const_r": const_r,
    }
    nc = bacc.Bacc("TRN2", target_bir_lowering=False, num_devices=1)
    args = {n: nc.dram_tensor(f"in_{n}", a.shape, F32, kind="ExternalInput").ap() for n, a in arrays.items()}
    out = nc.dram_tensor("out", (S, D), F32, kind="ExternalOutput").ap()
    build(nc, out=out, **args)
    got = run_bass_kernel_spmd(nc, [{f"in_{n}": a for n, a in arrays.items()}], core_ids=[0])
    return got.results[0]["out"].reshape(B, L, D)
```

```python
from contextlib import ExitStack

import numpy as np

import concourse.bass as bass
from concourse import mybir

F32 = mybir.dt.float32
F16 = mybir.dt.float16
ALU = mybir.AluOpType
ACT = mybir.ActivationFunctionType
AX_X = mybir.AxisListType.X

P = 128
B, L, D = 2, 2048, 512
M = 128
TOP_K = int(2 * np.log(L))
E, H = 16, 128
GROUPS, PER_GROUP, TOP_GROUPS, TOP_E = 4, 4, 2, 4
HS = 1024
SH = HS // H
KC = D // P
S = B * L
T = S // P
TB = 4
NB = S // (P * TB)
BLK = P * TB
NA = L // P
PTW = M + L + M
EPS = 1e-5
WS = 64.0
NP = S * TOP_E
BLOCKS = (NP + E * (P - 1)) // P + 1
FIRST = 4
OLD = FIRST * TB // (NB - FIRST)
TURNS = OLD + TB
ROUND = 12582912.0
GONE = -3.0e38

C_ID, C_ONES, C_J0, C_J1, C_IS, C_T = 0, 128, 132, 260, 388, 516
C_END = C_T + NA * P
R_EXP, R_BLK, R_TRI = 0, E, E + BLOCKS
R_END = R_TRI + P


def constants():
    c = np.zeros((P, C_END), np.float32)
    eye = np.eye(P, dtype=np.float32)
    c[:, C_ID:C_ID + P] = eye
    c[:, C_ONES:C_ONES + 4] = [1, 1, 1, -1]
    c[0, C_J0] = 1
    c[:, C_J1:C_J1 + P][1:, 1:] = eye[1:, 1:][::-1]
    scale = 1.0 / (4 * D)
    c[:, C_IS:C_IS + P] = eye * scale
    d = np.arange(L)
    hilbert = np.zeros(L)
    hilbert[1::2] = -2.0 / L / np.tan(np.pi * d[1::2] / L)
    q, p = np.arange(P)[:, None], np.arange(P)[None, :]
    for a in range(NA):
        c[:, C_T + a * P:C_T + (a + 1) * P] = scale * hilbert[(P * a + p - q) % L]
    r = np.zeros((P, R_END), np.float32)
    r[:, R_EXP:R_EXP + E] = np.arange(E)
    r[:, R_BLK:R_BLK + BLOCKS] = np.arange(BLOCKS)
    r[:, R_TRI:R_TRI + P] = q < p
    return c, r


class Links:

    def __init__(self, engine, semaphore):
        self.engine, self.semaphore, self.count = engine, semaphore, 0

    def start(self, instruction):
        self.count += 1
        instruction.then_inc(self.semaphore, 1)

    def wait(self):
        self.engine.wait_ge(self.semaphore, self.count)

    def done(self, instruction):
        self.start(instruction)
        self.wait()


def build(nc, x, ctxT, wk, wqT, wv, wo, biases, bo, cb, routerT, gu_w, dn_w, const, const_r, out):
    with ExitStack() as ctx:
        def sem(name):
            return ctx.enter_context(nc.semaphore(name))

        KB = 1024
        R1, R2, R3 = 48 * KB, 96 * KB, 65024
        arena = ctx.enter_context(nc.sbuf_tensor("arena", [P, (R1 + R2 + R3) // 4], F32))

        def view(offset, shape, dt=F32):
            n = int(np.prod(shape))
            v = arena[:, offset // 4:(offset + n * (2 if dt == F16 else 4)) // 4]
            if dt != F32:
                v = v.bitcast(dt)
            if len(shape) == 2:
                v = v.rearrange("p (a b) -> p a b", a=shape[0])
            elif len(shape) == 3:
                v = v.rearrange("p (a b c) -> p a b c", a=shape[0], b=shape[1])
            return v

        wk_sb, wq_sb = view(0, [KC, D]), view(8 * KB, [KC, D])
        wv_sb, wo_sb = view(16 * KB, [KC, D]), view(24 * KB, [KC, D])
        ctx_sb = view(32 * KB, [KC, B * M])
        kT, vT = view(36 * KB, [KC, B * M]), view(40 * KB, [KC, B * M])
        gu_hi_s, gu_lo_s = view(0, [SH, 2 * D], F16), view(16 * KB, [SH, 2 * D], F16)
        dn_hi_s, dn_lo_s = view(32 * KB, [SH, D], F16), view(40 * KB, [SH, D], F16)
        o = R1
        x_sb = view(o, [T, D])
        xnT = [view(o + 64 * KB, [KC, BLK]), view(o + 72 * KB, [KC, BLK])]
        skew_c, skew_d = view(o + 80 * KB, [L]), view(o + 88 * KB, [L])
        row, taken = view(o + 64 * KB, [L]), view(o + 72 * KB, [L])
        gu_hi_r, gu_lo_r = view(o, [E, 2 * D], F16), view(o + 32 * KB, [E, 2 * D], F16)
        dn_hi_r, dn_lo_r = view(o + 64 * KB, [E, D], F16), view(o + 80 * KB, [E, D], F16)
        scores, biased, tmp, cnt, slot = (view(o + 80 * KB + 2 * KB * i, [T * E]) for i in range(5))
        picked = [view(o + 90 * KB + KB * i, [T * E], F16) for i in range(TOP_E)]
        o1 = R1 + R2
        c_sb = view(o1, [C_END])
        vo = view(o1 + 10368, [B, D])
        st = [view(o1 + 14464, [BLK]), view(o1 + 16512, [BLK])]
        x1b = view(o1, [TB, D])
        s_silu, s_h = view(o1 + 8 * KB, [BLK]), view(o1 + 10 * KB, [BLK])
        s_hb = view(o1 + 12 * KB, [2, 2, BLK], F16)
        o2 = o1 + 18560
        pt = [view(o2, [PTW]), view(o2 + PTW * 4, [PTW])]
        hi16 = [view(o2, [TB, D], F16), view(o2 + 32 * KB, [TB, D], F16)]
        lo16 = [view(o2 + 4 * KB, [TB, D], F16), view(o + 92 * KB, [TB, D], F16)]
        top8 = view(o2, [T, 8])
        top8_at = view(o2 + KB, [T, 8], mybir.dt.uint32)
        top8_e = view(o2 + 2 * KB, [T, 8])
        xg = view(o2, [4, 2 * D], F16)
        ybuf0 = view(o2, [TOP_E, D])
        xtb = view(o2 + 8 * KB, [2, 2 * KC, BLK], F16)
        bo_sb = view(o2 + 20 * KB, [D])
        o3 = o2 + 24 * KB
        xn = view(o3, [TB, D])
        g_sb = view(o3 + 8 * KB, [KC, B * M])
        stage = [view(o + 80 * KB, [3 * D]), view(o + 86 * KB, [3 * D])]
        stage_r = view(o3, [3 * D])
        xgT = view(o3, [2, 2 * KC, P], F16)
        y_sb = view(o3 + 4 * KB, [2, D])
        r_silu, r_h = view(o3 + 8 * KB, [2, H]), view(o3 + 9 * KB, [2, H])
        r_hb, r_hT = view(o3 + 10 * KB, [2, 2, H], F16), view(o3 + 11 * KB, [2, 2, P], F16)
        ybuf = [ybuf0, view(o3, [TOP_E, D])]
        x1c = view(o3 + 8 * KB, [2, D])
        o4 = o3 + 12 * KB
        small = view(o4, [(R1 + R2 + R3 - o4) // 4])
        at = [0]

        def little(n, dt=F32):
            words = n if dt != F16 else (n + 1) // 2
            v = small[:, at[0]:at[0] + words]
            at[0] += words
            assert at[0] <= (R1 + R2 + R3 - o4) // 4
            return v if dt == F32 else v.bitcast(dt)

        I32 = mybir.dt.int32
        blocks_e = little(BLOCKS + 8, I32)
        chosen_after = little((T + 1) * E, F16)
        chosen = chosen_after[:, E:]
        bias_sb = little(3 * KC)
        bqk = little(B)
        id16 = little(P, F16)
        rt32 = little(KC * E)
        rt_hi, rt_lo = (little(KC * E, F16).rearrange("p (k e) -> p k e", k=KC) for _ in range(2))
        cb_sb = little(E)
        cr_sb = little(R_END)
        tri16, ones16 = little(P, F16), little(P, F16)
        stats = little(TB * 6).rearrange("p (t s) -> p t s", t=TB)
        mv = little(TB * 2).rearrange("p (t s) -> p t s", t=TB)
        var_eps, std, rstd = little(TB), little(TB), little(TB)
        sums = little(2 * NA).rearrange("p (v a) -> p v a", v=2)
        mirrored = little(2 * (NA + 1)).rearrange("p (v a) -> p v a", v=2)
        even_s = little(NA)
        even_w = little(2 * NA)
        mean_sb = little(NA)
        meanT = little(P)
        best = little(16)
        top_e = little(16)
        negmax, total, inv = little(1), little(1), little(1)
        token_id = little(T, I32)
        token_of = little(BLOCKS, I32)
        put_at, row_of = little(NP // P, I32), little(NP // P, I32)
        put_now, row_now = (little(4 * TOP_E, I32).rearrange("p (r i) -> p r i", r=4) for _ in range(2))
        id_now, token_now = little(4, I32), little(8, I32)
        pair_slot, pair_w, pair_blk = little(NP // P), little(NP // P), little(NP // P)
        load_e, nblk, first_a, first_b, last_blk = (little(E) for _ in range(5))

        bank = [ctx.enter_context(nc.psum_tensor(f"bank{i}", [P, 512], F32)) for i in range(8)]
        bank16 = [bk[:, :].bitcast(F16) for bk in bank]

        pt_dram = nc.dram_tensor("pt_dram", [B, P, PTW], F32)
        mean_dram = nc.dram_tensor("mean_dram", [B, L], F32)
        g_dram = nc.dram_tensor("g_dram", [B, M + L], F32)
        xt_dram = nc.dram_tensor("xt_dram", [NB, P, 2 * KC * BLK], F16)
        xr_dram = nc.dram_tensor("xr_dram", [S, 2 * D], F16)
        x1_dram = nc.dram_tensor("x1_dram", [S, D], F32)
        x1s_dram = nc.dram_tensor("x1s_dram", [S, D], F32)
        token_dram = nc.dram_tensor("token_dram", [P * BLOCKS, 1], I32)
        y_dram = nc.dram_tensor("y_dram", [BLOCKS * P, D], F32)
        x_rows = x.rearrange("(q t p) d -> q p t d", t=TB, p=P)
        xr_rows = xr_dram.rearrange("(q t p) d -> q p t d", t=TB, p=P)
        x1_rows = x1_dram.rearrange("(q t p) d -> q p t d", t=TB, p=P)
        x1s_rows = x1s_dram.rearrange("(q t p) d -> q p t d", t=TB, p=P)
        x1s_tiles = x1s_dram.rearrange("(t p) d -> t p d", p=P)
        out_rows = out.rearrange("(q t p) d -> q p t d", t=TB, p=P)
        out_tiles = out.rearrange("(t p) d -> t p d", p=P)
        y_tiles = y_dram.rearrange("(n p) d -> n p d", p=P)

        def only(v, i, *rest):
            v = v[(slice(None), bass.ds(i, 1)) + rest]
            names = "abcd"[:len(v.shape) - 1]
            if len(v.shape) == 3:
                return v.rearrange("p a b -> p (a b)")
            return v.rearrange("p a b c -> p (a b) c")

        def item(d, i):
            d = d[bass.ds(i, 1)]
            if len(d.shape) == 3:
                return d.rearrange("a p n -> (a p) n")
            return d.rearrange("a p t n -> (a p) t n")

        def skewed(b, start, pitch):
            return bass.AP(pt_dram, b * P * PTW + start, [[pitch, P], [1, L]])

        s_const, s_kw, s_qw, s_vw, s_ow = (sem(n) for n in ("const_in", "wk_in", "wq_in", "wv_in", "wo_in"))
        s_x = [sem(f"x_in{q}") for q in range(NB)]
        s_misc = sem("router_in")
        s_mm, s_mm_sb = sem("projection_done"), sem("projection_saved")
        s_var, s_std, s_xn = sem("var_ready"), sem("std_ready"), sem("xn_ready")
        s_tp, s_tp_sb = sem("transposed"), sem("transposes_saved")
        s_pt, s_pt_sb = sem("pt_done"), sem("pt_saved")
        s_ptw = [sem(f"pt_written{b}") for b in range(B)]
        s_sk = [sem(f"skew_in{b}") for b in range(B)]
        s_u, s_u_sb = sem("sums_done"), sem("sums_saved")
        s_ev, s_ev_sb = sem("even_done"), sem("even_saved")
        s_mean, s_mean_sb = sem("mean_done"), sem("mean_saved")
        s_mT, s_mT_sb = sem("mean_turned"), sem("meanT_saved")
        s_mw = [sem(f"mean_written{b}") for b in range(B)]
        s_row = [sem(f"row_in{b}") for b in range(B)]
        s_best, s_exp = sem("best_ready"), sem("exp_done")
        s_g, s_gw = sem("g_ready"), sem("g_written")
        s_xbo = sem("x_plus_bo")
        s_st = [sem("circulant_in0"), sem("circulant_in1")]
        s_at, s_x1, s_bn = sem("attention_done"), sem("x1_ready"), sem("bn_stats_done")
        s_mv, s_rstd = sem("moments_ready"), sem("rstd_ready")
        s_var2, s_std2, s_xn2 = sem("var2_ready"), sem("std2_ready"), sem("xn2_ready")
        s_hi, s_lo = sem("xn2_hi_ready"), sem("xn2_lo_ready")
        s_tp2, s_tp2_sb = sem("xn2_turned"), sem("xn2_turned_saved")
        s_lg = sem("logits_done")
        s_xtw, s_x1w = sem("xt_written"), sem("x1_written")
        s_xrw = [sem("xr_written0"), sem("xr_written1")]
        s_stage = [sem("stage_in0"), sem("stage_in1")]
        s_stage_r = sem("routed_stage_in")
        s_whi, s_wlo = sem("shared_w_hi"), sem("shared_w_lo")
        s_whi_r, s_wlo_r = sem("routed_w_hi"), sem("routed_w_lo")
        s_rt = sem("router_split")
        s_sig, s_chosen, s_rank = sem("scores_ready"), sem("chosen_ready"), sem("ranks_done")
        s_put, s_expert = sem("pair_places_ready"), sem("block_experts_ready")
        s_zero, s_cleared, s_tok = sem("zero_ready"), sem("tokens_cleared"), sem("tokens_in")
        s_scattered = [sem(f"tokens_scattered{r}") for r in range(4)]
        s_put_now, s_token_now, s_row_now = sem("places_copied"), sem("tokens_copied"), sem("rows_copied")
        s_ids = sem("token_ids_ready")
        s_dve = sem("dve_step")
        s_xt, s_x1i = [sem("xt_in0"), sem("xt_in1")], sem("x1_in")
        s_sg, s_su, s_ss, s_sh32 = sem("shared_gate"), sem("shared_up"), sem("shared_silu"), sem("shared_h32")
        s_shh, s_shl, s_sd = sem("shared_h_hi"), sem("shared_h_lo"), sem("shared_down")
        s_x1s, s_x1sw = sem("x1s_ready"), sem("x1s_written")
        s_xg = [sem(f"rows_gathered{r}") for r in range(4)]
        s_tx, s_txe = sem("rows_turned"), sem("rows_turned_saved")
        s_rg, s_rs, s_rh = sem("routed_gate_up"), sem("routed_silu"), sem("routed_h32")
        s_rhh, s_rhl = sem("routed_h_hi"), sem("routed_h_lo")
        s_ht, s_hte, s_rd = sem("routed_h_turned"), sem("routed_h_turned_saved"), sem("routed_down")
        s_ye = sem("y_saved")
        s_yw = [sem("y_written0"), sem("y_written1")]
        s_yg = [sem("y_gathered0"), sem("y_gathered1")]
        s_x1c = [sem("x1s_in0"), sem("x1s_in1")]
        s_cmb = sem("result_added")
        s_out = [sem("out_written0"), sem("out_written1")]
        s_out_blk = sem("out_block_written")

        block = ctx.enter_context(nc.Block())
        PARTS = ((0, 0), (0, 1), (1, 0))

        def settled(engine):
            engine.wait_ge(s_const, 16)

        @block.sync
        def _(sp):
            sp.dma_start(c_sb, const).then_inc(s_const, 16)
            sp.dma_start(ctx_sb, ctxT).then_inc(s_kw, 16)
            sp.dma_start(bias_sb, biases).then_inc(s_kw, 16)
            sp.dma_start(wk_sb, wk).then_inc(s_kw, 16)
            for q in range(NB):
                sp.dma_start(x_sb[:, TB * q:TB * q + TB, :], x_rows[q]).then_inc(s_x[q], 16)
                if q == 0:
                    sp.dma_start(wq_sb, wqT).then_inc(s_qw, 16)
                if q == 1:
                    sp.dma_start(bo_sb, bo).then_inc(s_misc, 16)
                    sp.dma_start(rt32, routerT).then_inc(s_misc, 16)
                    sp.dma_start(cb_sb, cb).then_inc(s_misc, 16)
                    sp.dma_start(cr_sb, const_r).then_inc(s_misc, 16)
            sp.dma_start(wv_sb, wv).then_inc(s_vw, 16)
            sp.dma_start(wo_sb, wo).then_inc(s_ow, 16)
            for b in range(B):
                sp.wait_ge(s_pt_sb, 4 * (b + 1))
                sp.dma_start(pt_dram[b], pt[b]).then_inc(s_ptw[b], 16)
                sp.wait_ge(s_ptw[b], 16)
                if b:
                    sp.wait_ge(s_u, b)
                sp.dma_start(skew_c, skewed(b, 2 * M - 1, PTW - 1)).then_inc(s_sk[b], 16)
                sp.dma_start(skew_d, skewed(b, 1, PTW + 1)).then_inc(s_sk[b], 16)

            def means(b):
                sp.wait_ge(s_mT_sb, b + 1)
                sp.dma_start(mean_dram[b].rearrange("(a p) -> a p", p=P), meanT[0:NA, :]).then_inc(s_mw[b], 16)
                sp.wait_ge(s_mw[b], 16)
                if b:
                    sp.wait_ge(s_gw, 32 * b)
                sp.dma_start(row[0:1, :], mean_dram[b:b + 1, :]).then_inc(s_row[b], 16)

            def delays(b):
                sp.wait_ge(s_g, b + 1)
                sp.dma_start(g_dram[b:b + 1, M:M + L], row[0:1, :]).then_inc(s_gw, 16)
                sp.dma_start(g_dram[b:b + 1, 0:M], row[0:1, L - M:L]).then_inc(s_gw, 16)

            def circulant(k, j):
                sp.dma_start(st[j], bass.AP(g_dram, (k // (NB // B)) * (M + L) + k % (NB // B) * BLK + 1, [[1, P], [1, BLK]])
                             ).then_inc(s_st[j], 16)

            def shared_weights(n, j, fresh):
                if not fresh:
                    sp.wait_ge(s_wlo, n - 1)
                sp.dma_start(stage[j][:, 0:2 * D], item3(gu_w, n)).then_inc(s_stage[j], 16)
                sp.dma_start(stage[j][:, 2 * D:3 * D], item3(dn_w, n)).then_inc(s_stage[j], 16)

            def item3(d, i):
                return d[bass.ds(i, 1)].rearrange("a p n -> (a p) n")

            def second_norm_out(k, j, more):
                if more:
                    sp.wait_ge(s_at, TB * (k + 1))
                    circulant(k + 2, j)
                sp.wait_ge(s_x1, TB * (k + 1))
                sp.dma_start(item(x1_rows, k), x_sb[:, bass.ds(k * TB, TB), :]).then_inc(s_x1w, 16)
                sp.wait_ge(s_hi, k + 1)
                sp.dma_start(item(xr_rows, k)[:, :, 0:D], hi16[j]).then_inc(s_xrw[j], 16)
                sp.wait_ge(s_lo, k + 1)
                sp.dma_start(item(xr_rows, k)[:, :, D:2 * D], lo16[j]).then_inc(s_xrw[j], 16)
                if more:
                    shared_weights(k + 2, j, False)
                settled(sp)
                sp.wait_ge(s_tp2_sb, TB * (k + 1))
                if not isinstance(k, int) or k:
                    sp.wait_ge(s_xtw, 16 * k)
                sp.dma_start(item(xt_dram, k), xtb[:, j, :, :].rearrange("p n q -> p (n q)")).then_inc(s_xtw, 16)

            means(0)
            sp.wait_ge(s_u, B)
            sp.wait_ge(s_mm_sb, 15)
            for k in range(2):
                shared_weights(k, k, True)
            delays(0)
            sp.wait_ge(s_gw, 32)
            for k in range(2):
                circulant(k, k)
            means(1)
            second_norm_out(0, 0, True)
            delays(1)
            sp.wait_ge(s_gw, 64)
            second_norm_out(1, 1, True)
            with sp.Fori(1, NB // 2 - 1) as i:
                for j in range(2):
                    second_norm_out(2 * i + j, j, True)
            for j in range(2):
                second_norm_out(NB - 2 + j, j, False)

            sp.wait_ge(s_xtw, 16 * NB)
            sp.wait_ge(s_x1w, 16 * NB)
            sp.wait_ge(s_lg, NB)
            for k in range(2):
                sp.dma_start(xtb[:, k, :, :].rearrange("p n q -> p (n q)"), xt_dram[k]).then_inc(s_xt[k], 16)
            sp.dma_start(x1b, x1_rows[0]).then_inc(s_x1i, 16)

            def routed_weights(n):
                sp.wait_ge(s_wlo_r, n)
                sp.dma_start(stage_r[:, 0:2 * D], item3(gu_w, SH + n)).then_inc(s_stage_r, 16)
                sp.dma_start(stage_r[:, 2 * D:3 * D], item3(dn_w, SH + n)).then_inc(s_stage_r, 16)

            def shared_io(k, j, more_x, more_xt):
                sp.wait_ge(s_x1s, TB * (k + 1))
                sp.dma_start(item(x1s_rows, k), x1b).then_inc(s_x1sw, 16)
                if more_xt:
                    sp.dma_start(xtb[:, j, :, :].rearrange("p n q -> p (n q)"), item(xt_dram, k + 2)).then_inc(s_xt[j], 16)
                if more_x:
                    sp.wait_ge(s_x1sw, 16 * (k + 1))
                    sp.dma_start(x1b, item(x1_rows, k + 1)).then_inc(s_x1i, 16)

            with sp.Fori(0, FIRST // 2) as i:
                for j in range(2):
                    for e in range(E // FIRST):
                        routed_weights((2 * i + j) * (E // FIRST) + e)
                    shared_io(2 * i + j, j, True, True)
            with sp.Fori(0, BLOCKS // 2) as i:
                for j in range(2):
                    sp.wait_ge(s_ye, 2 * i + j + 1)
                    sp.dma_start(item(y_tiles, 2 * i + j), y_sb[:, j, :]).then_inc(s_yw[j], 16)
            def take(o, j):
                if not isinstance(o, int) or o >= 2:
                    sp.wait_ge(s_out[j], 16 * (o >> 1))
                sp.dma_start(x1c[:, j, :], item(x1s_tiles, o)).then_inc(s_x1c[j], 16)

            def results_out(k, last):
                for p in range(OLD):
                    o = (k - FIRST) * OLD + p
                    sp.wait_ge(s_cmb, TOP_E * ((k - FIRST) * TURNS + p + 1))
                    sp.dma_start(item(out_tiles, o), x1c[:, p % 2, :]).then_inc(s_out[p % 2], 16)
                    if not last or p < OLD - 2:
                        take(o + 2, p % 2)
                sp.wait_ge(s_x1s, TB * (k + 1))
                sp.dma_start(item(out_rows, k), x1b).then_inc(s_out_blk, 16)

            sp.wait_ge(s_rd, BLOCKS)
            for j in range(2):
                sp.wait_ge(s_yw[j], 16 * BLOCKS // 2)
            sp.wait_ge(s_x1sw, 16 * FIRST)
            for o in range(2):
                take(o, o)
            for k in range(FIRST, NB):
                results_out(k, k == NB - 1)
                if k + 2 < NB:
                    sp.dma_start(xtb[:, k % 2, :, :].rearrange("p n q -> p (n q)"), xt_dram[k + 2]).then_inc(s_xt[k % 2], 16)
                sp.wait_ge(s_out_blk, 16 * (k - FIRST + 1))
                if k + 1 < NB:
                    sp.dma_start(x1b, x1_rows[k + 1]).then_inc(s_x1i, 16)
            for j in range(2):
                sp.wait_ge(s_out[j], 16 * FIRST * TB // 2)

        @block.tensor
        def _(pe):
            mm, turn = nc.tensor.matmul, nc.tensor.transpose

            def project(dst, lhs, rhs):
                for k in range(KC):
                    last = mm(dst, lhs(k), rhs(k), start=(k == 0), stop=(k == KC - 1))
                last.then_inc(s_mm, 1)

            pe.wait_ge(s_const, 16)
            pe.wait_ge(s_kw, 48)
            for c in range(KC):
                project(bank[c][:, 0:B * M], lambda k: wk_sb[:, k, c * P:c * P + P], lambda k: ctx_sb[:, k, :])
            pe.wait_ge(s_qw, 16)
            pe.wait_ge(s_mm_sb, 4)
            for c in range(KC):
                project(bank[4 + c][:, 0:B * M], lambda k: wq_sb[:, k, c * P:c * P + P], lambda k: kT[:, k, :])
            for b in range(B):
                for k in range(KC):
                    last = mm(bank[0][:, b:b + 1], kT[:, k, b * M:b * M + M], bias_sb[:, k:k + 1],
                              start=(k == 0), stop=(k == KC - 1))
            last.then_inc(s_mm, 1)
            pe.wait_ge(s_mm_sb, 9)

            def skewed_sums(b):
                pe.wait_ge(s_sk[b], 32)
                if b:
                    pe.wait_ge(s_mT_sb, b)
                for a in range(NA):
                    mm(bank[6][:, 2 * a:2 * a + 2], skew_c[:, a * P:a * P + P], c_sb[:, C_ONES:C_ONES + 2],
                       start=True, stop=False)
                    last = mm(bank[6][:, 2 * a:2 * a + 2], skew_d[:, a * P:a * P + P],
                              c_sb[:, C_ONES + 2:C_ONES + 4], start=False, stop=True)
                last.then_inc(s_u, 1)

            def mean_correlation(b):
                pe.wait_ge(s_u_sb, 3 * (b + 1))
                e = bank[7][:, 0:2 * NA].rearrange("p (v a) -> p v a", v=2)
                mm(e, c_sb[:, C_ID:C_ID + P], sums, start=True, stop=False)
                mm(e, c_sb[:, C_J0:C_J0 + P], mirrored[:, :, 0:NA], start=False, stop=False)
                mm(e, c_sb[:, C_J1:C_J1 + P], mirrored[:, :, 1:NA + 1], start=False, stop=True).then_inc(s_ev, 1)
                pe.wait_ge(s_ev_sb, 3 * (b + 1))
                m = bank[7][:, 64:64 + NA]
                mm(m, c_sb[:, C_IS:C_IS + P], even_s, start=True, stop=False)
                for a in range(NA):
                    last = mm(m, c_sb[:, C_T + a * P:C_T + a * P + P], even_w[:, NA - a:2 * NA - a],
                              start=False, stop=(a == NA - 1))
                last.then_inc(s_mean, 1)
                pe.wait_ge(s_mean_sb, b + 1)
                turn(bank[6][0:NA, 64:64 + P], mean_sb, c_sb[:, C_ID:C_ID + P]).then_inc(s_mT, 1)

            for q in range(NB):
                for t in range(TB):
                    pe.wait_ge(s_xn, q * TB + t + 1)
                    if q:
                        pe.wait_ge(s_tp_sb, (q - 1) * TB + t + 1)
                    for k in range(KC):
                        last = turn(bank[t][:, k * P:k * P + P], xn[:, t, k * P:k * P + P], c_sb[:, C_ID:C_ID + P])
                    last.then_inc(s_tp, 1)
                pe.wait_ge(s_tp_sb, q * TB + TB)
                if q >= 2:
                    pe.wait_ge(s_pt_sb, q - 1)
                b = q // 4
                for k in range(KC):
                    last = mm(bank[4 + q % 2][:, :], g_sb[:, k, b * M:b * M + M], xnT[q % 2][:, k, :],
                              start=(k == 0), stop=(k == KC - 1))
                last.then_inc(s_pt, 1)
                if q == NB - 2:
                    skewed_sums(0)
            mean_correlation(0)
            pe.wait_ge(s_vw, 16)
            for c in range(KC):
                project(bank[c][:, 0:B * M], lambda k: wv_sb[:, k, c * P:c * P + P], lambda k: ctx_sb[:, k, :])
            pe.wait_ge(s_ow, 16)
            pe.wait_ge(s_mm_sb, 13)
            pe.wait_ge(s_pt_sb, NB)
            for b in range(B):
                project(bank[4 + b][:, :], lambda k: vT[:, k, b * M:b * M + M], lambda k: wo_sb[:, k, :])
            skewed_sums(1)
            mean_correlation(1)

            pe.wait_ge(s_rt, 3)
            pe.wait_ge(s_mm_sb, 15)

            def attention(k, j):
                pe.wait_ge(s_st[j], 16 * ((k >> 1) + 1))
                for t in range(TB):
                    if not isinstance(k, int) or k * TB + t >= 2:
                        pe.wait_ge(s_x1, k * TB + t - 1)
                    mm(bank[t % 2][:, :], st[j][:, t * P:t * P + P], only(vo, k // (NB // B)), start=True, stop=True
                       ).then_inc(s_at, 1)

            def turn_and_route(k, j):
                pe.wait_ge(s_hi, k + 1)
                pe.wait_ge(s_lo, k + 1)
                for t in range(TB):
                    if not isinstance(k, int) or k * TB + t >= 2:
                        pe.wait_ge(s_tp2_sb, k * TB + t - 1)
                    for n in range(2 * KC):
                        src = (hi16, lo16)[n // KC][j]
                        last = turn(bank16[2 + t % 2][:, n * P:n * P + P], src[:, t, n % KC * P:n % KC * P + P], id16)
                    last.then_inc(s_tp2, 1)
                for t in range(TB):
                    pe.wait_ge(s_tp2_sb, k * TB + t + 1)
                    lg = bank[4][:, bass.ds((k * TB + t) * E, E)]
                    n = 0
                    for xv, wp in PARTS:
                        for c in range(KC):
                            last = mm(lg, xtb[:, j, xv * KC + c, t * P:t * P + P], (rt_hi, rt_lo)[wp][:, c, :],
                                      start=(n == 0), stop=(n == 3 * KC - 1))
                            n += 1
                last.then_inc(s_lg, 1)

            attention(0, 0)
            turn_and_route(0, 0)
            attention(1, 1)
            with pe.Fori(0, NB // 2 - 1) as i:
                for j in range(2):
                    attention(2 * i + 2 + j, j)
                    turn_and_route(2 * i + 1 + j, 1 - j)
            turn_and_route(NB - 1, 1)

            pe.wait_ge(s_chosen, 1)
            mm(bank[5][:, :], tri16, chosen, start=True, stop=False)
            for t in range(T - 1, 1, -1):
                mm(bank[5][:, t * E:T * E], ones16, chosen[:, 0:(T - t) * E], start=False, stop=False, skip_group_check=True)
            mm(bank[5][:, :], ones16, chosen_after[:, 0:T * E], start=False, stop=True)
            for t in range(T):
                last = mm(bank[6][:, 0:E], ones16, chosen[:, t * E:t * E + E], start=(t == 0), stop=(t == T - 1))
            last.then_inc(s_rank, 1)

            pe.wait_ge(s_whi, SH)
            pe.wait_ge(s_wlo, SH)

            def shared_gate_up(k, j, c, first):
                for g, s_done, s_read in ((0, s_sg, s_ss), (1, s_su, s_sh32)):
                    if not first:
                        pe.wait_ge(s_read, k * SH + c)
                    n = 0
                    for xv, wp in PARTS:
                        for kc in range(KC):
                            w = only((gu_hi_s, gu_lo_s)[wp], c, slice(kc * 2 * H + g * H, kc * 2 * H + g * H + H))
                            last = mm(bank[g][:, :], w, xtb[:, j, xv * KC + kc, :],
                                      start=(n == 0), stop=(n == 3 * KC - 1))
                            n += 1
                    last.then_inc(s_done, 1)

            def shared_down(k, c, half, first, final):
                pe.wait_ge(s_shl, k * SH + c + 1)
                for t in range(TB):
                    for n, (hv, wp) in enumerate(PARTS):
                        last = mm(bank[2 + t][:, :], s_hb[:, half, hv, t * P:t * P + P], only((dn_hi_s, dn_lo_s)[wp], c),
                                  start=(first and n == 0), stop=(final and n == 2))
                last.then_inc(s_sd, 1)

            def shared(k, j, again):
                pe.wait_ge(s_xt[j], 16 * ((k >> 1) + 1))
                if again:
                    pe.wait_ge(s_sh32, k * SH)
                shared_gate_up(k, j, 0, True)
                shared_gate_up(k, j, 1, False)
                if again:
                    pe.wait_ge(s_x1s, k * TB)
                shared_down(k, 0, 0, True, False)
                with pe.Fori(0, SH // 2 - 1) as i:
                    for h in range(2):
                        shared_gate_up(k, j, 2 * i + 2 + h, False)
                        shared_down(k, 2 * i + 1 + h, 1 - h, False, False)
                shared_down(k, SH - 1, 1, False, True)

            pe.wait_ge(s_put, 1)
            with pe.Fori(0, FIRST // 2) as i:
                for j in range(2):
                    shared(2 * i + j, j, True)

            pe.wait_ge(s_sh32, FIRST * SH)
            pe.wait_ge(s_x1s, FIRST * TB)
            pe.wait_ge(s_whi_r, E)
            pe.wait_ge(s_wlo_r, E)
            pe.wait_ge(s_expert, 1)

            def experts(at):
                return nc.values_load_multi_w_load_instructions(
                    blocks_e[0:1, bass.ds(at, 8)], engines=[mybir.EngineType.PE], min_val=0, max_val=E - 1,
                    skip_runtime_bounds_check_because="VectorE counts at most E - 1 experts before a block")[1]

            def turn_rows(s, r, j, fresh):
                pe.wait_ge(s_xg[r], 16 * ((s >> 2) + 1))
                if not fresh:
                    pe.wait_ge(s_txe, s - 1)
                for n in range(2 * KC):
                    last = turn(bank16[j][:, n * P:n * P + P], xg[:, r, n * P:n * P + P], id16)
                last.then_inc(s_tx, 1)

            def gate_up(s, j, e, fresh):
                pe.wait_ge(s_txe, s + 1)
                if not fresh:
                    pe.wait_ge(s_rh, s - 1)
                n = 0
                for xv, wp in PARTS:
                    for kc in range(KC):
                        last = mm(bank[2 + j][:, 0:2 * H], xgT[:, j, xv * KC + kc, :],
                                  only((gu_hi_r, gu_lo_r)[wp], e, slice(kc * 2 * H, (kc + 1) * 2 * H)),
                                  start=(n == 0), stop=(n == 3 * KC - 1))
                        n += 1
                last.then_inc(s_rg, 1)

            def turn_h(s, j, fresh):
                pe.wait_ge(s_rhl, s + 1)
                if not fresh:
                    pe.wait_ge(s_hte, s - 1)
                for v in range(2):
                    last = turn(bank16[4 + j][:, v * P:v * P + P], r_hb[:, j, v, :], id16)
                last.then_inc(s_ht, 1)

            def down(s, j, e, fresh):
                pe.wait_ge(s_hte, s + 1)
                if not fresh:
                    pe.wait_ge(s_ye, s - 1)
                for n, (hv, wp) in enumerate(PARTS):
                    last = mm(bank[6 + j][:, :], r_hT[:, j, hv, :], only((dn_hi_r, dn_lo_r)[wp], e),
                              start=(n == 0), stop=(n == 2))
                last.then_inc(s_rd, 1)

            e = experts(0)
            turn_rows(0, 0, 0, True)
            turn_rows(1, 1, 1, True)
            gate_up(0, 0, e[0], True)
            turn_rows(2, 2, 0, False)
            gate_up(1, 1, e[1], True)
            turn_h(0, 0, True)
            def four(i, first):
                e = experts(4 * i)
                for n in range(4):
                    s = 4 * i + 1 + n
                    turn_rows(s + 2, (3 + n) % 4, (1 + n) % 2, False)
                    gate_up(s + 1, n % 2, e[n + 2], False)
                    turn_h(s, (1 + n) % 2, first and n == 0)
                    down(s - 1, n % 2, e[n], first and n < 2)

            four(0, True)
            with pe.Fori(1, BLOCKS // 4 - 1) as i:
                four(i, False)
            e = experts(BLOCKS - 4)
            turn_rows(BLOCKS - 1, 3, 1, False)
            gate_up(BLOCKS - 2, 0, e[2], False)
            turn_h(BLOCKS - 3, 1, False)
            down(BLOCKS - 4, 0, e[0], False)
            gate_up(BLOCKS - 1, 1, e[3], False)
            turn_h(BLOCKS - 2, 0, False)
            down(BLOCKS - 3, 1, e[1], False)
            turn_h(BLOCKS - 1, 1, False)
            down(BLOCKS - 2, 0, e[2], False)
            down(BLOCKS - 1, 1, e[3], False)

            pe.wait_ge(s_ye, BLOCKS)
            with pe.Fori(FIRST // 2, NB // 2) as i:
                for j in range(2):
                    shared(2 * i + j, j, True)

        @block.scalar
        def _(act):
            A = nc.scalar.activation

            for c in range(KC):
                act.wait_ge(s_mm, c + 1)
                A(kT[:, c, :], bank[c][:, 0:B * M], ACT.Identity, bias=bias_sb[:, KC + c:KC + c + 1]).then_inc(s_mm_sb, 1)
            act.wait_ge(s_var, 1)
            A(std, var_eps, ACT.Sqrt).then_inc(s_std, 1)
            for c in range(KC):
                act.wait_ge(s_mm, 4 + c + 1)
                A(g_sb[:, c, :], bank[4 + c][:, 0:B * M], ACT.Copy).then_inc(s_mm_sb, 1)
            act.wait_ge(s_mm, 9)
            A(bqk, bank[0][:, 0:B], ACT.Copy).then_inc(s_mm_sb, 1)
            act.wait_ge(s_mm_sb, 9)

            def save_pt(q):
                b, n = q // 4, q % 4
                act.wait_ge(s_pt, q + 1)
                src, bias = bank[4 + q % 2], bqk[:, b:b + 1]
                if n == 0:
                    A(pt[b][:, M + L:PTW], src[:, 0:M], ACT.Identity, bias=bias)
                if n == 3:
                    A(pt[b][:, 0:M], src[:, BLK - M:BLK], ACT.Identity, bias=bias)
                A(pt[b][:, M + n * BLK:M + (n + 1) * BLK], src[:, :], ACT.Identity, bias=bias).then_inc(s_pt_sb, 1)

            for q in range(NB):
                if q:
                    act.wait_ge(s_var, q + 1)
                    A(std, var_eps, ACT.Sqrt).then_inc(s_std, 1)
                    save_pt(q - 1)
                for t in range(TB):
                    act.wait_ge(s_tp, q * TB + t + 1)
                    A(xnT[q % 2][:, :, t * P:t * P + P], bank[t][:, :].rearrange("p (k n) -> p k n", k=KC), ACT.Copy
                      ).then_inc(s_tp_sb, 1)
            save_pt(NB - 1)
            for c in range(KC):
                act.wait_ge(s_mm, 9 + c + 1)
                A(vT[:, c, :], bank[c][:, 0:B * M], ACT.Identity, bias=bias_sb[:, 2 * KC + c:2 * KC + c + 1]
                  ).then_inc(s_mm_sb, 1)
            for b in range(B):
                act.wait_ge(s_mm, 13 + b + 1)
                A(vo[:, b, :], bank[4 + b][:, :], ACT.Copy).then_inc(s_mm_sb, 1)
            def softmax(b):
                nc.scalar.wait_ge(s_best, b + 1)
                nc.scalar.activation(top_e[0:1, :], best[0:1, :], ACT.Exp, bias=negmax[0:1, :],
                                     accum_out=total[0:1, :]).then_inc(s_exp, 1)
                nc.scalar.activation(row[0:1, :], row[0:1, :], ACT.Exp, bias=negmax[0:1, :]).then_inc(s_exp, 1)

            softmax(0)

            def second_std(k):
                act.wait_ge(s_var2, k + 1)
                A(std, var_eps, ACT.Sqrt).then_inc(s_std2, 1)

            def second_norm(k, j, more):
                act.wait_ge(s_xn2, TB * (k + 1))
                if not isinstance(k, int) or k >= 2:
                    act.wait_ge(s_tp2, TB * (k - 1))
                    act.wait_ge(s_xrw[j], 32 * (k >> 1))
                A(hi16[j], xn, ACT.Copy).then_inc(s_hi, 1)
                act.wait_ge(s_stage[j], 32 * ((k >> 1) + 1))
                A(only(gu_hi_s, k), stage[j][:, 0:2 * D], ACT.Copy, scale=WS)
                A(only(dn_hi_s, k), stage[j][:, 2 * D:3 * D], ACT.Copy, scale=WS).then_inc(s_whi, 1)
                if more:
                    second_std(k + 1)
                if not isinstance(k, int) or k >= 2:
                    act.wait_ge(s_xtw, 16 * (k - 1))
                    act.wait_ge(s_lg, k - 1)
                for t in range(TB):
                    act.wait_ge(s_tp2, k * TB + t + 1)
                    A(xtb[:, j, :, t * P:t * P + P], bank16[2 + t % 2].rearrange("p (n q) -> p n q", n=2 * KC), ACT.Copy
                      ).then_inc(s_tp2_sb, 1)

            second_std(0)
            second_norm(0, 0, False)
            softmax(1)
            second_std(1)
            second_norm(1, 1, True)
            with act.Fori(1, NB // 2 - 1) as i:
                for j in range(2):
                    second_norm(2 * i + j, j, True)
            for j in range(2):
                second_norm(NB - 2 + j, j, j == 0)
            act.wait_ge(s_lg, NB)
            A(scores, bank[4][:, :], ACT.Sigmoid, scale=1.0 / WS).then_inc(s_sig, 1)

            def shared_chunk(k, c, h):
                n = k * SH + c
                act.wait_ge(s_sg, n + 1)
                act.wait_ge(s_sh32, n)
                A(s_silu, bank[0][:, :], ACT.Silu, scale=1.0 / WS).then_inc(s_ss, 1)
                act.wait_ge(s_sh32, n + 1)
                if not isinstance(n, int) or n >= 2:
                    act.wait_ge(s_sd, n - 1)
                A(s_hb[:, h, 0, :], s_h, ACT.Copy).then_inc(s_shh, 1)

            def routed_weights_hi(n):
                act.wait_ge(s_stage_r, 32 * (n + 1))
                A(only(gu_hi_r, n), stage_r[:, 0:2 * D], ACT.Copy, scale=WS)
                A(only(dn_hi_r, n), stage_r[:, 2 * D:3 * D], ACT.Copy, scale=WS).then_inc(s_whi_r, 1)

            act.wait_ge(s_x1w, 16 * NB)
            act.wait_ge(s_xn2, TB * NB)
            for h in range(2):
                shared_chunk(0, h, h)
            routed_weights_hi(0)
            with act.Fori(1, FIRST * SH // 2) as i:
                for h in range(2):
                    shared_chunk(0, 2 * i + h, h)
                routed_weights_hi(i)

            def silu_hi(s, j, fresh):
                act.wait_ge(s_rg, s + 1)
                if not fresh:
                    act.wait_ge(s_rh, s - 1)
                A(r_silu[:, j, :], bank[2 + j][:, 0:H], ACT.Silu, scale=1.0 / WS).then_inc(s_rs, 1)
                act.wait_ge(s_rh, s + 1)
                if not fresh:
                    act.wait_ge(s_ht, s - 1)
                A(r_hb[:, j, 0, :], r_h[:, j, :], ACT.Copy).then_inc(s_rhh, 1)

            def save_y(s, j, half):
                act.wait_ge(s_rd, s + 1)
                if not isinstance(half, int) or half:
                    act.wait_ge(s_yw[j], 16 * half)
                A(y_sb[:, j, :], bank[6 + j][:, :], ACT.Copy, scale=1.0 / WS).then_inc(s_ye, 1)

            silu_hi(0, 0, True)
            silu_hi(1, 1, True)
            with act.Fori(0, BLOCKS // 4 - 1) as i:
                for n in range(4):
                    silu_hi(4 * i + 2 + n, n % 2, False)
                    save_y(4 * i + n, n % 2, 2 * i + n // 2)
            for n in range(2):
                silu_hi(BLOCKS - 2 + n, n, False)
                save_y(BLOCKS - 4 + n, n, BLOCKS // 2 - 2)
            for n in range(2):
                save_y(BLOCKS - 2 + n, n, BLOCKS // 2 - 1)

            with act.Fori(FIRST, NB) as k:
                for c in range(SH):
                    shared_chunk(k, c, c % 2)

        @block.vector
        def _(dve):
            link = Links(dve, s_dve)
            V = nc.vector

            for q in range(NB):
                dve.wait_ge(s_x[q], 16)
                for t in range(TB):
                    link.start(V.bn_stats(stats[:, t, :], x_sb[:, q * TB + t, :]))
                link.wait()
                if q:
                    dve.wait_ge(s_xn, q * TB)
                for t in range(TB):
                    link.start(V.bn_aggr(mv[:, t, :], stats[:, t, :]))
                link.wait()
                V.tensor_scalar(var_eps, mv[:, :, 1], EPS, None, ALU.add).then_inc(s_var, 1)
                dve.wait_ge(s_std, q + 1)
                link.done(V.reciprocal(rstd, std))
                for t in range(TB):
                    if q:
                        dve.wait_ge(s_tp, (q - 1) * TB + t + 1)
                    V.tensor_scalar(xn[:, t, :], x_sb[:, q * TB + t, :], mv[:, t, 0:1], rstd[:, t:t + 1],
                                    ALU.subtract, ALU.mult).then_inc(s_xn, 1)
                if q == 2:
                    dve.wait_ge(s_misc, 64)
                    dve.wait_ge(s_const, 16)
                    r3 = rt32.rearrange("p (k e) -> p k e", k=KC)
                    link.done(V.tensor_scalar(rt_hi, r3, WS, None, ALU.mult))
                    V.scalar_tensor_tensor(rt_lo, r3, WS, rt_hi, ALU.mult, ALU.subtract).then_inc(s_rt, 1)
                    V.tensor_copy(id16, c_sb[:, C_ID:C_ID + P]).then_inc(s_rt, 1)
                    V.tensor_copy(tri16, cr_sb[:, R_TRI:R_TRI + P])
                    V.memset(chosen_after[:, 0:E], 0.0)
                    V.memset(ones16, 1.0).then_inc(s_rt, 1)

            def mean_correlation(b):
                dve.wait_ge(s_u, b + 1)
                u = bank[6][:, 0:2 * NA].rearrange("p (a v) -> p v a", v=2)
                V.tensor_copy(sums, u).then_inc(s_u_sb, 1)
                V.tensor_copy(mirrored[:, :, 0:1], u[:, :, 0:1]).then_inc(s_u_sb, 1)
                V.tensor_copy(mirrored[:, :, 1:NA + 1], u[:, :, ::-1]).then_inc(s_u_sb, 1)
                dve.wait_ge(s_ev, b + 1)
                V.tensor_copy(even_s, bank[7][:, 0:NA]).then_inc(s_ev_sb, 1)
                V.tensor_copy(even_w[:, 0:NA], bank[7][:, NA:2 * NA]).then_inc(s_ev_sb, 1)
                V.tensor_copy(even_w[:, NA:2 * NA], bank[7][:, NA:2 * NA]).then_inc(s_ev_sb, 1)
                dve.wait_ge(s_mean, b + 1)
                V.tensor_copy(mean_sb, bank[7][:, 64:64 + NA]).then_inc(s_mean_sb, 1)
                dve.wait_ge(s_mT, b + 1)
                if b:
                    dve.wait_ge(s_mw[0], 16)
                V.tensor_copy(meanT[0:NA, :], bank[6][0:NA, 64:64 + P]).then_inc(s_mT_sb, 1)

            def delays(b):
                r, k = row[0:1, :], taken[0:1, :]
                dve.wait_ge(s_row[b], 16)
                link.done(V.max(best[0:1, 0:8], r))
                link.done(V.match_replace(k, best[0:1, 0:8], r, GONE))
                link.done(V.max(best[0:1, 8:16], k))
                link.start(V.memset(best[0:1, TOP_K:16], GONE))
                link.start(V.tensor_scalar(negmax[0:1, :], best[0:1, 0:1], -1.0, None, ALU.mult))
                link.wait()
                V.match_replace(k, best[0:1, 8:16], k, GONE).then_inc(s_best, 1)
                dve.wait_ge(s_best, b + 1)
                dve.wait_ge(s_exp, 2 * b + 2)
                link.done(V.reciprocal(inv[0:1, :], total[0:1, :]))
                link.done(V.tensor_scalar(k, k, GONE, inv[0:1, :], ALU.is_le, ALU.mult))
                V.tensor_tensor(r, r, k, ALU.mult).then_inc(s_g, 1)

            def second_norm(k, j):
                for t in range(TB):
                    n = k * TB + t
                    xr = only(x_sb, n)
                    dve.wait_ge(s_at, n + 1)
                    V.tensor_tensor(xr, bank[t % 2][:, :], xr, ALU.add).then_inc(s_x1, 1)
                    settled(dve)
                    dve.wait_ge(s_x1, n + 1)
                    V.bn_stats(stats[:, t, :], xr).then_inc(s_bn, 1)
                settled(dve)
                dve.wait_ge(s_bn, k * TB + TB)
                for t in range(TB):
                    V.bn_aggr(mv[:, t, :], stats[:, t, :]).then_inc(s_mv, 1)
                dve.wait_ge(s_mv, k * TB + TB)
                V.tensor_scalar(var_eps, mv[:, :, 1], EPS, None, ALU.add).then_inc(s_var2, 1)
                dve.wait_ge(s_std2, k + 1)
                V.reciprocal(rstd, std).then_inc(s_rstd, 1)
                dve.wait_ge(s_rstd, k + 1)
                dve.wait_ge(s_hi, k)
                dve.wait_ge(s_lo, k)
                for t in range(TB):
                    V.tensor_scalar(xn[:, t, :], only(x_sb, k * TB + t), mv[:, t, 0:1], rstd[:, t:t + 1],
                                    ALU.subtract, ALU.mult).then_inc(s_xn2, 1)
                dve.wait_ge(s_whi, k + 1)
                V.scalar_tensor_tensor(only(gu_lo_s, k), stage[j][:, 0:2 * D], WS, only(gu_hi_s, k), ALU.mult, ALU.subtract)
                V.scalar_tensor_tensor(only(dn_lo_s, k), stage[j][:, 2 * D:3 * D], WS, only(dn_hi_s, k),
                                       ALU.mult, ALU.subtract).then_inc(s_wlo, 1)

            mean_correlation(0)
            delays(0)
            mean_correlation(1)
            dve.wait_ge(s_xbo, NB)
            second_norm(0, 0)
            delays(1)
            second_norm(1, 1)
            with dve.Fori(1, NB // 2) as i:
                for j in range(2):
                    second_norm(2 * i + j, j)

            def tiles(v, n=E):
                return v.rearrange("p (t e) -> p t e", e=n)

            dve.wait_ge(s_sig, 1)
            dve.wait_ge(s_lo, NB)
            for j in range(2):
                dve.wait_ge(s_xrw[j], 16 * NB)
            link.done(V.tensor_tensor(tiles(biased), tiles(scores), cb_sb.unsqueeze(1).broadcast_to([P, T, E]), ALU.add))
            G4 = T * GROUPS
            pairs = biased.rearrange("p (g a) -> p g a", a=2)
            hi2, lo2 = tmp[:, 0:2 * G4], tmp[:, 2 * G4:4 * G4]
            one = lambda v: v.unsqueeze(2)
            link.start(V.tensor_tensor(one(hi2), pairs[:, :, 0:1], pairs[:, :, 1:2], ALU.max))
            link.done(V.tensor_tensor(one(lo2), pairs[:, :, 0:1], pairs[:, :, 1:2], ALU.min))
            hv, lv = (v.rearrange("p (g a) -> p g a", a=2) for v in (hi2, lo2))
            m1, m2, m3 = (cnt[:, i * G4:(i + 1) * G4] for i in range(3))
            link.start(V.tensor_tensor(one(m1), hv[:, :, 0:1], hv[:, :, 1:2], ALU.max))
            link.start(V.tensor_tensor(one(m2), hv[:, :, 0:1], hv[:, :, 1:2], ALU.min))
            link.done(V.tensor_tensor(one(m3), lv[:, :, 0:1], lv[:, :, 1:2], ALU.max))
            link.done(V.tensor_tensor(m2, m2, m3, ALU.max))
            link.done(V.tensor_tensor(m1, m1, m2, ALU.add))
            gs, rank, beats = tiles(m1, GROUPS), tiles(m2, GROUPS), tiles(m3, GROUPS)
            for i in range(GROUPS):
                link.start(V.memset(rank[:, :, i:i + 1], float(GROUPS - 1 - i)))
            for d in range(1, GROUPS):
                n = GROUPS - d
                link.done(V.tensor_tensor(beats[:, :, 0:n], gs[:, :, 0:n], gs[:, :, d:GROUPS], ALU.is_ge))
                link.done(V.tensor_tensor(rank[:, :, d:GROUPS], rank[:, :, d:GROUPS], beats[:, :, 0:n], ALU.add))
                link.done(V.tensor_tensor(rank[:, :, 0:n], rank[:, :, 0:n], beats[:, :, 0:n], ALU.subtract))
            link.done(V.tensor_scalar(m2, m2, float(TOP_GROUPS) - 0.5, 1.0e30, ALU.is_gt, ALU.mult))
            by_group = biased.rearrange("p (g a) -> p g a", a=PER_GROUP)
            link.done(V.tensor_tensor(by_group, by_group, m2.unsqueeze(2).broadcast_to([P, G4, PER_GROUP]), ALU.subtract))
            b3 = tiles(biased)
            for t in range(T):
                link.start(V.max(top8[:, t, :], b3[:, t, :]))
            link.wait()
            for t in range(T):
                link.start(V.max_index(top8_at[:, t, :], top8[:, t, :], b3[:, t, :]))
            link.wait()
            link.done(V.tensor_copy(top8_e, top8_at))
            expert = cr_sb[:, R_EXP:R_EXP + E].unsqueeze(1).broadcast_to([P, T, E])
            for i in range(TOP_E):
                link.start(V.tensor_tensor(tiles(picked[i]), expert, top8_e[:, :, i:i + 1].broadcast_to([P, T, E]),
                                           ALU.is_equal))
            link.wait()
            link.start(V.tensor_tensor(chosen, picked[0], picked[1], ALU.add))
            link.done(V.tensor_tensor(cnt, picked[2], picked[3], ALU.add))
            V.tensor_tensor(chosen, chosen, cnt, ALU.add).then_inc(s_chosen, 1)
            w3 = pair_w.rearrange("p (i t) -> p i t", i=TOP_E)
            for i in range(TOP_E):
                link.done(V.tensor_tensor(tmp, picked[i], scores, ALU.mult))
                link.done(V.tensor_reduce(w3[:, i, :], tiles(tmp), AX_X, ALU.add))
            link.done(V.tensor_reduce(tmp[:, 0:T], pair_w.rearrange("p (i t) -> p t i", i=TOP_E), AX_X, ALU.add))
            link.done(V.tensor_scalar(tmp[:, 0:T], tmp[:, 0:T], 1e-20, None, ALU.add))
            link.done(V.reciprocal(tmp[:, T:2 * T], tmp[:, 0:T]))
            link.done(V.tensor_tensor(w3, w3, tmp[:, T:2 * T].unsqueeze(1).broadcast_to([P, TOP_E, T]), ALU.mult))

            dve.wait_ge(s_rank, 1)
            def whole(v, src, low):
                link.done(V.tensor_scalar(v, src, 1.0 / P, low, ALU.mult, ALU.add))
                link.done(V.tensor_scalar(v, v, ROUND, ROUND, ALU.add, ALU.subtract))

            link.done(V.tensor_copy(load_e, bank[6][:, 0:E]))
            whole(nblk, load_e, (P - 1.0) / P - 0.5 + 0.5 / P)
            link.done(V.tensor_copy(first_a, nblk))
            src, dst = first_a, first_b
            for d in (1, 2, 4, 8):
                link.start(V.tensor_copy(dst[:, 0:d], src[:, 0:d]))
                link.done(V.tensor_tensor(dst[:, d:E], src[:, d:E], src[:, 0:E - d], ALU.add))
                src, dst = dst, src
            link.done(V.tensor_copy(last_blk, src))
            link.done(V.tensor_tensor(first_b, last_blk, nblk, ALU.subtract))
            link.done(V.tensor_scalar(first_b, first_b, float(P), None, ALU.mult))
            link.done(V.tensor_tensor(tiles(slot), bank[5][:, :].rearrange("p (t e) -> p t e", e=E),
                                      first_b.unsqueeze(1).broadcast_to([P, T, E]), ALU.add))
            sl3 = pair_slot.rearrange("p (i t) -> p i t", i=TOP_E)
            for i in range(TOP_E):
                link.done(V.tensor_tensor(tmp, picked[i], slot, ALU.mult))
                link.done(V.tensor_reduce(sl3[:, i, :], tiles(tmp), AX_X, ALU.add))
            whole(pair_blk, pair_slot, -0.5 + 0.5 / P)
            link.start(V.tensor_copy(row_of, pair_slot))
            link.done(V.tensor_scalar(pair_blk, pair_blk, 1.0 - P * BLOCKS, None, ALU.mult))
            link.done(V.scalar_tensor_tensor(pair_blk, pair_slot, float(BLOCKS), pair_blk, ALU.mult, ALU.add))
            V.tensor_copy(put_at, pair_blk).then_inc(s_put, 1)
            link.done(V.memset(tmp[:, 0:BLOCKS], 0.0))
            for e in range(E - 1):
                link.done(V.scalar_tensor_tensor(tmp[:, 0:BLOCKS], cr_sb[:, R_BLK:R_BLK + BLOCKS], last_blk[:, e:e + 1],
                                                 tmp[:, 0:BLOCKS], ALU.is_ge, ALU.add))
            link.start(V.memset(blocks_e[:, BLOCKS:BLOCKS + 8], 0))
            link.done(V.tensor_copy(blocks_e[:, 0:BLOCKS], tmp[:, 0:BLOCKS]))
            V.engine_nop().then_inc(s_expert, 1)

            def shared_chunk(k, c, h):
                n = k * SH + c
                dve.wait_ge(s_ss, n + 1)
                dve.wait_ge(s_su, n + 1)
                if not isinstance(n, int) or n >= 1:
                    dve.wait_ge(s_shh, n)
                    dve.wait_ge(s_shl, n)
                V.scalar_tensor_tensor(s_h, bank[1][:, :], 1.0 / WS, s_silu, ALU.mult, ALU.mult).then_inc(s_sh32, 1)
                dve.wait_ge(s_shh, n + 1)
                V.tensor_tensor(s_hb[:, h, 1, :], s_h, s_hb[:, h, 0, :], ALU.subtract).then_inc(s_shl, 1)

            def shared_sum(k):
                dve.wait_ge(s_sd, SH * (k + 1))
                dve.wait_ge(s_x1i, 16 * (k + 1))
                for t in range(TB):
                    V.scalar_tensor_tensor(x1b[:, t, :], bank[2 + t][:, :], 1.0 / WS, x1b[:, t, :], ALU.mult, ALU.add
                                           ).then_inc(s_x1s, 1)

            def routed_weights_lo(n):
                dve.wait_ge(s_whi_r, n + 1)
                V.scalar_tensor_tensor(only(gu_lo_r, n), stage_r[:, 0:2 * D], WS, only(gu_hi_r, n), ALU.mult, ALU.subtract)
                V.scalar_tensor_tensor(only(dn_lo_r, n), stage_r[:, 2 * D:3 * D], WS, only(dn_hi_r, n),
                                       ALU.mult, ALU.subtract).then_inc(s_wlo_r, 1)

            with dve.Fori(0, FIRST) as k:
                with dve.Fori(0, SH // 2) as i:
                    for h in range(2):
                        shared_chunk(k, 2 * i + h, h)
                    routed_weights_lo(k * (SH // 2) + i)
                shared_sum(k)

            def save_rows(s, j, fresh):
                dve.wait_ge(s_tx, s + 1)
                if not fresh:
                    dve.wait_ge(s_rg, s - 1)
                V.tensor_copy(xgT[:, j, :, :], bank16[j].rearrange("p (n q) -> p n q", n=2 * KC)).then_inc(s_txe, 1)

            def save_h(s, j, fresh):
                dve.wait_ge(s_ht, s + 1)
                if not fresh:
                    dve.wait_ge(s_rd, s - 1)
                V.tensor_copy(r_hT[:, j, :, :], bank16[4 + j][:, 0:2 * P].rearrange("p (v q) -> p v q", v=2)
                              ).then_inc(s_hte, 1)

            def hidden(s, j, fresh):
                dve.wait_ge(s_rs, s + 1)
                if not fresh:
                    dve.wait_ge(s_rhh, s - 1)
                    dve.wait_ge(s_rhl, s - 1)
                V.scalar_tensor_tensor(r_h[:, j, :], bank[2 + j][:, H:2 * H], 1.0 / WS, r_silu[:, j, :], ALU.mult, ALU.mult
                                       ).then_inc(s_rh, 1)
                dve.wait_ge(s_rhh, s + 1)
                V.tensor_tensor(r_hb[:, j, 1, :], r_h[:, j, :], r_hb[:, j, 0, :], ALU.subtract).then_inc(s_rhl, 1)

            save_rows(0, 0, True)
            save_rows(1, 1, True)
            hidden(0, 0, True)
            save_rows(2, 0, False)
            hidden(1, 1, True)
            save_h(0, 0, True)
            with dve.Fori(0, BLOCKS // 4 - 1) as i:
                for n in range(4):
                    s = 4 * i + 1 + n
                    save_rows(s + 2, (1 + n) % 2, False)
                    hidden(s + 1, n % 2, False)
                    save_h(s, (1 + n) % 2, False)
            save_rows(BLOCKS - 1, 1, False)
            hidden(BLOCKS - 2, 0, False)
            save_h(BLOCKS - 3, 1, False)
            hidden(BLOCKS - 1, 1, False)
            save_h(BLOCKS - 2, 0, False)
            save_h(BLOCKS - 1, 1, False)

            def combine(k, p):
                i = k - FIRST
                n = i * TURNS + p
                dve.wait_ge(s_yg[p % 2], 16 * TOP_E * (i * (TURNS // 2) + p // 2 + 1))
                if p < OLD:
                    m, acc = i * OLD + p, x1c[:, p % 2, :]
                    dve.wait_ge(s_x1c[p % 2], 16 * (i * (OLD // 2) + p // 2 + 1))
                else:
                    m, acc = k * TB + p - OLD, x1b[:, p - OLD, :]
                    dve.wait_ge(s_x1i, 16 * (k + 1))
                for e in range(TOP_E):
                    if e:
                        dve.wait_ge(s_cmb, TOP_E * n + e)
                    w = pair_w[:, bass.ds(m + e * T, 1)]
                    V.scalar_tensor_tensor(acc, ybuf[p % 2][:, e, :], w, acc, ALU.mult, ALU.add).then_inc(s_cmb, 1)

            with dve.Fori(FIRST, NB) as k:
                for c in range(SH):
                    shared_chunk(k, c, c % 2)
                    for p in range(c * TURNS // SH, (c + 1) * TURNS // SH):
                        combine(k, p)
                dve.wait_ge(s_cmb, TOP_E * TURNS * (k - FIRST + 1))
                shared_sum(k)

        @block.gpsimd
        def _(pool):
            pool.memset(token_of, 0).then_inc(s_zero, 1)
            pool.wait_ge(s_zero, 1)
            pool.dma_start(token_dram.rearrange("(p n) o -> p (n o)", p=P), token_of).then_inc(s_cleared, 16)
            pool.iota(token_id, pattern=[[P, T]], base=0, channel_multiplier=1).then_inc(s_ids, 1)
            pool.wait_ge(s_misc, 64)
            for q in range(NB):
                pool.wait_ge(s_xn, q * TB + TB)
                xq = x_sb[:, q * TB:q * TB + TB, :]
                pool.tensor_tensor(xq, xq, bo_sb.unsqueeze(1).broadcast_to([P, TB, D]), ALU.add).then_inc(s_xbo, 1)
            def second_norm_lo(k, j):
                pool.wait_ge(s_hi, k + 1)
                if not isinstance(k, int):
                    pool.wait_ge(s_tp2, TB * (k - 1))
                    pool.wait_ge(s_xrw[j], 32 * (k >> 1))
                pool.tensor_tensor(lo16[j], xn, hi16[j], ALU.subtract).then_inc(s_lo, 1)

            for j in range(2):
                second_norm_lo(j, j)
            with pool.Fori(1, NB // 2) as i:
                for j in range(2):
                    second_norm_lo(2 * i + j, j)
            pool.wait_ge(s_put, 1)
            pool.wait_ge(s_ids, 1)
            pool.wait_ge(s_cleared, 16)
            put3 = put_at.rearrange("p (i t) -> p i t", i=TOP_E)
            row3 = row_of.rearrange("p (i t) -> p i t", i=TOP_E)

            def copy_places(t, r):
                pool.tensor_copy(put_now[:, r, :].unsqueeze(2), put3[:, :, bass.ds(t, 1)])
                pool.tensor_copy(id_now[:, r:r + 1], token_id[:, bass.ds(t, 1)]).then_inc(s_put_now, 1)

            def scatter(t, r, last):
                pool.wait_ge(s_put_now, t + 1)
                if not last:
                    n = (r + 1) % 4
                    if not isinstance(t, int) or t >= 3:
                        pool.wait_ge(s_scattered[n], 16 * TOP_E * ((t + 1) // 4))
                    copy_places(t + 1, n)
                for i in range(TOP_E):
                    pool.indirect_dma_start(
                        out=token_dram[:, :], out_offset=bass.IndirectOffsetOnAxis(ap=put_now[:, r, i:i + 1], axis=0),
                        in_=id_now[:, r:r + 1], in_offset=None).then_inc(s_scattered[r], 16)

            copy_places(0, 0)
            for t in range(4):
                scatter(t, t, False)
            with pool.Fori(1, T // 4 - 1) as h:
                for r in range(4):
                    scatter(4 * h + r, r, False)
            for r in range(4):
                scatter(T - 4 + r, r, r == 3)
            for r in range(4):
                pool.wait_ge(s_scattered[r], 16 * NP // P // 4)
            pool.dma_start(token_of, token_dram.rearrange("(p n) o -> p (n o)", p=P)).then_inc(s_tok, 16)
            pool.wait_ge(s_tok, 16)

            def copy_tokens(s, r):
                pool.tensor_copy(token_now[:, r:r + 1], token_of[:, bass.ds(s, 1)]).then_inc(s_token_now, 1)

            def gather(s, r, fresh, last):
                if not fresh:
                    pool.wait_ge(s_tx, s - 3)
                pool.wait_ge(s_token_now, s + 1)
                if not last:
                    copy_tokens(s + 1, (r + 1) % 8)
                pool.indirect_dma_start(
                    out=xg[:, r % 4, :], out_offset=None, in_=xr_dram[:, :],
                    in_offset=bass.IndirectOffsetOnAxis(ap=token_now[:, r:r + 1], axis=0)).then_inc(s_xg[r % 4], 16)

            copy_tokens(0, 0)
            for r in range(8):
                gather(r, r, r < 4, False)
            with pool.Fori(1, BLOCKS // 8 - 1) as i:
                for r in range(8):
                    gather(8 * i + r, r, False, False)
            for r in range(8):
                gather(BLOCKS - 8 + r, r, False, r == 7)
            for j in range(2):
                pool.wait_ge(s_yw[j], 16 * BLOCKS // 2)
            pool.wait_ge(s_rd, BLOCKS)

            def copy_rows(i, p):
                m = i * OLD + p if p < OLD else (FIRST + i) * TB + p - OLD
                pool.tensor_copy(row_now[:, p % 4, :].unsqueeze(2), row3[:, :, bass.ds(m, 1)]).then_inc(s_row_now, 1)

            def gather_y(i, p):
                n = i * TURNS + p
                if not isinstance(n, int) or n >= 2:
                    pool.wait_ge(s_cmb, TOP_E * (n - 1))
                pool.wait_ge(s_row_now, n + 1)
                copy_rows(i + (p + 1) // TURNS, (p + 1) % TURNS)
                for e in range(TOP_E):
                    pool.indirect_dma_start(
                        out=ybuf[p % 2][:, e, :], out_offset=None, in_=y_dram[:, :],
                        in_offset=bass.IndirectOffsetOnAxis(ap=row_now[:, p % 4, e:e + 1], axis=0)).then_inc(s_yg[p % 2], 16)

            copy_rows(0, 0)
            for p in range(TURNS):
                gather_y(0, p)
            with pool.Fori(1, NB - FIRST) as i:
                for p in range(TURNS):
                    gather_y(i, p)


def kernel(x, ctx_1024, L0_xattn_Wq, L0_xattn_bq, L0_xattn_Wk, L0_xattn_bk, L0_xattn_Wv, L0_xattn_bv,
           L0_xattn_Wo, L0_xattn_bo, L0_ffn_router_w, L0_ffn_correction_bias, L0_ffn_gate_w, L0_ffn_up_w,
           L0_ffn_down_w, L0_ffn_shared_gate_w, L0_ffn_shared_up_w, L0_ffn_shared_down_w):
    import concourse.bacc as bacc
    from concourse.bass_utils import run_bass_kernel_spmd

    def chunks(w):
        w = np.asarray(w)
        return np.ascontiguousarray(w.reshape(-1, P, w.shape[-1]).transpose(1, 0, 2))

    def columns(v):
        return np.asarray(v).reshape(-1, P).T

    def rows(v):
        return np.ascontiguousarray(np.broadcast_to(np.asarray(v)[None, :], (P, len(v))))

    ctx = np.asarray(ctx_1024)[:, ::-1, :].reshape(B * M, D)
    gate = np.concatenate([np.asarray(L0_ffn_shared_gate_w).reshape(SH, H, D).transpose(0, 2, 1),
                           np.asarray(L0_ffn_gate_w)])
    up = np.concatenate([np.asarray(L0_ffn_shared_up_w).reshape(SH, H, D).transpose(0, 2, 1),
                         np.asarray(L0_ffn_up_w)])
    gu = np.concatenate([gate, up], axis=2).reshape(SH + E, KC, P, 2 * H).transpose(0, 2, 1, 3)
    dn = np.concatenate([np.asarray(L0_ffn_shared_down_w).T.reshape(SH, H, D), np.asarray(L0_ffn_down_w)])
    const, const_r = constants()
    arrays = {
        "x": np.ascontiguousarray(np.asarray(x).reshape(S, D)),
        "ctxT": chunks(ctx.T),
        "wk": chunks(L0_xattn_Wk), "wqT": chunks(np.asarray(L0_xattn_Wq).T),
        "wv": chunks(L0_xattn_Wv), "wo": chunks(L0_xattn_Wo),
        "biases": np.ascontiguousarray(np.concatenate(
            [columns(L0_xattn_bq), columns(L0_xattn_bk), columns(L0_xattn_bv)], axis=1)),
        "bo": rows(L0_xattn_bo), "cb": rows(L0_ffn_correction_bias),
        "routerT": np.ascontiguousarray(chunks(np.asarray(L0_ffn_router_w).T).reshape(P, KC * E)),
        "gu_w": np.ascontiguousarray(gu.reshape(SH + E, P, 2 * D)),
        "dn_w": np.ascontiguousarray(dn),
        "const": const, "const_r": const_r,
    }
    nc = bacc.Bacc("TRN2", target_bir_lowering=False, num_devices=1)
    args = {n: nc.dram_tensor(f"in_{n}", a.shape, F32, kind="ExternalInput").ap() for n, a in arrays.items()}
    out = nc.dram_tensor("out", (S, D), F32, kind="ExternalOutput").ap()
    build(nc, out=out, **args)
    got = run_bass_kernel_spmd(nc, [{f"in_{n}": a for n, a in arrays.items()}], core_ids=[0])
    return got.results[0]["out"].reshape(B, L, D)
```

```python
from contextlib import ExitStack

import numpy as np

import concourse.bass as bass
from concourse import mybir

F32 = mybir.dt.float32
F16 = mybir.dt.float16
ALU = mybir.AluOpType
ACT = mybir.ActivationFunctionType
AX_X = mybir.AxisListType.X

P = 128
B, L, D = 2, 2048, 512
M = 128
TOP_K = int(2 * np.log(L))
E, H = 16, 128
GROUPS, PER_GROUP, TOP_GROUPS, TOP_E = 4, 4, 2, 4
HS = 1024
SH = HS // H
KC = D // P
S = B * L
T = S // P
TB = 4
NB = S // (P * TB)
BLK = P * TB
NA = L // P
PTW = M + L + M
EARLY = L - BLK
EPS = 1e-5
WS = 64.0
NP = S * TOP_E
BLOCKS = (NP + E * (P - 1)) // P + 1
WITH = NB // 2 - 1
FIRST = WITH + 2
SPLIT = E // (FIRST - WITH)
OLD = 2 * TB
OLD_LAST = FIRST * TB - (NB - FIRST - 1) * OLD
TURNS = OLD + TB
RING = 4
ROWS_RING = 6
ID_MID = S / 2.0
ROUND = 12582912.0
GONE = -3.0e38

C_ID, C_ONES, C_J0, C_J1, C_IS, C_T = 0, 128, 132, 260, 388, 516
C_END = C_T + NA * P
R_EXP, R_BLK, R_TRI = 0, E, E + BLOCKS
R_END = R_TRI + P


def constants():
    c = np.zeros((P, C_END), np.float32)
    eye = np.eye(P, dtype=np.float32)
    c[:, C_ID:C_ID + P] = eye
    c[:, C_ONES:C_ONES + 4] = [1, 1, 1, -1]
    c[0, C_J0] = 1
    c[:, C_J1:C_J1 + P][1:, 1:] = eye[1:, 1:][::-1]
    scale = 1.0 / (4 * D)
    c[:, C_IS:C_IS + P] = eye * scale
    d = np.arange(L)
    hilbert = np.zeros(L)
    hilbert[1::2] = -2.0 / L / np.tan(np.pi * d[1::2] / L)
    q, p = np.arange(P)[:, None], np.arange(P)[None, :]
    for a in range(NA):
        c[:, C_T + a * P:C_T + (a + 1) * P] = scale * hilbert[(P * a + p - q) % L]
    r = np.zeros((P, R_END), np.float32)
    r[:, R_EXP:R_EXP + E] = np.arange(E)
    r[:, R_BLK:R_BLK + BLOCKS] = np.arange(BLOCKS)
    r[:, R_TRI:R_TRI + P] = q < p
    return c, r


class Links:

    def __init__(self, engine, semaphore):
        self.engine, self.semaphore, self.count = engine, semaphore, 0

    def start(self, instruction):
        self.count += 1
        instruction.then_inc(self.semaphore, 1)

    def wait(self):
        self.engine.wait_ge(self.semaphore, self.count)

    def done(self, instruction):
        self.start(instruction)
        self.wait()


def build(nc, x, ctxT, wk, wqT, wv, wo, biases, bo, cb, routerT, gu_w, dn_w, const, const_r, out):
    with ExitStack() as ctx:
        def sem(name):
            return ctx.enter_context(nc.semaphore(name))

        KB = 1024
        R1, R2, R3 = 48 * KB, 96 * KB, 65280
        arena = ctx.enter_context(nc.sbuf_tensor("arena", [P, (R1 + R2 + R3) // 4], F32))

        def view(offset, shape, dt=F32):
            n = int(np.prod(shape))
            v = arena[:, offset // 4:(offset + n * (2 if dt == F16 else 4)) // 4]
            if dt != F32:
                v = v.bitcast(dt)
            if len(shape) == 2:
                v = v.rearrange("p (a b) -> p a b", a=shape[0])
            elif len(shape) == 3:
                v = v.rearrange("p (a b c) -> p a b c", a=shape[0], b=shape[1])
            return v

        wk_sb, wq_sb = view(0, [KC, D]), view(8 * KB, [KC, D])
        wv_sb, wo_sb = view(16 * KB, [KC, D]), view(24 * KB, [KC, D])
        ctx_sb = view(32 * KB, [KC, B * M])
        kT, vT = view(36 * KB, [KC, B * M]), view(40 * KB, [KC, B * M])
        gu_hi_s, gu_lo_s = view(0, [SH, 2 * D], F16), view(16 * KB, [SH, 2 * D], F16)
        dn_hi_s, dn_lo_s = view(32 * KB, [SH, D], F16), view(40 * KB, [SH, D], F16)
        o = R1
        x_sb = view(o, [T, D])
        xnT = [view(o + 64 * KB, [KC, BLK]), view(o + 72 * KB, [KC, BLK])]
        skew_c, skew_d = view(o + 80 * KB, [L]), view(o + 88 * KB, [L])
        xtb_c = view(o + 80 * KB, [2, 2 * KC, BLK], F16)
        gu_hi_r, gu_lo_r = view(o, [E, 2 * D], F16), view(o + 32 * KB, [E, 2 * D], F16)
        dn_hi_r, dn_lo_r = view(o + 64 * KB, [E, D], F16), view(o + 80 * KB, [E, D], F16)
        o1 = R1 + R2
        c_sb = view(o1, [C_END])
        vo = view(o1 + 10368, [B, D])
        st = [view(o1 + 14464, [BLK]), view(o1 + 16512, [BLK])]
        s_silu, s_h = view(o1, [BLK]), view(o1 + 2 * KB, [BLK])
        s_hb = view(o1 + 4 * KB, [2, 2, BLK], F16)
        scores = view(o1 + 8 * KB, [T * E])
        xtb_p = arena[:, (o1 + 10368) // 4:(o1 + 10368 + 32 * KB) // 4].bitcast(F16).rearrange(
            "p (j r) -> p j r", j=2)[:, :, 0:2 * KC * BLK].rearrange("p j (n q) -> p j n q", n=2 * KC)
        o2 = o1 + 18560
        pt = [view(o2, [PTW]), view(o2 + PTW * 4, [PTW])]
        hi16 = [view(o2, [TB, D], F16), view(o2 + 32 * KB, [TB, D], F16)]
        lo16 = [view(o2 + 4 * KB, [TB, D], F16), view(o + 76 * KB, [TB, D], F16)]
        biased, tmp, cnt, slot = (view(o2 + 2 * KB * i, [T * E]) for i in range(4))
        xg = view(o2, [4, 2 * D], F16)
        router_rows = view(o2 + 8 * KB, [2 * KC, BLK], F16)
        x1b = view(o2 + 16 * KB, [TB, D])
        row, taken = [view(o2, [L]), view(o2 + 16 * KB, [L])], [view(0, [L]), view(o + 64 * KB, [L])]
        bo_sb = view(o2 + 20 * KB, [D])
        o3 = o2 + 24 * KB
        xn = view(o3, [TB, D])
        g_sb = view(o3 + 8 * KB, [KC, B * M])
        stage = [view(o + 64 * KB, [3 * D]), view(o + 70 * KB, [3 * D])]
        stage_r = [view(o3, [3 * D]), view(o3 + 6 * KB, [3 * D])]
        top8 = view(o + 89 * KB, [T, 8])
        top8_at = view(o + 90 * KB, [T, 8], mybir.dt.uint32)
        top8_e = view(o + 91 * KB, [T, 8])
        picked = [view(o + 92 * KB + KB * i, [T * E], F16) for i in range(TOP_E)]
        hot_row = [view(o2 + KB * i, [TOP_E, P], F16) for i in range(4)]
        hot_blk = [view(o2 + 4 * KB + 2 * BLOCKS * TOP_E * i, [TOP_E, BLOCKS], F16) for i in range(3)]
        hot_blk.append(view(o1 + 8 * KB, [TOP_E, BLOCKS], F16))
        xgT = view(o3, [2, 2 * KC, P], F16)
        xgT_odd = view(o1, [2, 2 * KC, P], F16)
        y_sb = view(o3 + 4 * KB, [2, D])
        r_silu, r_h = view(o3 + 8 * KB, [2, H]), view(o3 + 9 * KB, [2, H])
        r_hb, r_hT = view(o3 + 10 * KB, [2, 2, H], F16), view(o3 + 11 * KB, [2, 2, P], F16)
        ybuf = [view(o + 8 * KB * r, [TOP_E, D]) for r in range(RING)]
        x1c = view(o + 8 * KB * RING, [RING, D])
        o4 = o3 + 12 * KB
        small = view(o4, [(R1 + R2 + R3 - o4) // 4])
        at = [0]

        def little(n, dt=F32):
            words = n if dt != F16 else (n + 1) // 2
            v = small[:, at[0]:at[0] + words]
            at[0] += words
            assert at[0] <= (R1 + R2 + R3 - o4) // 4
            return v if dt == F32 else v.bitcast(dt)

        I32 = mybir.dt.int32
        blocks_e = little(BLOCKS + 8, I32)
        chosen_after = little((T + 1) * E, F16)
        chosen = chosen_after[:, E:]
        bias_sb = little(3 * KC)
        bqk = little(B)
        id16 = little(P, F16)
        early = little(2 * TB * E)
        rt32 = little(KC * E)
        rt_hi, rt_lo = (little(KC * E, F16).rearrange("p (k e) -> p k e", k=KC) for _ in range(2))
        cb_sb = little(E)
        cr_sb = little(R_END)
        tri16, ones16 = little(P, F16), little(P, F16)
        stats = little(TB * 6).rearrange("p (t s) -> p t s", t=TB)
        mv2 = [little(TB * 2).rearrange("p (t s) -> p t s", t=TB) for _ in range(2)]
        var2, std2, rstd2 = ([little(TB) for _ in range(2)] for _ in range(3))
        mv, var_eps, std, rstd = mv2[0], var2[0], std2[0], rstd2[0]
        sums = little(2 * NA).rearrange("p (v a) -> p v a", v=2)
        mirrored = little(2 * (NA + 1)).rearrange("p (v a) -> p v a", v=2)
        even_s = little(NA)
        even_w = little(2 * NA)
        meanT = little(P)
        best = little(16)
        top_e = little(16)
        negmax, total, inv = little(1), little(1), little(1)
        token_int = little(T, I32)
        token_of = little(BLOCKS, I32)
        row_of = little(NP // P, I32)
        pair_row = little(NP // P, F16)
        places16 = little(BLOCKS, F16)
        token_id = little(T)
        row_now = little(ROWS_RING * TOP_E, I32).rearrange("p (r i) -> p r i", r=ROWS_RING)
        token_now = little(8, I32)
        pair_slot, pair_w, pair_blk = little(NP // P), little(NP // P), little(NP // P)
        load_e, nblk, first_a, first_b, last_blk = (early[:, E * i:E * i + E] for i in range(5))

        bank = [ctx.enter_context(nc.psum_tensor(f"bank{i}", [P, 512], F32)) for i in range(8)]
        bank16 = [bk[:, :].bitcast(F16) for bk in bank]

        pt_dram = nc.dram_tensor("pt_dram", [B, P, PTW], F32)
        mean_dram = nc.dram_tensor("mean_dram", [B, L], F32)
        g_dram = nc.dram_tensor("g_dram", [B, M + L], F32)
        xr_dram = nc.dram_tensor("xr_dram", [S, 2 * D], F16)
        x1_dram = nc.dram_tensor("x1_dram", [S, D], F32)
        x1s_dram = nc.dram_tensor("x1s_dram", [S, D], F32)
        y_dram = nc.dram_tensor("y_dram", [BLOCKS * P, D], F32)
        x_rows = x.rearrange("(q t p) d -> q p t d", t=TB, p=P)
        xr_rows = xr_dram.rearrange("(q t p) d -> q p t d", t=TB, p=P)
        x1_rows = x1_dram.rearrange("(q t p) d -> q p t d", t=TB, p=P)
        x1s_rows = x1s_dram.rearrange("(q t p) d -> q p t d", t=TB, p=P)
        x1s_tiles = x1s_dram.rearrange("(t p) d -> t p d", p=P)
        out_rows = out.rearrange("(q t p) d -> q p t d", t=TB, p=P)
        out_tiles = out.rearrange("(t p) d -> t p d", p=P)
        y_tiles = y_dram.rearrange("(n p) d -> n p d", p=P)

        def only(v, i, *rest):
            v = v[(slice(None), bass.ds(i, 1)) + rest]
            names = "abcd"[:len(v.shape) - 1]
            if len(v.shape) == 3:
                return v.rearrange("p a b -> p (a b)")
            return v.rearrange("p a b c -> p (a b) c")

        def item(d, i):
            d = d[bass.ds(i, 1)]
            if len(d.shape) == 3:
                return d.rearrange("a p n -> (a p) n")
            return d.rearrange("a p t n -> (a p) t n")

        def skewed(b, start, pitch, first, end):
            return bass.AP(pt_dram, b * P * PTW + start + first, [[pitch, P], [1, end - first]])

        s_const, s_tables, s_kw2 = sem("identity_in"), sem("tables_in"), sem("wk_in_2")
        s_kw, s_qw, s_vw, s_ow = (sem(n) for n in ("wk_in", "wq_in", "wv_in", "wo_in"))
        s_x = [sem(f"x_in{q}") for q in range(NB)]
        s_misc = sem("router_in")
        s_mm, s_mm_sb = sem("projection_done"), sem("projection_saved")
        s_var, s_std, s_xn = sem("var_ready"), sem("std_ready"), sem("xn_ready")
        s_tp, s_tp_sb = sem("transposed"), sem("transposes_saved")
        s_pt, s_pt_sb = sem("pt_done"), sem("pt_saved")
        s_ptw = [sem(f"pt_written{b}") for b in range(B)]
        s_sk, s_sk2 = ([sem(f"skew_{part}_in{b}") for b in range(B)] for part in ("early", "late"))
        s_u, s_u_sb = sem("sums_done"), sem("sums_saved")
        s_ev, s_ev_sb = sem("even_done"), sem("even_saved")
        s_mT, s_mT_sb = sem("mean_done"), sem("mean_saved")
        s_mw = [sem(f"mean_written{b}") for b in range(B)]
        s_row = [sem(f"row_in{b}") for b in range(B)]
        s_best, s_exp = sem("best_ready"), sem("exp_done")
        s_g, s_gw = sem("g_ready"), sem("g_written")
        s_xbo = sem("x_plus_bo")
        s_st = [sem("circulant_in0"), sem("circulant_in1")]
        s_at, s_x1, s_bn = sem("attention_done"), sem("x1_ready"), sem("bn_stats_done")
        s_mv, s_rstd = sem("moments_ready"), sem("rstd_ready")
        s_var2, s_std2, s_xn2 = sem("var2_ready"), sem("std2_ready"), sem("xn2_ready")
        s_hi, s_lo = sem("xn2_hi_ready"), sem("xn2_lo_ready")
        s_tp2 = sem("xn2_turned")
        s_lg, s_lgs = sem("logits_done"), sem("logits_saved")
        s_x1w = sem("x1_written")
        s_xrw = [sem("xr_written0"), sem("xr_written1")]
        s_stage = [sem("stage_in0"), sem("stage_in1")]
        s_stage_r = [sem("routed_stage_in0"), sem("routed_stage_in1")]
        s_whi, s_wlo = sem("shared_w_hi"), sem("shared_w_lo")
        s_wrd_r = sem("routed_w_read")
        s_whi_r, s_wlo_r = sem("routed_w_hi"), sem("routed_w_lo")
        s_rt = sem("router_split")
        s_sig, s_chosen, s_rank = sem("scores_ready"), sem("chosen_ready"), sem("ranks_done")
        s_expert = sem("block_experts_ready")
        s_hot, s_hot_used, s_tok = sem("one_hot_ready"), sem("one_hot_used"), sem("tokens_ready")
        s_token_now, s_row_now = sem("tokens_copied"), sem("rows_copied")
        s_ids = sem("token_ids_ready")
        s_dve = sem("dve_step")
        s_xt, s_x1i = sem("xt_in"), sem("x1_in")
        s_sg, s_su, s_ss, s_sh32 = sem("shared_gate"), sem("shared_up"), sem("shared_silu"), sem("shared_h32")
        s_shh, s_shl, s_sd = sem("shared_h_hi"), sem("shared_h_lo"), sem("shared_down")
        s_x1s, s_x1sw = sem("x1s_ready"), sem("x1s_written")
        s_xg = [sem(f"rows_gathered{r}") for r in range(4)]
        s_tx, s_txe = sem("even_rows_turned"), sem("even_rows_turned_saved")
        s_odd = [sem(f"odd_rows_turned{h}") for h in range(2)]
        s_rg, s_rs, s_rh = sem("routed_gate_up"), sem("routed_silu"), sem("routed_h32")
        s_rhh, s_rhl = sem("routed_h_hi"), sem("routed_h_lo")
        s_ht, s_hte, s_rd = sem("routed_h_turned"), sem("routed_h_turned_saved"), sem("routed_down")
        s_ye = sem("y_saved")
        s_yw = [sem("y_written0"), sem("y_written1")]
        s_yg = [sem(f"y_gathered{r}") for r in range(RING)]
        s_x1c = [sem(f"x1s_in{r}") for r in range(RING)]
        s_cmb = sem("result_added")
        s_out = [sem(f"out_written{r}") for r in range(RING)]
        s_out_blk = sem("out_block_written")

        block = ctx.enter_context(nc.Block())
        PARTS = ((0, 0), (0, 1), (1, 0))

        def settled(engine):
            engine.wait_ge(s_const, 16)

        @block.sync
        def _(sp):
            sp.dma_start(ctx_sb, ctxT).then_inc(s_kw, 16)
            sp.dma_start(wk_sb[:, 0:KC // 2, :], wk[:, 0:KC // 2, :]).then_inc(s_kw, 16)
            sp.dma_start(bias_sb, biases).then_inc(s_kw, 16)
            sp.dma_start(wk_sb[:, KC // 2:KC, :], wk[:, KC // 2:KC, :]).then_inc(s_kw2, 16)
            for q in range(NB):
                sp.dma_start(x_sb[:, TB * q:TB * q + TB, :], x_rows[q]).then_inc(s_x[q], 16)
                if q == 0:
                    sp.dma_start(wq_sb, wqT).then_inc(s_qw, 16)
                    sp.dma_start(c_sb[:, 0:C_J0], const[:, 0:C_J0]).then_inc(s_const, 16)
                if q == 1:
                    sp.dma_start(bo_sb, bo).then_inc(s_misc, 16)
                    sp.dma_start(rt32, routerT).then_inc(s_misc, 16)
                    sp.dma_start(cb_sb, cb).then_inc(s_misc, 16)
                    sp.dma_start(cr_sb, const_r).then_inc(s_misc, 16)
            sp.dma_start(c_sb[:, C_J0:C_END], const[:, C_J0:C_END]).then_inc(s_tables, 16)
            sp.dma_start(wv_sb, wv).then_inc(s_vw, 16)
            sp.dma_start(wo_sb, wo).then_inc(s_ow, 16)

            def skew_early(b):
                sp.wait_ge(s_pt_sb, 4 * b + 3)
                sp.dma_start(pt_dram[b][:, M:M + EARLY], pt[b][:, M:M + EARLY]).then_inc(s_ptw[b], 16)
                sp.wait_ge(s_ptw[b], 16)
                if b:
                    sp.wait_ge(s_u, b)
                sp.dma_start(skew_c[:, 0:EARLY - M], skewed(b, 2 * M - 1, PTW - 1, 0, EARLY - M)).then_inc(s_sk[b], 16)
                sp.dma_start(skew_d[:, M:EARLY], skewed(b, 1, PTW + 1, M, EARLY)).then_inc(s_sk[b], 16)

            def skew_late(b):
                sp.wait_ge(s_pt_sb, 4 * (b + 1))
                sp.dma_start(pt_dram[b][:, M + EARLY:PTW], pt[b][:, M + EARLY:PTW]).then_inc(s_ptw[b], 16)
                sp.dma_start(pt_dram[b][:, 0:M], pt[b][:, 0:M]).then_inc(s_ptw[b], 16)
                sp.wait_ge(s_ptw[b], 48)
                sp.dma_start(skew_c[:, EARLY - M:L], skewed(b, 2 * M - 1, PTW - 1, EARLY - M, L)).then_inc(s_sk2[b], 16)
                sp.dma_start(skew_d[:, EARLY:L], skewed(b, 1, PTW + 1, EARLY, L)).then_inc(s_sk2[b], 16)
                sp.dma_start(skew_d[:, 0:M], skewed(b, 1, PTW + 1, 0, M)).then_inc(s_sk2[b], 16)

            def means(b):
                sp.wait_ge(s_mT_sb, b + 1)
                sp.dma_start(mean_dram[b].rearrange("(a p) -> a p", p=P), meanT[0:NA, :]).then_inc(s_mw[b], 16)
                sp.wait_ge(s_mw[b], 16)
                sp.dma_start(row[b][0:1, :], mean_dram[b:b + 1, :]).then_inc(s_row[b], 16)

            def delays(b):
                sp.wait_ge(s_g, b + 1)
                sp.dma_start(g_dram[b:b + 1, M:M + L], row[b][0:1, :]).then_inc(s_gw, 16)
                sp.dma_start(g_dram[b:b + 1, 0:M], row[b][0:1, L - M:L]).then_inc(s_gw, 16)
                sp.wait_ge(s_gw, 32 * (b + 1))

            def circulant(k, j):
                sp.dma_start(st[j], bass.AP(g_dram, (k // (NB // B)) * (M + L) + k % (NB // B) * BLK + 1, [[1, P], [1, BLK]])
                             ).then_inc(s_st[j], 16)

            def x1_out(k):
                sp.wait_ge(s_x1, TB * (k + 1))
                sp.dma_start(x1_rows[k], x_sb[:, k * TB:k * TB + TB, :]).then_inc(s_x1w, 16)

            def second_norm_out(k, j):
                sp.wait_ge(s_hi, k + 1)
                sp.dma_start(xr_rows[k][:, :, 0:D], hi16[j]).then_inc(s_xrw[j], 16)
                sp.wait_ge(s_lo, k + 1)
                sp.dma_start(xr_rows[k][:, :, D:2 * D], lo16[j]).then_inc(s_xrw[j], 16)

            def next_circulant(k, j):
                sp.wait_ge(s_at, TB * (k + 1))
                circulant(k + 2, j)

            def turned(k, dst):
                sp.wait_ge(s_xrw[k % 2], 32 * (k // 2 + 1))
                return sp.dma_start_transpose(dst, xr_dram[k * BLK:(k + 1) * BLK, :])

            def for_router(k):
                sp.wait_ge(s_lg, k)
                turned(k, router_rows).then_inc(s_tp2, 16)

            def turned_in(k, dst):
                sp.wait_ge(s_xt, 16 * k)
                turned(k, dst).then_inc(s_xt, 16)

            def x1_in(k):
                sp.dma_start(x1b, x1_rows[k]).then_inc(s_x1i, 16)

            def x1s_out(k):
                sp.wait_ge(s_x1s, TB * (k + 1))
                sp.dma_start(x1s_rows[k], x1b).then_inc(s_x1sw, 16)

            def routed_weights(n, j):
                if not isinstance(n, int) or n >= 2:
                    sp.wait_ge(s_wlo_r, n - 1)
                sp.dma_start(stage_r[j][:, 0:2 * D], item3(gu_w, SH + n)).then_inc(s_stage_r[j], 16)
                sp.dma_start(stage_r[j][:, 2 * D:3 * D], item3(dn_w, SH + n)).then_inc(s_stage_r[j], 16)

            def item3(d, i):
                return d[bass.ds(i, 1)].rearrange("a p n -> (a p) n")

            skew_early(0)
            skew_late(0)
            means(0)
            skew_early(1)
            skew_late(1)
            delays(0)
            for k in range(2):
                circulant(k, k)
            for k in range(2):
                next_circulant(k, k)
            second_norm_out(0, 0)
            sp.wait_ge(s_u, B)
            turned_in(0, xtb_c[:, 0, :, :])
            second_norm_out(1, 1)
            turned_in(1, xtb_c[:, 1, :, :])
            sp.wait_ge(s_xbo, NB)
            means(1)
            for k in range(2):
                x1_out(k)
            for i in range(1, NB // 2):
                a, b = 2 * i, 2 * i + 1
                if 1 < i < NB // 2 - 1:
                    next_circulant(a, 0)
                x1_out(a)
                second_norm_out(a, 0)
                for_router(a)
                if 1 < i < NB // 2 - 1:
                    next_circulant(b, 1)
                x1_out(b)
                second_norm_out(b, 1)
                for_router(b)
                if i == 1:
                    delays(1)
                    next_circulant(a, 0)
                    next_circulant(b, 1)
                    x1_in(0)
                if i == WITH:
                    turned_in(WITH, xtb_p[:, 0, :, :])
                if i == WITH:
                    sp.wait_ge(s_lo, NB)
                    sp.wait_ge(s_xrw[1], 16 * NB)
                    for n in range(2):
                        routed_weights(n, n)
                x1s_out(i - 1)
                if i + 1 < WITH:
                    turned_in(i + 1, xtb_c[:, (i + 1) % 2, :, :])
                if i == WITH:
                    sp.wait_ge(s_lg, NB)
                    turned_in(WITH + 1, xtb_p[:, 1, :, :])
                sp.wait_ge(s_x1sw, 16 * i)
                sp.wait_ge(s_x1w, 16 * (2 * i + 2))
                x1_in(i)

            def later_turned_in(k):
                turned_in(k + 2, xtb_p[:, (k - WITH) % 2, :, :])

            def next_x1_in(k):
                sp.wait_ge(s_x1sw, 16 * (k + 1))
                x1_in(k + 1)

            for k in range(WITH, FIRST):
                with sp.Fori(0, SPLIT // 2 - (k == FIRST - 1)) as e:
                    for j in range(2):
                        routed_weights((k - WITH) * SPLIT + 2 * e + 2 + j, j)
                if k < FIRST - 1:
                    x1s_out(k)
                    later_turned_in(k)
                    next_x1_in(k)

            def y_out(s, j):
                sp.wait_ge(s_ye, s + 1)
                sp.dma_start(item(y_tiles, s), y_sb[:, j, :]).then_inc(s_yw[j], 16)

            def turn_odd(h, gathered, used):
                settled(sp)
                sp.wait_ge(s_xg[2 * h + 1], gathered)
                if used is not None:
                    sp.wait_ge(s_rg, used)
                sp.dma_start_transpose(xgT_odd[:, h, :, :], xg[:, 2 * h + 1, :]).then_inc(s_odd[h], 16)

            def four_blocks(i):
                loop = not isinstance(i, int)
                gathered = sp.to_reg(16 * i + 16) if loop else 16 * i + 16
                for h in range(2):
                    used = 4 * i + (2 * h - 2)
                    turn_odd(h, gathered, sp.to_reg(used) if loop else used)
                    for r in (2 * h, 2 * h + 1):
                        y_out(4 * i - 4 + r, r % 2)

            sp.wait_ge(s_shl, FIRST * SH)
            for h in range(2):
                turn_odd(h, 16, None)
            four_blocks(1)
            x1s_out(FIRST - 1)
            four_blocks(2)
            later_turned_in(FIRST - 1)
            four_blocks(3)
            next_x1_in(FIRST - 1)
            with sp.Fori(4, BLOCKS // 4) as i:
                four_blocks(i)
            for s in range(BLOCKS - 4, BLOCKS):
                y_out(s, s % 2)

            def take(o, j):
                if not isinstance(o, int) or o >= RING:
                    sp.wait_ge(s_out[j], 16 * (o // RING))
                sp.dma_start(x1c[:, j, :], item(x1s_tiles, o)).then_inc(s_x1c[j], 16)

            def results_out(k, old, last):
                for p in range(old):
                    o = (k - FIRST) * OLD + p
                    sp.wait_ge(s_cmb, TOP_E * ((k - FIRST) * TURNS + p + 1))
                    sp.dma_start(item(out_tiles, o), x1c[:, p % RING, :]).then_inc(s_out[p % RING], 16)
                    if not last or p < old - RING:
                        take(o + RING, p % RING)
                sp.wait_ge(s_x1s, TB * (k + 1))
                sp.dma_start(item(out_rows, k), x1b).then_inc(s_out_blk, 16)

            sp.wait_ge(s_rd, BLOCKS)
            for j in range(2):
                sp.wait_ge(s_yw[j], 16 * BLOCKS // 2)
            sp.wait_ge(s_x1sw, 16 * FIRST)
            for o in range(RING):
                take(o, o)
            for k in range(FIRST, NB):
                results_out(k, OLD_LAST if k == NB - 1 else OLD, k == NB - 1)
                if k + 2 < NB:
                    turned_in(k + 2, xtb_p[:, (k - WITH) % 2, :, :])
                sp.wait_ge(s_out_blk, 16 * (k - FIRST + 1))
                if k + 1 < NB:
                    sp.dma_start(x1b, x1_rows[k + 1]).then_inc(s_x1i, 16)
            for r in range(RING):
                sp.wait_ge(s_out[r], 16 * (FIRST * TB // RING))

        @block.tensor
        def _(pe):
            mm, turn = nc.tensor.matmul, nc.tensor.transpose

            def project(dst, lhs, rhs):
                for k in range(KC):
                    last = mm(dst, lhs(k), rhs(k), start=(k == 0), stop=(k == KC - 1))
                last.then_inc(s_mm, 1)

            def turn_first(q):
                for t in range(TB):
                    pe.wait_ge(s_xn, q * TB + t + 1)
                    if q:
                        pe.wait_ge(s_tp_sb, (q - 1) * TB + t + 1)
                    for k in range(KC):
                        last = turn(bank[t][:, k * P:k * P + P], xn[:, t, k * P:k * P + P], c_sb[:, C_ID:C_ID + P])
                    last.then_inc(s_tp, 1)

            def correlate(q):
                pe.wait_ge(s_tp_sb, q * TB + TB)
                if q >= 2:
                    pe.wait_ge(s_pt_sb, q - 1)
                b = q // 4
                for k in range(KC):
                    last = mm(bank[4 + q % 2][:, :], g_sb[:, k, b * M:b * M + M], xnT[q % 2][:, k, :],
                              start=(k == 0), stop=(k == KC - 1))
                last.then_inc(s_pt, 1)

            pe.wait_ge(s_kw, 48)
            for k in range(KC):
                if k == KC // 2:
                    pe.wait_ge(s_kw2, 16)
                for c in range(KC):
                    last = mm(bank[c][:, 0:B * M], wk_sb[:, k, c * P:c * P + P], ctx_sb[:, k, :],
                              start=(k == 0), stop=(k == KC - 1))
                    if k == KC - 1:
                        last.then_inc(s_mm, 1)
            pe.wait_ge(s_mm_sb, 4)
            for b in range(B):
                for k in range(KC):
                    last = mm(bank[7][:, B * M + b:B * M + b + 1], kT[:, k, b * M:b * M + M], bias_sb[:, k:k + 1],
                              start=(k == 0), stop=(k == KC - 1))
            last.then_inc(s_mm, 1)
            pe.wait_ge(s_qw, 16)
            pe.wait_ge(s_const, 16)
            for c in range(KC):
                if c == 2:
                    turn_first(0)
                if c == 3:
                    pe.wait_ge(s_mm_sb, 5)
                project(bank[4 + c][:, 0:B * M], lambda k: wq_sb[:, k, c * P:c * P + P], lambda k: kT[:, k, :])
            pe.wait_ge(s_mm_sb, 9)

            def skewed_sums(b, tiles):
                for a in tiles:
                    mm(bank[6][:, 2 * a:2 * a + 2], skew_c[:, a * P:a * P + P], c_sb[:, C_ONES:C_ONES + 2],
                       start=True, stop=False)
                    last = mm(bank[6][:, 2 * a:2 * a + 2], skew_d[:, a * P:a * P + P],
                              c_sb[:, C_ONES + 2:C_ONES + 4], start=False, stop=True)
                return last

            def sums_early(b):
                pe.wait_ge(s_sk[b], 32)
                if b:
                    pe.wait_ge(s_u_sb, 3 * b)
                skewed_sums(b, range(1, EARLY // P - 1))

            def sums_late(b):
                pe.wait_ge(s_sk2[b], 48)
                skewed_sums(b, [0, *range(EARLY // P - 1, NA)]).then_inc(s_u, 1)

            def even_parts(b):
                pe.wait_ge(s_u_sb, 3 * (b + 1))
                pe.wait_ge(s_tables, 16)
                if b:
                    pe.wait_ge(s_mT_sb, b)
                e = bank[7][:, 0:2 * NA].rearrange("p (v a) -> p v a", v=2)
                mm(e, c_sb[:, C_ID:C_ID + P], sums, start=True, stop=False)
                mm(e, c_sb[:, C_J0:C_J0 + P], mirrored[:, :, 0:NA], start=False, stop=False)
                mm(e, c_sb[:, C_J1:C_J1 + P], mirrored[:, :, 1:NA + 1], start=False, stop=True).then_inc(s_ev, 1)

            def mean_correlation(b):
                pe.wait_ge(s_ev_sb, 3 * (b + 1))
                m = bank[7][0:NA, 64:64 + P]
                mm(m, even_s, c_sb[:, C_IS:C_IS + P], start=True, stop=False)
                for a in range(NA):
                    last = mm(m, even_w[:, NA - a:2 * NA - a], c_sb[:, C_T + a * P:C_T + a * P + P],
                              start=False, stop=(a == NA - 1))
                last.then_inc(s_mT, 1)

            for q in range(NB - 2):
                turn_first(q + 1)
                if q == NB - 3:
                    sums_early(0)
                correlate(q)
            sums_late(0)
            turn_first(NB - 1)
            even_parts(0)
            mean_correlation(0)
            correlate(NB - 2)
            correlate(NB - 1)
            pe.wait_ge(s_vw, 16)
            pe.wait_ge(s_tp_sb, T)
            for c in range(KC):
                project(bank[c][:, 0:B * M], lambda k: wv_sb[:, k, c * P:c * P + P], lambda k: ctx_sb[:, k, :])
            pe.wait_ge(s_ow, 16)
            pe.wait_ge(s_mm_sb, 13)
            pe.wait_ge(s_pt_sb, NB)
            for b in range(B):
                project(bank[4 + b][:, :], lambda k: vT[:, k, b * M:b * M + M], lambda k: wo_sb[:, k, :])


            pe.wait_ge(s_rt, 3)
            pe.wait_ge(s_mm_sb, 15)

            def attention(n, j, banks):
                pe.wait_ge(s_st[j], 16 * ((n >> 1) + 1))
                for t in range(TB):
                    if t == 2 and banks[t] == 6:
                        pe.wait_ge(s_lgs, n)
                    elif t >= 2 and banks[t] == t - 2:
                        pe.wait_ge(s_x1, t - 1)
                    mm(bank[banks[t]][:, :], st[j][:, t * P:t * P + P], only(vo, n // (NB // B)), start=True, stop=True
                       ).then_inc(s_at, 1)

            def logits(n, rows):
                for t in range(TB):
                    for m, (xv, wp, c) in enumerate((xv, wp, c) for xv, wp in PARTS for c in range(KC)):
                        last = mm(bank[6][:, t * E:t * E + E], rows[:, xv * KC + c, t * P:t * P + P],
                                  (rt_hi, rt_lo)[wp][:, c, :], start=(m == 0), stop=(m == 3 * KC - 1))
                last.then_inc(s_lg, 1)

            def shared_gate_up(k, xt, c, read):
                for g, s_done in ((0, s_sg), (1, s_su)):
                    if read:
                        pe.wait_ge(*read[g])
                    n = 0
                    for xv, wp in PARTS:
                        for kc in range(KC):
                            w = only((gu_hi_s, gu_lo_s)[wp], c, slice(kc * 2 * H + g * H, kc * 2 * H + g * H + H))
                            last = mm(bank[g][:, :], w, xt(xv * KC + kc), start=(n == 0), stop=(n == 3 * KC - 1))
                            n += 1
                    last.then_inc(s_done, 1)

            def used(k, c):
                return (s_ss, k * SH + c), (s_sh32, k * SH + c)

            def added(n):
                return (s_x1, n * TB + 1), (s_x1, n * TB + 2)

            def shared_down(k, c, half, first, final):
                pe.wait_ge(s_shl, k * SH + c + 1)
                for t in range(TB):
                    for n, (hv, wp) in enumerate(PARTS):
                        last = mm(bank[2 + t][:, :], s_hb[:, half, hv, t * P:t * P + P], only((dn_hi_s, dn_lo_s)[wp], c),
                                  start=(first and n == 0), stop=(final and n == 2))
                last.then_inc(s_sd, 1)

            sums_early(1)
            attention(0, 0, (0, 1, 2, 3))
            attention(1, 1, (4, 5, 0, 1))
            sums_late(1)
            even_parts(1)
            mean_correlation(1)
            pe.wait_ge(s_mT_sb, 2)
            for n in range(2):
                pe.wait_ge(s_xt, 16 * (n + 1))
                if n:
                    pe.wait_ge(s_lgs, n)
                logits(n, xtb_c[:, n, :, :])
            pe.wait_ge(s_x1, 2 * TB)
            with pe.Fori(1, NB // 2) as i:
                a, b, s = 2 * i, 2 * i + 1, i - 1
                xt = lambda n: only(xtb_c, s % 2, n)
                pe.wait_ge(s_xt, 16 * (s + 1))
                pe.wait_ge(s_sh32, s * SH)
                attention(a, 0, (0, 1, 6, 7))
                for c in range(SH):
                    pe.wait_ge(s_wlo, c + 1)
                    if c == TB:
                        pe.wait_ge(s_sh32, s * SH + c)
                        attention(b, 1, (0, 1, 6, 7))
                    shared_gate_up(s, xt, c, added(a) if c == 0 else added(b) if c == TB else used(s, c))
                    if c == 1:
                        pe.wait_ge(s_x1s, s * TB)
                    if c:
                        shared_down(s, c - 1, (c - 1) % 2, c == 1, False)
                    if c % TB == 3:
                        pe.wait_ge(s_tp2, 16 * (a + c // TB - 1))
                        logits(a + c // TB, router_rows)
                shared_down(s, SH - 1, 1, False, True)

            def places():
                pe.wait_ge(s_chosen, 1)
                mm(bank[6][:, :], tri16, chosen, start=True, stop=False)
                for t in range(T - 1, 1, -1):
                    mm(bank[6][:, t * E:T * E], ones16, chosen[:, 0:(T - t) * E], start=False, stop=False,
                       skip_group_check=True)
                mm(bank[6][:, :], ones16, chosen_after[:, 0:T * E], start=False, stop=True)
                for t in range(T):
                    last = mm(bank[7][:, 0:E], ones16, chosen[:, t * E:t * E + E], start=(t == 0), stop=(t == T - 1))
                last.then_inc(s_rank, 1)

            def shared_with_places():
                k, xt = WITH, lambda n: xtb_p[:, 0, n, :]
                pe.wait_ge(s_xt, 16 * (k + 1))
                for c in range(SH):
                    shared_gate_up(k, xt, c, used(k, c))
                    if c == 1:
                        pe.wait_ge(s_x1s, k * TB)
                    if c:
                        shared_down(k, c - 1, (c - 1) % 2, c == 1, False)
                    if c == 3:
                        places()
                shared_down(k, SH - 1, 1, False, True)

            def shared(k, after=None):
                xt = lambda n: only(xtb_p, (k - WITH) % 2, n)
                pe.wait_ge(s_xt, 16 * (k + 1))
                for c in range(2):
                    shared_gate_up(k, xt, c, used(k, c))
                pe.wait_ge(s_x1s, k * TB)
                shared_down(k, 0, 0, True, False)
                if after:
                    after(0)
                with pe.Fori(0, SH // 2 - 1) as i:
                    for h in range(2):
                        c = 2 * i + 1 + h
                        shared_gate_up(k, xt, c + 1, used(k, c + 1))
                        shared_down(k, c, 1 - h, False, False)
                        if after:
                            after(c)
                shared_down(k, SH - 1, 1, False, True)
                if after:
                    after(SH - 1)

            def tokens(c):
                for q in range(4):
                    pe.wait_ge(s_hot, 4 * c + q + 1)
                    for i in range(TOP_E):
                        last = mm(bank[6][:, 0:BLOCKS], hot_row[q][:, i, :], hot_blk[q][:, i, :],
                                  start=(isinstance(c, int) and c == q == i == 0),
                                  stop=(isinstance(c, int) and c == SH - 1 and q == 3 and i == TOP_E - 1))
                    last.then_inc(s_hot_used, 1)

            shared_with_places()
            shared(WITH + 1, tokens)

            pe.wait_ge(s_sh32, FIRST * SH)
            pe.wait_ge(s_x1s, FIRST * TB)
            pe.wait_ge(s_whi_r, E)
            pe.wait_ge(s_wlo_r, E)
            pe.wait_ge(s_expert, 1)

            def experts(at):
                return nc.values_load_multi_w_load_instructions(
                    blocks_e[0:1, bass.ds(at, 8)], engines=[mybir.EngineType.PE], min_val=0, max_val=E - 1,
                    skip_runtime_bounds_check_because="VectorE counts at most E - 1 experts before a block")[1]

            def turn_rows(u, j, fresh):
                pe.wait_ge(s_xg[2 * j], 16 * ((u >> 1) + 1))
                if not fresh:
                    pe.wait_ge(s_txe, u - 1)
                for n in range(2 * KC):
                    last = turn(bank16[j][:, n * P:n * P + P], xg[:, 2 * j, n * P:n * P + P], id16)
                last.then_inc(s_tx, 1)

            def gate_up(s, r, e, fresh):
                j, rows = r % 2, (xgT, xgT_odd)[r % 2]
                if r % 2:
                    pe.wait_ge(s_odd[r // 2], 16 * ((s >> 2) + 1))
                else:
                    pe.wait_ge(s_txe, (s >> 1) + 1)
                if not fresh:
                    pe.wait_ge(s_rh, s - 1)
                n = 0
                for xv, wp in PARTS:
                    for kc in range(KC):
                        last = mm(bank[2 + j][:, 0:2 * H], rows[:, r // 2, xv * KC + kc, :],
                                  only((gu_hi_r, gu_lo_r)[wp], e, slice(kc * 2 * H, (kc + 1) * 2 * H)),
                                  start=(n == 0), stop=(n == 3 * KC - 1))
                        n += 1
                last.then_inc(s_rg, 1)

            def turn_h(s, j, fresh):
                pe.wait_ge(s_rhl, s + 1)
                if not fresh:
                    pe.wait_ge(s_hte, s - 1)
                for v in range(2):
                    last = turn(bank16[4 + j][:, v * P:v * P + P], r_hb[:, j, v, :], id16)
                last.then_inc(s_ht, 1)

            def down(s, j, e, fresh):
                pe.wait_ge(s_hte, s + 1)
                if not fresh:
                    pe.wait_ge(s_ye, s - 1)
                for n, (hv, wp) in enumerate(PARTS):
                    last = mm(bank[6 + j][:, :], r_hT[:, j, hv, :], only((dn_hi_r, dn_lo_r)[wp], e),
                              start=(n == 0), stop=(n == 2))
                last.then_inc(s_rd, 1)

            e = experts(0)
            turn_rows(0, 0, True)
            gate_up(0, 0, e[0], True)
            turn_rows(1, 1, True)
            gate_up(1, 1, e[1], True)
            turn_h(0, 0, True)
            def four(i, first):
                e = experts(4 * i)
                for n in range(4):
                    s = 4 * i + 1 + n
                    if n % 2:
                        turn_rows(2 * i + 2 + n // 2, n // 2, False)
                    gate_up(s + 1, (n + 2) % 4, e[n + 2], False)
                    turn_h(s, (1 + n) % 2, first and n == 0)
                    down(s - 1, n % 2, e[n], first and n < 2)

            four(0, True)
            with pe.Fori(1, BLOCKS // 4 - 1) as i:
                four(i, False)
            e = experts(BLOCKS - 4)
            gate_up(BLOCKS - 2, 2, e[2], False)
            turn_h(BLOCKS - 3, 1, False)
            down(BLOCKS - 4, 0, e[0], False)
            gate_up(BLOCKS - 1, 3, e[3], False)
            turn_h(BLOCKS - 2, 0, False)
            down(BLOCKS - 3, 1, e[1], False)
            turn_h(BLOCKS - 1, 1, False)
            down(BLOCKS - 2, 0, e[2], False)
            down(BLOCKS - 1, 1, e[3], False)

            pe.wait_ge(s_ye, BLOCKS)
            with pe.Fori(FIRST, NB) as k:
                shared(k)

        @block.scalar
        def _(act):
            A = nc.scalar.activation

            for c in range(KC):
                act.wait_ge(s_mm, c + 1)
                A(kT[:, c, :], bank[c][:, 0:B * M], ACT.Identity, bias=bias_sb[:, KC + c:KC + c + 1]).then_inc(s_mm_sb, 1)
            act.wait_ge(s_mm, 5)
            A(bqk, bank[7][:, B * M:B * M + B], ACT.Copy).then_inc(s_mm_sb, 1)

            def save_pt(q):
                b, n = q // 4, q % 4
                act.wait_ge(s_pt, q + 1)
                src, bias = bank[4 + q % 2], bqk[:, b:b + 1]
                if n == 0:
                    A(pt[b][:, M + L:PTW], src[:, 0:M], ACT.Identity, bias=bias)
                if n == 3:
                    A(pt[b][:, 0:M], src[:, BLK - M:BLK], ACT.Identity, bias=bias)
                A(pt[b][:, M + n * BLK:M + (n + 1) * BLK], src[:, :], ACT.Identity, bias=bias).then_inc(s_pt_sb, 1)

            def first_std(q):
                act.wait_ge(s_var, q + 1)
                A(std2[q % 2], var2[q % 2], ACT.Sqrt).then_inc(s_std, 1)

            def save_turned(q):
                for t in range(TB):
                    act.wait_ge(s_tp, q * TB + t + 1)
                    A(xnT[q % 2][:, :, t * P:t * P + P], bank[t][:, :].rearrange("p (k n) -> p k n", k=KC), ACT.Copy
                      ).then_inc(s_tp_sb, 1)

            first_std(0)
            for c in range(KC):
                if c == 2:
                    first_std(1)
                    save_turned(0)
                act.wait_ge(s_mm, 5 + c + 1)
                A(g_sb[:, c, :], bank[4 + c][:, 0:B * M], ACT.Copy).then_inc(s_mm_sb, 1)
            act.wait_ge(s_mm_sb, 9)
            for q in range(1, NB):
                if q + 1 < NB:
                    first_std(q + 1)
                save_turned(q)
                save_pt(q - 1)
            save_pt(NB - 1)
            for c in range(KC):
                act.wait_ge(s_mm, 9 + c + 1)
                A(vT[:, c, :], bank[c][:, 0:B * M], ACT.Identity, bias=bias_sb[:, 2 * KC + c:2 * KC + c + 1]
                  ).then_inc(s_mm_sb, 1)
            def softmax(b):
                nc.scalar.wait_ge(s_best, b + 1)
                nc.scalar.activation(top_e[0:1, :], best[0:1, :], ACT.Exp, bias=negmax[0:1, :],
                                     accum_out=total[0:1, :]).then_inc(s_exp, 1)
                nc.scalar.activation(row[b][0:1, :], row[b][0:1, :], ACT.Exp, bias=negmax[0:1, :]).then_inc(s_exp, 1)

            softmax(0)
            for b in range(B):
                act.wait_ge(s_mm, 13 + b + 1)
                A(vo[:, b, :], bank[4 + b][:, :], ACT.Copy).then_inc(s_mm_sb, 1)

            def second_std(k):
                act.wait_ge(s_var2, k + 1)
                A(std, var_eps, ACT.Sqrt).then_inc(s_std2, 1)

            def second_hi(k, j):
                act.wait_ge(s_xn2, TB * (k + 1))
                if not isinstance(k, int) or k >= 2:
                    act.wait_ge(s_xrw[j], 32 * (k >> 1))
                A(hi16[j], xn, ACT.Copy).then_inc(s_hi, 1)

            def save_logits(k):
                act.wait_ge(s_lg, k + 1)
                dst = early if isinstance(k, int) and k < 2 else scores
                A(dst[:, bass.ds(k * TB * E, TB * E)], bank[6][:, 0:TB * E], ACT.Copy).then_inc(s_lgs, 1)

            def shared_weights_hi(n):
                act.wait_ge(s_stage[n % 2], 32 * (n // 2 + 1))
                A(gu_hi_s[:, n, :], stage[n % 2][:, 0:2 * D], ACT.Copy, scale=WS)
                A(dn_hi_s[:, n, :], stage[n % 2][:, 2 * D:3 * D], ACT.Copy, scale=WS).then_inc(s_whi, 1)

            def silu(k, c):
                n = k * SH + c
                act.wait_ge(s_sg, n + 1)
                act.wait_ge(s_sh32, n)
                A(s_silu, bank[0][:, :], ACT.Silu, scale=1.0 / WS).then_inc(s_ss, 1)

            def h_hi(k, c, h, fresh):
                n = k * SH + c
                act.wait_ge(s_sh32, n + 1)
                if not fresh:
                    act.wait_ge(s_sd, n - 1)
                A(s_hb[:, h, 0, :], s_h, ACT.Copy).then_inc(s_shh, 1)

            act.wait_ge(s_g, 1)
            shared_weights_hi(0)
            second_std(0)
            second_hi(0, 0)
            second_std(1)
            second_hi(1, 1)
            shared_weights_hi(1)
            save_logits(0)
            shared_weights_hi(2)
            save_logits(1)
            shared_weights_hi(3)

            def with_attention(i, first):
                a, s = 2 * i, i - 1
                for c in range(SH):
                    silu(s, c)
                    if c % TB == 0:
                        second_std(a + c // TB)
                    h_hi(s, c, c % 2, first and c < 2)
                    if c % TB == 1:
                        second_hi(a + c // TB, c // TB)
                    if first and c < SH - TB:
                        shared_weights_hi(TB + c)
                    if first and c == 5:
                        softmax(1)
                    if c % TB == 3:
                        save_logits(a + c // TB)

            with_attention(1, True)
            with act.Fori(2, NB // 2) as i:
                with_attention(i, False)
            act.wait_ge(s_lgs, NB)
            for src in (early, scores[:, 2 * TB * E:]):
                at_col = 0 if src is early else 2 * TB * E
                A(scores[:, at_col:at_col + src.shape[1]], src, ACT.Sigmoid, scale=1.0 / WS).then_inc(s_sig, 1)

            def shared_chunk(k, c, h):
                silu(k, c)
                h_hi(k, c, h, False)

            def routed_weights_hi(n, j):
                w = stage_r[j]
                act.wait_ge(s_stage_r[j], 32 * ((n >> 1) + 1))
                A(only(gu_hi_r, n), w[:, 0:2 * D], ACT.Copy, scale=WS)
                A(only(dn_hi_r, n), w[:, 2 * D:3 * D], ACT.Copy, scale=WS).then_inc(s_wrd_r, 1)
                act.wait_ge(s_wrd_r, n + 1)
                A(w, w, ACT.Copy, scale=WS).then_inc(s_whi_r, 1)

            act.wait_ge(s_x1w, 16 * NB)
            act.wait_ge(s_xn2, TB * NB)
            with act.Fori(WITH, FIRST) as k:
                with act.Fori(0, SH // 2) as i:
                    for h in range(2):
                        shared_chunk(k, 2 * i + h, h)
                        routed_weights_hi((k - WITH) * SPLIT + 2 * i + h, h)

            def silu_hi(s, j, fresh):
                act.wait_ge(s_rg, s + 1)
                if not fresh:
                    act.wait_ge(s_rh, s - 1)
                A(r_silu[:, j, :], bank[2 + j][:, 0:H], ACT.Silu, scale=1.0 / WS).then_inc(s_rs, 1)
                act.wait_ge(s_rh, s + 1)
                if not fresh:
                    act.wait_ge(s_ht, s - 1)
                A(r_hb[:, j, 0, :], r_h[:, j, :], ACT.Copy).then_inc(s_rhh, 1)

            def save_y(s, j, half):
                act.wait_ge(s_rd, s + 1)
                if not isinstance(half, int) or half:
                    act.wait_ge(s_yw[j], 16 * half)
                A(y_sb[:, j, :], bank[6 + j][:, :], ACT.Copy, scale=1.0 / WS).then_inc(s_ye, 1)

            silu_hi(0, 0, True)
            silu_hi(1, 1, True)
            with act.Fori(0, BLOCKS // 4 - 1) as i:
                for n in range(4):
                    silu_hi(4 * i + 2 + n, n % 2, False)
                    save_y(4 * i + n, n % 2, 2 * i + n // 2)
            for n in range(2):
                silu_hi(BLOCKS - 2 + n, n, False)
                save_y(BLOCKS - 4 + n, n, BLOCKS // 2 - 2)
            for n in range(2):
                save_y(BLOCKS - 2 + n, n, BLOCKS // 2 - 1)

            with act.Fori(FIRST, NB) as k:
                for c in range(SH):
                    shared_chunk(k, c, c % 2)

        @block.vector
        def _(dve):
            link = Links(dve, s_dve)
            V = nc.vector

            def save_sums(b):
                dve.wait_ge(s_u, b + 1)
                u = bank[6][:, 0:2 * NA].rearrange("p (a v) -> p v a", v=2)
                V.tensor_copy(sums, u).then_inc(s_u_sb, 1)
                V.tensor_copy(mirrored[:, :, 0:1], u[:, :, 0:1]).then_inc(s_u_sb, 1)
                V.tensor_copy(mirrored[:, :, 1:NA + 1], u[:, :, ::-1]).then_inc(s_u_sb, 1)

            def save_even(b):
                dve.wait_ge(s_ev, b + 1)
                V.tensor_copy(even_s, bank[7][:, 0:NA]).then_inc(s_ev_sb, 1)
                V.tensor_copy(even_w[:, 0:NA], bank[7][:, NA:2 * NA]).then_inc(s_ev_sb, 1)
                V.tensor_copy(even_w[:, NA:2 * NA], bank[7][:, NA:2 * NA]).then_inc(s_ev_sb, 1)

            def save_mean(b):
                dve.wait_ge(s_mT, b + 1)
                if b:
                    dve.wait_ge(s_mw[0], 16)
                V.tensor_copy(meanT[0:NA, :], bank[7][0:NA, 64:64 + P]).then_inc(s_mT_sb, 1)

            def delays(b, part):
                r, k = row[b][0:1, :], taken[b][0:1, :]
                if part == 0:
                    dve.wait_ge(s_row[b], 16)
                    link.done(V.max(best[0:1, 0:8], r))
                if part == 1:
                    link.done(V.match_replace(k, best[0:1, 0:8], r, GONE))
                    link.done(V.max(best[0:1, 8:16], k))
                if part == 2:
                    link.start(V.memset(best[0:1, TOP_K:16], GONE))
                    link.start(V.tensor_scalar(negmax[0:1, :], best[0:1, 0:1], -1.0, None, ALU.mult))
                    link.wait()
                    V.match_replace(k, best[0:1, 8:16], k, GONE).then_inc(s_best, 1)
                if part == 3:
                    dve.wait_ge(s_best, b + 1)
                    dve.wait_ge(s_exp, 2 * b + 2)
                    link.done(V.reciprocal(inv[0:1, :], total[0:1, :]))
                    link.done(V.tensor_scalar(k, k, GONE, inv[0:1, :], ALU.is_le, ALU.mult))
                    V.tensor_tensor(r, r, k, ALU.mult).then_inc(s_g, 1)

            def moments(q):
                dve.wait_ge(s_x[q], 16)
                for t in range(TB):
                    link.start(V.bn_stats(stats[:, t, :], x_sb[:, q * TB + t, :]))
                link.wait()
                if q >= 2:
                    dve.wait_ge(s_xn, (q - 1) * TB)
                for t in range(TB):
                    link.start(V.bn_aggr(mv2[q % 2][:, t, :], stats[:, t, :]))
                link.wait()
                V.tensor_scalar(var2[q % 2], mv2[q % 2][:, :, 1], EPS, None, ALU.add).then_inc(s_var, 1)

            def normalise(q):
                m, r = mv2[q % 2], rstd2[q % 2]
                dve.wait_ge(s_std, q + 1)
                link.done(V.reciprocal(r, std2[q % 2]))
                for t in range(TB):
                    if q:
                        dve.wait_ge(s_tp, (q - 1) * TB + t + 1)
                    V.tensor_scalar(xn[:, t, :], x_sb[:, q * TB + t, :], m[:, t, 0:1], r[:, t:t + 1],
                                    ALU.subtract, ALU.mult).then_inc(s_xn, 1)

            moments(0)
            for q in range(NB):
                if q + 1 < NB:
                    moments(q + 1)
                normalise(q)
            save_sums(0)
            save_even(0)
            save_mean(0)
            dve.wait_ge(s_misc, 64)
            dve.wait_ge(s_const, 16)
            r3 = rt32.rearrange("p (k e) -> p k e", k=KC)
            link.done(V.tensor_scalar(rt_hi, r3, WS, None, ALU.mult))
            V.scalar_tensor_tensor(rt_lo, r3, WS, rt_hi, ALU.mult, ALU.subtract).then_inc(s_rt, 1)
            V.tensor_copy(id16, c_sb[:, C_ID:C_ID + P]).then_inc(s_rt, 1)
            V.tensor_copy(tri16, cr_sb[:, R_TRI:R_TRI + P])
            V.memset(chosen_after[:, 0:E], 0.0)
            V.tensor_copy(places16, cr_sb[:, R_BLK:R_BLK + BLOCKS])
            dve.wait_ge(s_ids, 1)
            V.tensor_scalar(token_id, token_int, -ID_MID, None, ALU.add)
            V.memset(ones16, 1.0).then_inc(s_rt, 1)

            for part in range(4):
                delays(0, part)

            def x1_stage(k, banks):
                for t in range(TB):
                    n = k * TB + t
                    xr = only(x_sb, n)
                    dve.wait_ge(s_at, n + 1)
                    V.tensor_tensor(xr, bank[banks[t]][:, :], xr, ALU.add).then_inc(s_x1, 1)
                    settled(dve)
                    dve.wait_ge(s_x1, n + 1)
                    V.bn_stats(stats[:, t, :], xr).then_inc(s_bn, 1)
                settled(dve)
                dve.wait_ge(s_bn, k * TB + TB)
                for t in range(TB):
                    V.bn_aggr(mv[:, t, :], stats[:, t, :]).then_inc(s_mv, 1)
                dve.wait_ge(s_mv, k * TB + TB)
                V.tensor_scalar(var_eps, mv[:, :, 1], EPS, None, ALU.add).then_inc(s_var2, 1)

            def norm_stage(k):
                dve.wait_ge(s_std2, k + 1)
                V.reciprocal(rstd, std).then_inc(s_rstd, 1)
                dve.wait_ge(s_rstd, k + 1)
                dve.wait_ge(s_hi, k)
                dve.wait_ge(s_lo, k)
                for t in range(TB):
                    V.tensor_scalar(xn[:, t, :], only(x_sb, k * TB + t), mv[:, t, 0:1], rstd[:, t:t + 1],
                                    ALU.subtract, ALU.mult).then_inc(s_xn2, 1)

            def shared_chunk(k, c, h, fresh=False):
                n = k * SH + c
                dve.wait_ge(s_ss, n + 1)
                dve.wait_ge(s_su, n + 1)
                if not fresh:
                    dve.wait_ge(s_shh, n)
                    dve.wait_ge(s_shl, n)
                V.scalar_tensor_tensor(s_h, bank[1][:, :], 1.0 / WS, s_silu, ALU.mult, ALU.mult).then_inc(s_sh32, 1)
                dve.wait_ge(s_shh, n + 1)
                V.tensor_tensor(s_hb[:, h, 1, :], s_h, s_hb[:, h, 0, :], ALU.subtract).then_inc(s_shl, 1)

            def shared_sum(k):
                dve.wait_ge(s_sd, SH * (k + 1))
                dve.wait_ge(s_x1i, 16 * (k + 1))
                for t in range(TB):
                    V.scalar_tensor_tensor(x1b[:, t, :], bank[2 + t][:, :], 1.0 / WS, x1b[:, t, :], ALU.mult, ALU.add
                                           ).then_inc(s_x1s, 1)

            def shared_weights_lo(n):
                dve.wait_ge(s_whi, n + 1)
                V.scalar_tensor_tensor(gu_lo_s[:, n, :], stage[n % 2][:, 0:2 * D], WS, gu_hi_s[:, n, :],
                                       ALU.mult, ALU.subtract)
                V.scalar_tensor_tensor(dn_lo_s[:, n, :], stage[n % 2][:, 2 * D:3 * D], WS, dn_hi_s[:, n, :],
                                       ALU.mult, ALU.subtract).then_inc(s_wlo, 1)

            dve.wait_ge(s_xbo, NB)
            dve.wait_ge(s_xn, T)
            x1_stage(0, (0, 1, 2, 3))
            dve.wait_ge(s_tp, T)
            norm_stage(0)
            x1_stage(1, (4, 5, 0, 1))
            save_sums(1)
            norm_stage(1)
            save_even(1)
            shared_weights_lo(0)
            save_mean(1)
            shared_weights_lo(1)
            for n in range(2, TB):
                shared_weights_lo(n)

            def with_attention(i, first):
                a, s = 2 * i, i - 1
                x1_stage(a, (0, 1, 6, 7))
                for c in range(SH):
                    n = a + c // TB
                    if c == TB:
                        x1_stage(n, (0, 1, 6, 7))
                    shared_chunk(s, c, c % 2, first and c == 0)
                    if c % TB == 0:
                        norm_stage(n)
                    if first and c < SH - TB:
                        shared_weights_lo(TB + c)
                    if first and c >= 3 and c < 7:
                        delays(1, c - 3)
                shared_sum(s)

            with_attention(1, True)
            with dve.Fori(2, NB // 2) as i:
                with_attention(i, False)

            def tiles(v, n=E):
                return v.rearrange("p (t e) -> p t e", e=n)

            dve.wait_ge(s_sig, 2)
            dve.wait_ge(s_lo, NB)
            for j in range(2):
                dve.wait_ge(s_xrw[j], 16 * NB)
            link.done(V.tensor_tensor(tiles(biased), tiles(scores), cb_sb.unsqueeze(1).broadcast_to([P, T, E]), ALU.add))
            G4 = T * GROUPS
            pairs = biased.rearrange("p (g a) -> p g a", a=2)
            hi2, lo2 = tmp[:, 0:2 * G4], tmp[:, 2 * G4:4 * G4]
            one = lambda v: v.unsqueeze(2)
            link.start(V.tensor_tensor(one(hi2), pairs[:, :, 0:1], pairs[:, :, 1:2], ALU.max))
            link.done(V.tensor_tensor(one(lo2), pairs[:, :, 0:1], pairs[:, :, 1:2], ALU.min))
            hv, lv = (v.rearrange("p (g a) -> p g a", a=2) for v in (hi2, lo2))
            m1, m2, m3 = (cnt[:, i * G4:(i + 1) * G4] for i in range(3))
            link.start(V.tensor_tensor(one(m1), hv[:, :, 0:1], hv[:, :, 1:2], ALU.max))
            link.start(V.tensor_tensor(one(m2), hv[:, :, 0:1], hv[:, :, 1:2], ALU.min))
            link.done(V.tensor_tensor(one(m3), lv[:, :, 0:1], lv[:, :, 1:2], ALU.max))
            link.done(V.tensor_tensor(m2, m2, m3, ALU.max))
            link.done(V.tensor_tensor(m1, m1, m2, ALU.add))
            gs, rank, beats = tiles(m1, GROUPS), tiles(m2, GROUPS), tiles(m3, GROUPS)
            for i in range(GROUPS):
                link.start(V.memset(rank[:, :, i:i + 1], float(GROUPS - 1 - i)))
            for d in range(1, GROUPS):
                n = GROUPS - d
                link.done(V.tensor_tensor(beats[:, :, 0:n], gs[:, :, 0:n], gs[:, :, d:GROUPS], ALU.is_ge))
                link.done(V.tensor_tensor(rank[:, :, d:GROUPS], rank[:, :, d:GROUPS], beats[:, :, 0:n], ALU.add))
                link.done(V.tensor_tensor(rank[:, :, 0:n], rank[:, :, 0:n], beats[:, :, 0:n], ALU.subtract))
            link.done(V.tensor_scalar(m2, m2, float(TOP_GROUPS) - 0.5, 1.0e30, ALU.is_gt, ALU.mult))
            by_group = biased.rearrange("p (g a) -> p g a", a=PER_GROUP)
            link.done(V.tensor_tensor(by_group, by_group, m2.unsqueeze(2).broadcast_to([P, G4, PER_GROUP]), ALU.subtract))
            shared_chunk(WITH, 0, 0)
            b3 = tiles(biased)
            for t in range(T):
                link.start(V.max(top8[:, t, :], b3[:, t, :]))
            shared_chunk(WITH, 1, 1)
            link.wait()
            for t in range(T):
                link.start(V.max_index(top8_at[:, t, :], top8[:, t, :], b3[:, t, :]))
            link.wait()
            shared_chunk(WITH, 2, 0)
            link.done(V.tensor_copy(top8_e, top8_at))
            expert = cr_sb[:, R_EXP:R_EXP + E].unsqueeze(1).broadcast_to([P, T, E])
            for i in range(TOP_E):
                link.start(V.tensor_tensor(tiles(picked[i]), expert, top8_e[:, :, i:i + 1].broadcast_to([P, T, E]),
                                           ALU.is_equal))
            link.wait()
            link.start(V.tensor_tensor(chosen, picked[0], picked[1], ALU.add))
            link.done(V.tensor_tensor(cnt, picked[2], picked[3], ALU.add))
            V.tensor_tensor(chosen, chosen, cnt, ALU.add).then_inc(s_chosen, 1)
            shared_chunk(WITH, 3, 1)
            w3 = pair_w.rearrange("p (i t) -> p i t", i=TOP_E)
            for i in range(TOP_E):
                link.done(V.tensor_tensor(tmp, picked[i], scores, ALU.mult))
                link.done(V.tensor_reduce(w3[:, i, :], tiles(tmp), AX_X, ALU.add))
            link.done(V.tensor_reduce(tmp[:, 0:T], pair_w.rearrange("p (i t) -> p t i", i=TOP_E), AX_X, ALU.add))
            link.done(V.tensor_scalar(tmp[:, 0:T], tmp[:, 0:T], 1e-20, None, ALU.add))
            link.done(V.reciprocal(tmp[:, T:2 * T], tmp[:, 0:T]))
            link.done(V.tensor_tensor(w3, w3, tmp[:, T:2 * T].unsqueeze(1).broadcast_to([P, TOP_E, T]), ALU.mult))

            dve.wait_ge(s_rank, 1)
            def whole(v, src, low):
                link.done(V.tensor_scalar(v, src, 1.0 / P, low, ALU.mult, ALU.add))
                link.done(V.tensor_scalar(v, v, ROUND, ROUND, ALU.add, ALU.subtract))

            link.done(V.tensor_copy(load_e, bank[7][:, 0:E]))
            whole(nblk, load_e, (P - 1.0) / P - 0.5 + 0.5 / P)
            link.done(V.tensor_copy(first_a, nblk))
            src, dst = first_a, first_b
            for d in (1, 2, 4, 8):
                link.start(V.tensor_copy(dst[:, 0:d], src[:, 0:d]))
                link.done(V.tensor_tensor(dst[:, d:E], src[:, d:E], src[:, 0:E - d], ALU.add))
                src, dst = dst, src
            link.done(V.tensor_copy(last_blk, src))
            link.done(V.tensor_tensor(first_b, last_blk, nblk, ALU.subtract))
            link.done(V.tensor_scalar(first_b, first_b, float(P), None, ALU.mult))
            link.done(V.tensor_tensor(tiles(slot), bank[6][:, :].rearrange("p (t e) -> p t e", e=E),
                                      first_b.unsqueeze(1).broadcast_to([P, T, E]), ALU.add))
            sl3 = pair_slot.rearrange("p (i t) -> p i t", i=TOP_E)
            for i in range(TOP_E):
                link.done(V.tensor_tensor(tmp, picked[i], slot, ALU.mult))
                link.done(V.tensor_reduce(sl3[:, i, :], tiles(tmp), AX_X, ALU.add))
            shared_chunk(WITH, 4, 0)
            whole(pair_blk, pair_slot, -0.5 + 0.5 / P)
            link.start(V.tensor_copy(row_of, pair_slot))
            link.done(V.scalar_tensor_tensor(pair_row, pair_blk, -float(P), pair_slot, ALU.mult, ALU.add))
            shared_chunk(WITH, 5, 1)
            link.done(V.memset(tmp[:, 0:BLOCKS], 0.0))
            for e in range(E - 1):
                link.done(V.scalar_tensor_tensor(tmp[:, 0:BLOCKS], cr_sb[:, R_BLK:R_BLK + BLOCKS], last_blk[:, e:e + 1],
                                                 tmp[:, 0:BLOCKS], ALU.is_ge, ALU.add))
            link.start(V.memset(blocks_e[:, BLOCKS:BLOCKS + 8], 0))
            link.done(V.tensor_copy(blocks_e[:, 0:BLOCKS], tmp[:, 0:BLOCKS]))
            V.engine_nop().then_inc(s_expert, 1)
            for c in (6, 7):
                shared_chunk(WITH, c, c % 2)

            shared_sum(WITH)

            row3 = pair_row.rearrange("p (i t) -> p i t", i=TOP_E)
            with dve.Fori(0, SH // 2) as i:
                for h in range(2):
                    c = 2 * i + h
                    shared_chunk(WITH + 1, c, h)
                    for q in range(4):
                        t = 4 * c + q
                        dve.wait_ge(s_hot_used, 4 * c)
                        V.tensor_tensor(hot_row[q], places16[:, 0:P].unsqueeze(1).broadcast_to([P, TOP_E, P]),
                                        row3[:, :, bass.ds(t, 1)].broadcast_to([P, TOP_E, P]), ALU.is_equal)
                        for e in range(TOP_E):
                            last = V.tensor_scalar(hot_blk[q][:, e, :], places16, pair_blk[:, bass.ds(t + e * T, 1)],
                                                   token_id[:, bass.ds(t, 1)], ALU.is_equal, ALU.mult)
                        last.then_inc(s_hot, 1)
            dve.wait_ge(s_hot_used, T)
            V.tensor_scalar(token_of, bank[6][:, 0:BLOCKS], ID_MID, None, ALU.add).then_inc(s_tok, 1)
            shared_sum(WITH + 1)

            def save_rows(u, j, fresh):
                dve.wait_ge(s_tx, u + 1)
                if not fresh:
                    dve.wait_ge(s_rg, 2 * u - 3)
                V.tensor_copy(xgT[:, j, :, :], bank16[j].rearrange("p (n q) -> p n q", n=2 * KC)).then_inc(s_txe, 1)

            def save_h(s, j, fresh):
                dve.wait_ge(s_ht, s + 1)
                if not fresh:
                    dve.wait_ge(s_rd, s - 1)
                V.tensor_copy(r_hT[:, j, :, :], bank16[4 + j][:, 0:2 * P].rearrange("p (v q) -> p v q", v=2)
                              ).then_inc(s_hte, 1)

            def hidden(s, j, fresh):
                dve.wait_ge(s_rs, s + 1)
                if not fresh:
                    dve.wait_ge(s_rhh, s - 1)
                    dve.wait_ge(s_rhl, s - 1)
                V.scalar_tensor_tensor(r_h[:, j, :], bank[2 + j][:, H:2 * H], 1.0 / WS, r_silu[:, j, :], ALU.mult, ALU.mult
                                       ).then_inc(s_rh, 1)
                dve.wait_ge(s_rhh, s + 1)
                V.tensor_tensor(r_hb[:, j, 1, :], r_h[:, j, :], r_hb[:, j, 0, :], ALU.subtract).then_inc(s_rhl, 1)

            save_rows(0, 0, True)
            save_rows(1, 1, True)
            hidden(0, 0, True)
            hidden(1, 1, True)
            save_h(0, 0, True)
            with dve.Fori(0, BLOCKS // 4 - 1) as i:
                for n in range(4):
                    s = 4 * i + 1 + n
                    if n % 2:
                        save_rows(2 * i + 2 + n // 2, n // 2, False)
                    hidden(s + 1, n % 2, False)
                    save_h(s, (1 + n) % 2, False)
            hidden(BLOCKS - 2, 0, False)
            save_h(BLOCKS - 3, 1, False)
            hidden(BLOCKS - 1, 1, False)
            save_h(BLOCKS - 2, 0, False)
            save_h(BLOCKS - 1, 1, False)

            def combine(k, p, old):
                i = k - FIRST
                n = i * TURNS + p
                dve.wait_ge(s_yg[p % RING], 16 * TOP_E * (i * (TURNS // RING) + p // RING + 1))
                if p < old:
                    m, acc = i * OLD + p, x1c[:, p % RING, :]
                    dve.wait_ge(s_x1c[p % RING], 16 * (i * (OLD // RING) + p // RING + 1))
                else:
                    m, acc = k * TB + p - old, x1b[:, p - old, :]
                    dve.wait_ge(s_x1i, 16 * (k + 1))
                for e in range(TOP_E):
                    if e:
                        dve.wait_ge(s_cmb, TOP_E * n + e)
                    w = pair_w[:, bass.ds(m + e * T, 1)]
                    V.scalar_tensor_tensor(acc, ybuf[p % RING][:, e, :], w, acc, ALU.mult, ALU.add).then_inc(s_cmb, 1)

            def last_shared(k, old):
                turns = old + TB
                for c in range(SH):
                    shared_chunk(k, c, c % 2)
                    for p in range(c * turns // SH, (c + 1) * turns // SH):
                        combine(k, p, old)
                dve.wait_ge(s_cmb, TOP_E * ((k - FIRST) * TURNS + turns))
                shared_sum(k)

            with dve.Fori(FIRST, NB - 1) as k:
                last_shared(k, OLD)
            last_shared(NB - 1, OLD_LAST)

        @block.gpsimd
        def _(pool):
            pool.iota(token_int, pattern=[[P, T]], base=0, channel_multiplier=1).then_inc(s_ids, 1)
            pool.wait_ge(s_misc, 64)
            for q in range(NB):
                pool.wait_ge(s_xn, q * TB + TB)
                xq = x_sb[:, q * TB:q * TB + TB, :]
                pool.tensor_tensor(xq, xq, bo_sb.unsqueeze(1).broadcast_to([P, TB, D]), ALU.add).then_inc(s_xbo, 1)
            def second_norm_lo(k, j):
                pool.wait_ge(s_hi, k + 1)
                if not isinstance(k, int) or k >= 2:
                    pool.wait_ge(s_xrw[j], 32 * (k >> 1))
                pool.tensor_tensor(lo16[j], xn, hi16[j], ALU.subtract).then_inc(s_lo, 1)

            def shared_weights_in(n):
                pool.dma_start(stage[n % 2][:, 0:2 * D], gu_w[n]).then_inc(s_stage[n % 2], 16)
                pool.dma_start(stage[n % 2][:, 2 * D:3 * D], dn_w[n]).then_inc(s_stage[n % 2], 16)

            def next_weights(n):
                pool.wait_ge(s_wlo, n - 1)
                shared_weights_in(n)

            for n in range(2):
                pool.wait_ge(s_pt, NB - 1 + n)
                shared_weights_in(n)
            for k in range(2):
                second_norm_lo(k, k)
            for n in range(2, SH - 1):
                next_weights(n)
            second_norm_lo(2, 0)
            next_weights(SH - 1)
            second_norm_lo(3, 1)
            with pool.Fori(2, NB // 2) as i:
                for j in range(2):
                    second_norm_lo(2 * i + j, j)
            def routed_weights_lo(n, j):
                pool.wait_ge(s_whi_r, n + 1)
                pool.tensor_tensor(only(gu_lo_r, n), stage_r[j][:, 0:2 * D], only(gu_hi_r, n), ALU.subtract)
                pool.tensor_tensor(only(dn_lo_r, n), stage_r[j][:, 2 * D:3 * D], only(dn_hi_r, n), ALU.subtract
                                   ).then_inc(s_wlo_r, 1)

            for first in (0, E // 2):
                if first:
                    pool.wait_ge(s_expert, 1)
                with pool.Fori(first // 2, (first + E // 2) // 2) as i:
                    for j in range(2):
                        routed_weights_lo(2 * i + j, j)
            pool.wait_ge(s_tok, 1)
            row3 = row_of.rearrange("p (i t) -> p i t", i=TOP_E)

            def copy_tokens(s, r):
                pool.tensor_copy(token_now[:, r:r + 1], token_of[:, bass.ds(s, 1)]).then_inc(s_token_now, 1)

            def gather(s, r, fresh, last):
                if not fresh:
                    if r % 2:
                        pool.wait_ge(s_odd[r % 4 // 2], 16 * (s >> 2))
                    else:
                        pool.wait_ge(s_tx, (s - 2) >> 1)
                pool.wait_ge(s_token_now, s + 1)
                if not last:
                    copy_tokens(s + 1, (r + 1) % 8)
                pool.indirect_dma_start(
                    out=xg[:, r % 4, :], out_offset=None, in_=xr_dram[:, :],
                    in_offset=bass.IndirectOffsetOnAxis(ap=token_now[:, r:r + 1], axis=0)).then_inc(s_xg[r % 4], 16)

            copy_tokens(0, 0)
            for r in range(8):
                gather(r, r, r < 4, False)
            with pool.Fori(1, BLOCKS // 8 - 1) as i:
                for r in range(8):
                    gather(8 * i + r, r, False, False)
            for r in range(8):
                gather(BLOCKS - 8 + r, r, False, r == 7)
            for j in range(2):
                pool.wait_ge(s_yw[j], 16 * BLOCKS // 2)
            pool.wait_ge(s_rd, BLOCKS)

            def copy_rows(i, p, old):
                m = i * OLD + p if p < old else (FIRST + i) * TB + p - old
                pool.tensor_copy(row_now[:, p % ROWS_RING, :].unsqueeze(2), row3[:, :, bass.ds(m, 1)]).then_inc(s_row_now, 1)

            def gather_y(i, p, old):
                n = i * TURNS + p
                if not isinstance(n, int) or n >= RING:
                    pool.wait_ge(s_cmb, TOP_E * (n - (RING - 1)))
                pool.wait_ge(s_row_now, n + 1)
                if not isinstance(n, int) or n + 1 < T:
                    copy_rows(i + (p + 1) // TURNS, (p + 1) % TURNS, old)
                for e in range(TOP_E):
                    pool.indirect_dma_start(
                        out=ybuf[p % RING][:, e, :], out_offset=None, in_=y_dram[:, :],
                        in_offset=bass.IndirectOffsetOnAxis(ap=row_now[:, p % ROWS_RING, e:e + 1], axis=0)).then_inc(s_yg[p % RING], 16)

            copy_rows(0, 0, OLD)
            for p in range(TURNS):
                gather_y(0, p, OLD)
            with pool.Fori(1, NB - FIRST - 1) as i:
                for p in range(TURNS):
                    gather_y(i, p, OLD)
            for p in range(OLD_LAST + TB):
                gather_y(NB - FIRST - 1, p, OLD_LAST)


def kernel(x, ctx_1024, L0_xattn_Wq, L0_xattn_bq, L0_xattn_Wk, L0_xattn_bk, L0_xattn_Wv, L0_xattn_bv,
           L0_xattn_Wo, L0_xattn_bo, L0_ffn_router_w, L0_ffn_correction_bias, L0_ffn_gate_w, L0_ffn_up_w,
           L0_ffn_down_w, L0_ffn_shared_gate_w, L0_ffn_shared_up_w, L0_ffn_shared_down_w):
    import concourse.bacc as bacc
    from concourse.bass_utils import run_bass_kernel_spmd

    def chunks(w):
        w = np.asarray(w)
        return np.ascontiguousarray(w.reshape(-1, P, w.shape[-1]).transpose(1, 0, 2))

    def columns(v):
        return np.asarray(v).reshape(-1, P).T

    def rows(v):
        return np.ascontiguousarray(np.broadcast_to(np.asarray(v)[None, :], (P, len(v))))

    ctx = np.asarray(ctx_1024)[:, ::-1, :].reshape(B * M, D)
    gate = np.concatenate([np.asarray(L0_ffn_shared_gate_w).reshape(SH, H, D).transpose(0, 2, 1),
                           np.asarray(L0_ffn_gate_w)])
    up = np.concatenate([np.asarray(L0_ffn_shared_up_w).reshape(SH, H, D).transpose(0, 2, 1),
                         np.asarray(L0_ffn_up_w)])
    gu = np.concatenate([gate, up], axis=2).reshape(SH + E, KC, P, 2 * H).transpose(0, 2, 1, 3)
    dn = np.concatenate([np.asarray(L0_ffn_shared_down_w).T.reshape(SH, H, D), np.asarray(L0_ffn_down_w)])
    const, const_r = constants()
    arrays = {
        "x": np.ascontiguousarray(np.asarray(x).reshape(S, D)),
        "ctxT": chunks(ctx.T),
        "wk": chunks(L0_xattn_Wk), "wqT": chunks(np.asarray(L0_xattn_Wq).T),
        "wv": chunks(L0_xattn_Wv), "wo": chunks(L0_xattn_Wo),
        "biases": np.ascontiguousarray(np.concatenate(
            [columns(L0_xattn_bq), columns(L0_xattn_bk), columns(L0_xattn_bv)], axis=1)),
        "bo": rows(L0_xattn_bo), "cb": rows(L0_ffn_correction_bias),
        "routerT": np.ascontiguousarray(chunks(np.asarray(L0_ffn_router_w).T).reshape(P, KC * E)),
        "gu_w": np.ascontiguousarray(gu.reshape(SH + E, P, 2 * D)),
        "dn_w": np.ascontiguousarray(dn),
        "const": const, "const_r": const_r,
    }
    nc = bacc.Bacc("TRN2", target_bir_lowering=False, num_devices=1)
    args = {n: nc.dram_tensor(f"in_{n}", a.shape, F32, kind="ExternalInput").ap() for n, a in arrays.items()}
    out = nc.dram_tensor("out", (S, D), F32, kind="ExternalOutput").ap()
    build(nc, out=out, **args)
    got = run_bass_kernel_spmd(nc, [{f"in_{n}": a for n, a in arrays.items()}], core_ids=[0])
    return got.results[0]["out"].reshape(B, L, D)
```
